# Optimizing a Trainium2 kernel written in Bass

```python
import numpy as np
import jax
import jax.numpy as jnp

def _softmax(x, axis=-1):
    return jax.nn.softmax(x, axis=axis)

def _gelu(x):
    return jax.nn.gelu(x, approximate=True)

def _silu(x):
    return jax.nn.silu(x)

def _sigmoid(x):
    return jax.nn.sigmoid(x)

def _layernorm(x, axis=-1, eps=1e-05):
    m = jnp.mean(x, axis=axis, keepdims=True)
    v = jnp.var(x, axis=axis, keepdims=True)
    return (x - m) / jnp.sqrt(v + eps)

def _scatter_add(tgt, idx, src, axis=0):
    return tgt.at[idx].add(src)

def _segment_sum(src, seg, n):
    return jax.ops.segment_sum(src, seg, n)
kernel_name = 'mk_perceiver_d2_seqx_r8_e46d29'

def setup_inputs(seed: int=0):
    np.random.seed(seed)
    _w = jnp.asarray

    def _rec_inputs():
        import jax
        import jax.numpy as jnp
        _rk = jax.random.key(seed)
        x = -0.0002928 + 1 * jax.random.normal(jax.random.fold_in(_rk, 1), (64, 32, 128), jnp.float32)
        _lenS = 32 - jax.random.randint(jax.random.fold_in(_rk, 7), (64,), 0, max(1, 32 // 4) + 1, jnp.int32)
        _lenS2 = 257 - jax.random.randint(jax.random.fold_in(_rk, 8), (64,), 0, max(1, 257 // 4) + 1, jnp.int32)
        _ctx_1024P = jax.random.normal(jax.random.fold_in(_rk, 11), (64, 16, 128), jnp.float32)
        _ctx_1024c = jax.random.dirichlet(jax.random.fold_in(_rk, 511), 0.3 * jnp.ones((16,), jnp.float32), (64, 257))
        _ctx_1024t = jnp.einsum('bsk,bkd->bsd', _ctx_1024c, _ctx_1024P)
        _ctx_1024t = _ctx_1024t * jax.lax.rsqrt(jnp.mean(jnp.square(_ctx_1024t)) + 1e-12) * 0.953939
        ctx_1024 = -1.39393e-06 + 0.999914 * (_ctx_1024t + 0.3 * jax.random.normal(jax.random.fold_in(_rk, 611), (64, 257, 128), jnp.float32))
        _validS = jnp.arange(32)[None, :] < _lenS[:, None]
        _validS2 = jnp.arange(257)[None, :] < _lenS2[:, None]
        _causal = jnp.tril(jnp.ones((32, 32), dtype=bool))
        mask_Bx1x1xS2_fk0 = jnp.where(jnp.broadcast_to(_validS2[:, None, None, :], (64, 1, 1, 257)), 0.0, 1.0).astype(jnp.float32)
        mask_BxS2_bk0 = jnp.logical_not(jnp.broadcast_to(_validS2[:, :], (64, 257)))
        return (x, ctx_1024, mask_Bx1x1xS2_fk0, mask_BxS2_bk0)
    x, ctx_1024, mask_Bx1x1xS2_fk0, mask_BxS2_bk0 = _rec_inputs()

    def _L0_xattn_setup():
        import jax, jax.numpy as jnp
        import numpy as np
        B, S, D, H = (2, 256, 128, 16)
        DH = D // H

        def _split_heads(x):
            b, s, _ = x.shape
            return x.reshape(b, s, H, DH).transpose(0, 2, 1, 3)
        key = jax.random.key(seed)
        ks = jax.random.split(key, 8)
        scale = 0.02
        return {'query': jax.random.normal(ks[0], (B, S, D), jnp.float32), 'key': jax.random.normal(ks[1], (B, S, D), jnp.float32), 'value': jax.random.normal(ks[2], (B, S, D), jnp.float32), 'mask': jax.random.randint(ks[3], (B, 1, 1, S), 0, 2).astype(jnp.float32), 'Wq': jax.random.normal(ks[4], (D, D), jnp.float32) * scale, 'bq': jnp.zeros((D,), jnp.float32), 'Wk': jax.random.normal(ks[5], (D, D), jnp.float32) * scale, 'bk': jnp.zeros((D,), jnp.float32), 'Wv': jax.random.normal(ks[6], (D, D), jnp.float32) * scale, 'bv': jnp.zeros((D,), jnp.float32), 'Wo': jax.random.normal(ks[7], (D, D), jnp.float32) * scale, 'bo': jnp.zeros((D,), jnp.float32)}
    _L0_xattn_all = _L0_xattn_setup()
    _L0_xattn_in = {k: v for k, v in _L0_xattn_all.items() if k in ('Wq', 'bq', 'Wk', 'bk', 'Wv', 'bv', 'Wo', 'bo')}
    del _L0_xattn_all

    def _L0_attn_setup():
        import jax, jax.numpy as jnp
        import numpy as np
        D_MODEL, N_QUERY, N_HEAD = (128, 2, 8)
        D_HEAD = D_MODEL // (N_QUERY * N_HEAD)
        KV = D_HEAD * N_HEAD

        def _reference_tuple_inner(x, Wq, Wk, Wv, memory, memory_norm, memory_weight):
            B, S, _ = x.shape
            QH = N_QUERY * N_HEAD
            scale = 1.0 / jnp.sqrt(jnp.float32(D_HEAD))
            q = x @ Wq
            k = x @ Wk
            v = x @ Wv
            q4 = q.reshape(B, S, QH, D_HEAD)
            k4 = jnp.repeat(k.reshape(B, S, N_HEAD, D_HEAD), N_QUERY, axis=2)
            v4 = jnp.repeat(v.reshape(B, S, N_HEAD, D_HEAD), N_QUERY, axis=2)
            scores = jnp.einsum('bsnd,btnd->bnst', q4, k4) * scale
            probs = jax.nn.softmax(scores, axis=-1)
            a_dot = jnp.einsum('bnst,btnd->bsnd', probs, v4)
            sigma_q = jax.nn.elu(q.reshape(B, S, N_QUERY, KV))
            num = sigma_q @ memory
            den = (sigma_q @ memory_norm)[..., None]
            a_mem = (num / den).reshape(B, S, QH, D_HEAD)
            sigma_k = jax.nn.elu(k)
            retrieved = sigma_k @ memory / (sigma_k @ memory_norm)[..., None]
            new_memory = memory + jnp.einsum('bsk,bsv->kv', sigma_k, v - retrieved)
            new_memory_norm = memory_norm + jnp.sum(sigma_k, axis=(0, 1))
            w = jax.nn.sigmoid(memory_weight)
            out = (a_dot * (1.0 - w) + a_mem * w).reshape(B, S, D_MODEL)
            return (out, new_memory, new_memory_norm)
        key = jax.random.key(seed)
        ks = jax.random.split(key, 6)
        B, S = (2, 256)
        x = jax.random.normal(ks[0], (B, S, D_MODEL), jnp.float32)
        Wq = jax.random.normal(ks[1], (D_MODEL, D_MODEL), jnp.float32) / np.sqrt(D_MODEL)
        Wk = jax.random.normal(ks[2], (D_MODEL, KV), jnp.float32) / np.sqrt(D_MODEL)
        Wv = jax.random.normal(ks[3], (D_MODEL, KV), jnp.float32) / np.sqrt(D_MODEL)
        memory = jax.random.normal(ks[4], (KV, KV), jnp.float32)
        memory_norm = jnp.ones((KV,), jnp.float32)
        memory_weight = jnp.ones((1,), jnp.float32)
        return {'x': x, 'Wq': Wq, 'Wk': Wk, 'Wv': Wv, 'memory': memory, 'memory_norm': memory_norm, 'memory_weight': memory_weight}
    _L0_attn_all = _L0_attn_setup()
    _L0_attn_in = {k: v for k, v in _L0_attn_all.items() if k in ('Wq', 'Wk', 'Wv', 'memory', 'memory_norm', 'memory_weight')}
    del _L0_attn_all

    def _L0_ffn_setup():
        import jax, jax.numpy as jnp
        import numpy as np
        NEG_INF = -1e+30

        def _moe_forward(x, router_w, router_b, w1, b1, w2, b2, top_k=2):
            B, S, D = x.shape
            E = router_w.shape[1]
            logits = jnp.einsum('bsd,de->bse', x, router_w) + router_b
            top_vals, top_idx = jax.lax.top_k(logits, top_k)
            keep = jax.nn.one_hot(top_idx, E, dtype=logits.dtype).sum(-2) > 0
            sparse_logits = jnp.where(keep, logits, NEG_INF)
            gating = jax.nn.softmax(sparse_logits, axis=-1)
            xf = x.reshape(-1, D)
            gf = gating.reshape(-1, E)
            h = jax.nn.relu(jnp.einsum('td,edh->eth', xf, w1) + b1[:, None, :])
            y = jnp.einsum('eth,ehd->etd', h, w2) + b2[:, None, :]
            out = jnp.einsum('etd,te->td', y, gf)
            return out.reshape(B, S, D)
        key = jax.random.key(seed)
        ks = jax.random.split(key, 5)
        B, S, D, E, H = (2, 256, 128, 8, 512)
        scale = 0.02
        return {'x': jax.random.normal(ks[0], (B, S, D), dtype=jnp.float32), 'router_w': jax.random.normal(ks[1], (D, E), dtype=jnp.float32) * scale, 'router_b': jnp.zeros((E,), dtype=jnp.float32), 'w1': jax.random.normal(ks[2], (E, D, H), dtype=jnp.float32) * scale, 'b1': jnp.zeros((E, H), dtype=jnp.float32), 'w2': jax.random.normal(ks[3], (E, H, D), dtype=jnp.float32) * scale, 'b2': jnp.zeros((E, D), dtype=jnp.float32)}
    _L0_ffn_all = _L0_ffn_setup()
    _L0_ffn_in = {k: v for k, v in _L0_ffn_all.items() if k in ('router_w', 'router_b', 'w1', 'b1', 'w2', 'b2')}
    del _L0_ffn_all

    def _L1_xattn_setup():
        import jax, jax.numpy as jnp
        import numpy as np
        DIM = 128
        DIM_HEAD = 64
        NUM_HEADS = 16
        HIDDEN = DIM_HEAD * NUM_HEADS
        EPS = 1e-05

        def layer_norm(t, gamma, beta):
            mu = jnp.mean(t, axis=-1, keepdims=True)
            var = jnp.var(t, axis=-1, keepdims=True)
            return (t - mu) * jax.lax.rsqrt(var + EPS) * gamma + beta
        key = jax.random.key(seed)
        ks = jax.random.split(key, 12)
        B, F, Q = (8, 512, 64)
        x = jax.random.normal(ks[0], (B, F, DIM), dtype=jnp.float32)
        latents = jax.random.normal(ks[1], (B, Q, DIM), dtype=jnp.float32)
        mask = jax.random.randint(ks[2], (B, F), 0, 2) == 1
        s = 1.0 / np.sqrt(DIM)
        Wq = jax.random.normal(ks[3], (DIM, HIDDEN), dtype=jnp.float32) * s
        Wkv = jax.random.normal(ks[4], (DIM, 2 * HIDDEN), dtype=jnp.float32) * s
        Wout = jax.random.normal(ks[5], (HIDDEN, DIM), dtype=jnp.float32) * (1.0 / np.sqrt(HIDDEN))
        bout = jnp.zeros((DIM,), dtype=jnp.float32)
        g_media = jnp.ones((DIM,), dtype=jnp.float32)
        b_media = jnp.zeros((DIM,), dtype=jnp.float32)
        g_latent = jnp.ones((DIM,), dtype=jnp.float32)
        b_latent = jnp.zeros((DIM,), dtype=jnp.float32)
        return {'x': x, 'latents': latents, 'mask': mask, 'Wq': Wq, 'Wkv': Wkv, 'Wout': Wout, 'bout': bout, 'g_media': g_media, 'b_media': b_media, 'g_latent': g_latent, 'b_latent': b_latent}
    _L1_xattn_all = _L1_xattn_setup()
    _L1_xattn_in = {k: v for k, v in _L1_xattn_all.items() if k in ('Wq', 'Wkv', 'Wout', 'bout', 'g_media', 'b_media', 'g_latent', 'b_latent')}
    del _L1_xattn_all

    def _L1_attn_setup():
        import jax, jax.numpy as jnp
        import numpy as np
        B, L, DIM = (4, 256, 128)
        K = 4
        EXP = 192
        MULT = 4

        def layer_norm(x, g, b, eps=1e-05):
            m = jnp.mean(x, axis=-1, keepdims=True)
            v = jnp.var(x, axis=-1, keepdims=True)
            return (x - m) / jnp.sqrt(v + eps) * g + b

        def log_g(x):
            return jnp.where(x >= 0, jnp.log(jax.nn.relu(x) + 0.5), -jax.nn.softplus(-x))

        def parallel_scan_log(log_coeffs, log_values):
            a_star = jnp.pad(jnp.cumsum(log_coeffs, axis=1), ((0, 0), (1, 0), (0, 0)))
            log_h = a_star + jax.lax.cumlogsumexp(log_values - a_star, axis=1)
            return jnp.exp(log_h)[:, 1:]
        key = jax.random.key(seed)
        ks = jax.random.split(key, 8)
        s = 0.02
        return {'x': jax.random.normal(ks[0], (B, L, DIM), jnp.float32), 'dw_w': jax.random.normal(ks[1], (DIM, 1, K), jnp.float32) * s, 'dw_b': jnp.zeros((DIM,), jnp.float32), 'pw_w': jax.random.normal(ks[2], (DIM, DIM), jnp.float32) * s, 'pw_b': jnp.zeros((DIM,), jnp.float32), 'ln1_g': jnp.ones((DIM,), jnp.float32), 'ln1_b': jnp.zeros((DIM,), jnp.float32), 'f_w': jax.random.normal(ks[3], (2 * EXP, DIM), jnp.float32) * s, 'f_b': jnp.zeros((2 * EXP,), jnp.float32), 'dp_w': jax.random.normal(ks[4], (DIM, EXP), jnp.float32) * s, 'ln2_g': jnp.ones((DIM,), jnp.float32), 'ln2_b': jnp.zeros((DIM,), jnp.float32), 'mlp_w1': jax.random.normal(ks[5], (MULT * DIM, DIM), jnp.float32) * s, 'mlp_b1': jnp.zeros((MULT * DIM,), jnp.float32), 'mlp_w2': jax.random.normal(ks[6], (DIM, MULT * DIM), jnp.float32) * s, 'mlp_b2': jnp.zeros((DIM,), jnp.float32), 'ln3_g': jnp.ones((DIM,), jnp.float32), 'ln3_b': jnp.zeros((DIM,), jnp.float32)}
    _L1_attn_all = _L1_attn_setup()
    _L1_attn_in = {k: v for k, v in _L1_attn_all.items() if k in ('dw_w', 'dw_b', 'pw_w', 'pw_b', 'ln1_g', 'ln1_b', 'f_w', 'f_b', 'dp_w', 'ln2_g', 'ln2_b', 'mlp_w1', 'mlp_b1', 'mlp_w2', 'mlp_b2', 'ln3_g', 'ln3_b')}
    del _L1_attn_all

    def _L1_ffn_setup():
        import jax, jax.numpy as jnp
        import numpy as np
        HIDDEN = 128
        INNER = 512

        def _weight_quant(w):
            scale = 1.0 / jnp.clip(jnp.mean(jnp.abs(w)), 1e-05)
            wq = jnp.clip(jnp.round(w * scale), -1.0, 1.0) / scale
            return w + jax.lax.stop_gradient(wq - w)

        def _act_quant(x):
            scale = 127.0 / jnp.clip(jnp.max(jnp.abs(x), axis=-1, keepdims=True), 1e-05)
            xq = jnp.clip(jnp.round(x * scale), -128.0, 127.0) / scale
            return x + jax.lax.stop_gradient(xq - x)

        def _bitlinear(x, w):
            return jnp.einsum('bsi,oi->bso', _act_quant(x), _weight_quant(w))
        key = jax.random.key(seed)
        k0, k1, k2, k3 = jax.random.split(key, 4)
        x = jax.random.normal(k0, (4, 256, HIDDEN), dtype=jnp.float32)
        w_gate = jax.random.normal(k1, (INNER, HIDDEN), dtype=jnp.float32) / np.sqrt(HIDDEN)
        w_up = jax.random.normal(k2, (INNER, HIDDEN), dtype=jnp.float32) / np.sqrt(HIDDEN)
        w_down = jax.random.normal(k3, (HIDDEN, INNER), dtype=jnp.float32) / np.sqrt(INNER)
        return {'x': x, 'w_gate': w_gate, 'w_up': w_up, 'w_down': w_down}
    _L1_ffn_all = _L1_ffn_setup()
    _L1_ffn_in = {k: v for k, v in _L1_ffn_all.items() if k in ('w_gate', 'w_up', 'w_down')}
    del _L1_ffn_all
    return {'x': x, 'ctx_1024': ctx_1024, 'mask_Bx1x1xS2_fk0': mask_Bx1x1xS2_fk0, 'mask_BxS2_bk0': mask_BxS2_bk0, 'L0_xattn_Wq': _L0_xattn_in['Wq'], 'L0_xattn_bq': _L0_xattn_in['bq'], 'L0_xattn_Wk': _L0_xattn_in['Wk'], 'L0_xattn_bk': _L0_xattn_in['bk'], 'L0_xattn_Wv': _L0_xattn_in['Wv'], 'L0_xattn_bv': _L0_xattn_in['bv'], 'L0_xattn_Wo': _L0_xattn_in['Wo'], 'L0_xattn_bo': _L0_xattn_in['bo'], 'L0_attn_Wq': _L0_attn_in['Wq'], 'L0_attn_Wk': _L0_attn_in['Wk'], 'L0_attn_Wv': _L0_attn_in['Wv'], 'L0_attn_memory': _L0_attn_in['memory'], 'L0_attn_memory_norm': _L0_attn_in['memory_norm'], 'L0_attn_memory_weight': _L0_attn_in['memory_weight'], 'L0_ffn_router_w': _L0_ffn_in['router_w'], 'L0_ffn_router_b': _L0_ffn_in['router_b'], 'L0_ffn_w1': _L0_ffn_in['w1'], 'L0_ffn_b1': _L0_ffn_in['b1'], 'L0_ffn_w2': _L0_ffn_in['w2'], 'L0_ffn_b2': _L0_ffn_in['b2'], 'L1_xattn_Wq': _L1_xattn_in['Wq'], 'L1_xattn_Wkv': _L1_xattn_in['Wkv'], 'L1_xattn_Wout': _L1_xattn_in['Wout'], 'L1_xattn_bout': _L1_xattn_in['bout'], 'L1_xattn_g_media': _L1_xattn_in['g_media'], 'L1_xattn_b_media': _L1_xattn_in['b_media'], 'L1_xattn_g_latent': _L1_xattn_in['g_latent'], 'L1_xattn_b_latent': _L1_xattn_in['b_latent'], 'L1_attn_dw_w': _L1_attn_in['dw_w'], 'L1_attn_dw_b': _L1_attn_in['dw_b'], 'L1_attn_pw_w': _L1_attn_in['pw_w'], 'L1_attn_pw_b': _L1_attn_in['pw_b'], 'L1_attn_ln1_g': _L1_attn_in['ln1_g'], 'L1_attn_ln1_b': _L1_attn_in['ln1_b'], 'L1_attn_f_w': _L1_attn_in['f_w'], 'L1_attn_f_b': _L1_attn_in['f_b'], 'L1_attn_dp_w': _L1_attn_in['dp_w'], 'L1_attn_ln2_g': _L1_attn_in['ln2_g'], 'L1_attn_ln2_b': _L1_attn_in['ln2_b'], 'L1_attn_mlp_w1': _L1_attn_in['mlp_w1'], 'L1_attn_mlp_b1': _L1_attn_in['mlp_b1'], 'L1_attn_mlp_w2': _L1_attn_in['mlp_w2'], 'L1_attn_mlp_b2': _L1_attn_in['mlp_b2'], 'L1_attn_ln3_g': _L1_attn_in['ln3_g'], 'L1_attn_ln3_b': _L1_attn_in['ln3_b'], 'L1_ffn_w_gate': _L1_ffn_in['w_gate'], 'L1_ffn_w_up': _L1_ffn_in['w_up'], 'L1_ffn_w_down': _L1_ffn_in['w_down']}

def reference(x, ctx_1024, mask_Bx1x1xS2_fk0, mask_BxS2_bk0, L0_xattn_Wq, L0_xattn_bq, L0_xattn_Wk, L0_xattn_bk, L0_xattn_Wv, L0_xattn_bv, L0_xattn_Wo, L0_xattn_bo, L0_attn_Wq, L0_attn_Wk, L0_attn_Wv, L0_attn_memory, L0_attn_memory_norm, L0_attn_memory_weight, L0_ffn_router_w, L0_ffn_router_b, L0_ffn_w1, L0_ffn_b1, L0_ffn_w2, L0_ffn_b2, L1_xattn_Wq, L1_xattn_Wkv, L1_xattn_Wout, L1_xattn_bout, L1_xattn_g_media, L1_xattn_b_media, L1_xattn_g_latent, L1_xattn_b_latent, L1_attn_dw_w, L1_attn_dw_b, L1_attn_pw_w, L1_attn_pw_b, L1_attn_ln1_g, L1_attn_ln1_b, L1_attn_f_w, L1_attn_f_b, L1_attn_dp_w, L1_attn_ln2_g, L1_attn_ln2_b, L1_attn_mlp_w1, L1_attn_mlp_b1, L1_attn_mlp_w2, L1_attn_mlp_b2, L1_attn_ln3_g, L1_attn_ln3_b, L1_ffn_w_gate, L1_ffn_w_up, L1_ffn_w_down):
    import jax
    import jax.numpy as jnp

    def _L0_xattn_ref(query, key, value, mask, Wq, bq, Wk, bk, Wv, bv, Wo, bo):
        import jax, jax.numpy as jnp
        import numpy as np
        B, S, D, H = (2, 256, 128, 16)
        DH = D // H

        def _split_heads(x):
            b, s, _ = x.shape
            return x.reshape(b, s, H, DH).transpose(0, 2, 1, 3)
        q = _split_heads(query @ Wq + bq)
        k = _split_heads(key @ Wk + bk)
        v = _split_heads(value @ Wv + bv)
        logits = jnp.einsum('bhqd,bhkd->bhqk', q, k) / jnp.sqrt(jnp.float32(DH))
        logits = logits + mask * -1000000000.0
        attn = jax.nn.softmax(logits, axis=-1)
        out = jnp.einsum('bhqk,bhkd->bhqd', attn, v)
        out = out.transpose(0, 2, 1, 3).reshape(query.shape[0], -1, D)
        return out @ Wo + bo

    def _L0_attn_ref(x, Wq, Wk, Wv, memory, memory_norm, memory_weight):
        import jax, jax.numpy as jnp
        import numpy as np
        D_MODEL, N_QUERY, N_HEAD = (128, 2, 8)
        D_HEAD = D_MODEL // (N_QUERY * N_HEAD)
        KV = D_HEAD * N_HEAD

        def _reference_tuple_inner(x, Wq, Wk, Wv, memory, memory_norm, memory_weight):
            B, S, _ = x.shape
            QH = N_QUERY * N_HEAD
            scale = 1.0 / jnp.sqrt(jnp.float32(D_HEAD))
            q = x @ Wq
            k = x @ Wk
            v = x @ Wv
            q4 = q.reshape(B, S, QH, D_HEAD)
            k4 = jnp.repeat(k.reshape(B, S, N_HEAD, D_HEAD), N_QUERY, axis=2)
            v4 = jnp.repeat(v.reshape(B, S, N_HEAD, D_HEAD), N_QUERY, axis=2)
            scores = jnp.einsum('bsnd,btnd->bnst', q4, k4) * scale
            probs = jax.nn.softmax(scores, axis=-1)
            a_dot = jnp.einsum('bnst,btnd->bsnd', probs, v4)
            sigma_q = jax.nn.elu(q.reshape(B, S, N_QUERY, KV))
            num = sigma_q @ memory
            den = (sigma_q @ memory_norm)[..., None]
            a_mem = (num / den).reshape(B, S, QH, D_HEAD)
            sigma_k = jax.nn.elu(k)
            retrieved = sigma_k @ memory / (sigma_k @ memory_norm)[..., None]
            new_memory = memory + jnp.einsum('bsk,bsv->kv', sigma_k, v - retrieved)
            new_memory_norm = memory_norm + jnp.sum(sigma_k, axis=(0, 1))
            w = jax.nn.sigmoid(memory_weight)
            out = (a_dot * (1.0 - w) + a_mem * w).reshape(B, S, D_MODEL)
            return (out, new_memory, new_memory_norm)
        return _reference_tuple_inner(x, Wq, Wk, Wv, memory, memory_norm, memory_weight)[0]

    def _L0_ffn_ref(x, router_w, router_b, w1, b1, w2, b2):
        import jax, jax.numpy as jnp
        import numpy as np
        NEG_INF = -1e+30

        def _moe_forward(x, router_w, router_b, w1, b1, w2, b2, top_k=2):
            B, S, D = x.shape
            E = router_w.shape[1]
            logits = jnp.einsum('bsd,de->bse', x, router_w) + router_b
            top_vals, top_idx = jax.lax.top_k(logits, top_k)
            keep = jax.nn.one_hot(top_idx, E, dtype=logits.dtype).sum(-2) > 0
            sparse_logits = jnp.where(keep, logits, NEG_INF)
            gating = jax.nn.softmax(sparse_logits, axis=-1)
            xf = x.reshape(-1, D)
            gf = gating.reshape(-1, E)
            h = jax.nn.relu(jnp.einsum('td,edh->eth', xf, w1) + b1[:, None, :])
            y = jnp.einsum('eth,ehd->etd', h, w2) + b2[:, None, :]
            out = jnp.einsum('etd,te->td', y, gf)
            return out.reshape(B, S, D)
        return _moe_forward(x, router_w, router_b, w1, b1, w2, b2, top_k=2)

    def _L1_xattn_ref(x, latents, mask, Wq, Wkv, Wout, bout, g_media, b_media, g_latent, b_latent):
        import jax, jax.numpy as jnp
        import numpy as np
        DIM = 128
        DIM_HEAD = 64
        NUM_HEADS = 16
        HIDDEN = DIM_HEAD * NUM_HEADS
        EPS = 1e-05

        def layer_norm(t, gamma, beta):
            mu = jnp.mean(t, axis=-1, keepdims=True)
            var = jnp.var(t, axis=-1, keepdims=True)
            return (t - mu) * jax.lax.rsqrt(var + EPS) * gamma + beta
        B, F, _ = x.shape
        Q = latents.shape[1]
        scale = DIM_HEAD ** (-0.5)
        xn = layer_norm(x, g_media, b_media)
        ln = layer_norm(latents, g_latent, b_latent)
        q = (ln @ Wq).reshape(B, Q, NUM_HEADS, DIM_HEAD).transpose(0, 2, 1, 3) * scale
        kv_input = jnp.concatenate([xn, ln], axis=1)
        kv = kv_input @ Wkv
        k, v = jnp.split(kv, 2, axis=-1)
        k = k.reshape(B, F + Q, NUM_HEADS, DIM_HEAD).transpose(0, 2, 1, 3)
        v = v.reshape(B, F + Q, NUM_HEADS, DIM_HEAD).transpose(0, 2, 1, 3)
        sim = jnp.einsum('bhqd,bhfd->bhqf', q, k)
        latent_mask = jnp.zeros((B, Q), dtype=bool)
        full_mask = jnp.concatenate([mask, latent_mask], axis=1)
        max_neg = -jnp.finfo(sim.dtype).max
        sim = jnp.where(full_mask[:, None, None, :], max_neg, sim)
        alphas = jax.nn.softmax(sim, axis=-1)
        out = jnp.einsum('bhqf,bhfv->bhqv', alphas, v)
        out = out.transpose(0, 2, 1, 3).reshape(B, Q, HIDDEN)
        return out @ Wout + bout

    def _L1_attn_ref(x, dw_w, dw_b, pw_w, pw_b, ln1_g, ln1_b, f_w, f_b, dp_w, ln2_g, ln2_b, mlp_w1, mlp_b1, mlp_w2, mlp_b2, ln3_g, ln3_b):
        import jax, jax.numpy as jnp
        import numpy as np
        B, L, DIM = (4, 256, 128)
        K = 4
        EXP = 192
        MULT = 4

        def layer_norm(x, g, b, eps=1e-05):
            m = jnp.mean(x, axis=-1, keepdims=True)
            v = jnp.var(x, axis=-1, keepdims=True)
            return (x - m) / jnp.sqrt(v + eps) * g + b

        def log_g(x):
            return jnp.where(x >= 0, jnp.log(jax.nn.relu(x) + 0.5), -jax.nn.softplus(-x))

        def parallel_scan_log(log_coeffs, log_values):
            a_star = jnp.pad(jnp.cumsum(log_coeffs, axis=1), ((0, 0), (1, 0), (0, 0)))
            log_h = a_star + jax.lax.cumlogsumexp(log_values - a_star, axis=1)
            return jnp.exp(log_h)[:, 1:]
        res = x
        h = layer_norm(x, ln1_g, ln1_b).transpose(0, 2, 1)
        h = jnp.pad(h, ((0, 0), (0, 0), (K - 1, 0)))
        h = jax.lax.conv_general_dilated(h, dw_w, window_strides=(1,), padding='VALID', dimension_numbers=('NCH', 'OIH', 'NCH'), feature_group_count=DIM)
        h = h + dw_b[None, :, None]
        h = jnp.einsum('oc,bcl->bol', pw_w, h) + pw_b[None, :, None]
        x = h.transpose(0, 2, 1) + res
        res = x
        g = layer_norm(x, ln2_g, ln2_b)
        kh = g @ f_w.T + f_b
        k_, hx = jnp.split(kh, 2, axis=-1)
        log_z = -jax.nn.softplus(-k_)
        log_coeffs = -jax.nn.softplus(k_)
        log_tilde_h = log_g(hx)
        log_h0 = jnp.full((x.shape[0], 1, EXP), jnp.log(0.5), x.dtype)
        log_values = jnp.concatenate([log_h0, log_tilde_h + log_z], axis=1)
        hseq = parallel_scan_log(log_coeffs, log_values)
        x = hseq @ dp_w.T + res
        res = x
        m = layer_norm(x, ln3_g, ln3_b)
        m = jax.nn.gelu(m @ mlp_w1.T + mlp_b1, approximate=False)
        return m @ mlp_w2.T + mlp_b2 + res

    def _L1_ffn_ref(x, w_gate, w_up, w_down):
        import jax, jax.numpy as jnp
        import numpy as np
        HIDDEN = 128
        INNER = 512

        def _weight_quant(w):
            scale = 1.0 / jnp.clip(jnp.mean(jnp.abs(w)), 1e-05)
            wq = jnp.clip(jnp.round(w * scale), -1.0, 1.0) / scale
            return w + jax.lax.stop_gradient(wq - w)

        def _act_quant(x):
            scale = 127.0 / jnp.clip(jnp.max(jnp.abs(x), axis=-1, keepdims=True), 1e-05)
            xq = jnp.clip(jnp.round(x * scale), -128.0, 127.0) / scale
            return x + jax.lax.stop_gradient(xq - x)

        def _bitlinear(x, w):
            return jnp.einsum('bsi,oi->bso', _act_quant(x), _weight_quant(w))
        gate = jax.nn.silu(_bitlinear(x, w_gate))
        up = _bitlinear(x, w_up)
        return _bitlinear(gate * up, w_down)
    x = x + _L0_xattn_ref(_layernorm(x, axis=-1), ctx_1024, ctx_1024, mask_Bx1x1xS2_fk0, L0_xattn_Wq, L0_xattn_bq, L0_xattn_Wk, L0_xattn_bk, L0_xattn_Wv, L0_xattn_bv, L0_xattn_Wo, L0_xattn_bo)
    x = x + _L0_attn_ref(_layernorm(x, axis=-1), L0_attn_Wq, L0_attn_Wk, L0_attn_Wv, L0_attn_memory, L0_attn_memory_norm, L0_attn_memory_weight)
    x = x + _L0_ffn_ref(_layernorm(x, axis=-1), L0_ffn_router_w, L0_ffn_router_b, L0_ffn_w1, L0_ffn_b1, L0_ffn_w2, L0_ffn_b2)
    x = x + _L1_xattn_ref(ctx_1024, _layernorm(x, axis=-1), mask_BxS2_bk0, L1_xattn_Wq, L1_xattn_Wkv, L1_xattn_Wout, L1_xattn_bout, L1_xattn_g_media, L1_xattn_b_media, L1_xattn_g_latent, L1_xattn_b_latent)
    x = x + _L1_attn_ref(_layernorm(x, axis=-1), L1_attn_dw_w, L1_attn_dw_b, L1_attn_pw_w, L1_attn_pw_b, L1_attn_ln1_g, L1_attn_ln1_b, L1_attn_f_w, L1_attn_f_b, L1_attn_dp_w, L1_attn_ln2_g, L1_attn_ln2_b, L1_attn_mlp_w1, L1_attn_mlp_b1, L1_attn_mlp_w2, L1_attn_mlp_b2, L1_attn_ln3_g, L1_attn_ln3_b)
    x = x + _L1_ffn_ref(_layernorm(x, axis=-1), L1_ffn_w_gate, L1_ffn_w_up, L1_ffn_w_down)
    return x

_drawn_inputs = setup_inputs


def setup_inputs(seed=0):
    import zlib

    import numpy as np

    out = dict(_drawn_inputs(seed))
    spreads = {'L0_xattn_bq': (0.0, 0.1),
     'L0_xattn_bk': (0.0, 0.8),
     'L0_xattn_bv': (0.0, 0.1),
     'L0_xattn_bo': (0.0, 0.1),
     'L0_attn_memory_norm': (1.0, 0.2),
     'L0_ffn_router_b': (0.0, 0.8),
     'L0_ffn_b1': (0.0, 0.8),
     'L0_ffn_b2': (0.0, 0.8),
     'L1_xattn_bout': (0.0, 0.8),
     'L1_xattn_g_media': (1.0, 0.6),
     'L1_xattn_b_media': (0.0, 0.8),
     'L1_xattn_g_latent': (1.0, 0.6),
     'L1_xattn_b_latent': (0.0, 0.8),
     'L1_attn_dw_b': (0.0, 0.8),
     'L1_attn_pw_b': (0.0, 0.8),
     'L1_attn_ln1_g': (1.0, 0.6),
     'L1_attn_ln1_b': (0.0, 0.8),
     'L1_attn_f_b': (0.0, 0.8),
     'L1_attn_ln2_g': (1.0, 0.6),
     'L1_attn_ln2_b': (0.0, 0.8),
     'L1_attn_mlp_b1': (0.0, 0.8),
     'L1_attn_mlp_b2': (0.0, 0.8),
     'L1_attn_ln3_g': (1.0, 0.6),
     'L1_attn_ln3_b': (0.0, 0.8)}
    factors = {'L0_attn_Wk': 8.0,
     'L0_attn_Wv': 8.0,
     'L0_ffn_router_w': 8.0,
     'L0_ffn_w1': 8.0,
     'L0_ffn_w2': 8.0,
     'L1_xattn_Wq': 5.66,
     'L1_attn_dw_w': 8.0,
     'L1_attn_pw_w': 8.0,
     'L1_attn_f_w': 8.0,
     'L1_attn_dp_w': 8.0,
     'L1_attn_mlp_w1': 8.0,
     'L1_attn_mlp_w2': 8.0,
     'L1_ffn_w_gate': 8.0,
     'L1_ffn_w_up': 8.0,
     'L1_ffn_w_down': 8.0}
    for name, (base, spread) in spreads.items():
        noise = np.random.default_rng([zlib.crc32(name.encode()), seed]).standard_normal(out[name].shape)
        drawn = base * np.exp(spread * noise) if base else spread * noise
        out[name] = jnp.asarray(drawn.astype(out[name].dtype))
    for name, factor in factors.items():
        out[name] = (out[name] * factor).astype(out[name].dtype)
    return out
```

```python
import concourse.bass as bass
from concourse import mybir
from contextlib import ExitStack

F32 = mybir.dt.float32
BF16 = mybir.dt.bfloat16
ALU = mybir.AluOpType
ACT = mybir.ActivationFunctionType
AXX = mybir.AxisListType.X

BATCH, LAT, D, CTX = 64, 32, 128, 257
TOK = BATCH * LAT
HEADS = 16
CHUNK = 512
NCH = TOK // CHUNK
TILES = TOK // 128
EPS = 1e-5


def bf16_parts(value, count):
    import numpy as np

    parts = []
    rest = np.float32(value)
    for _ in range(count):
        part = (rest.view(np.uint32) & np.uint32(0xFFFF0000)).view(np.float32)
        parts.append(float(part))
        rest = np.float32(rest - part)
    return parts


class Core:

    def __init__(self, nc, ctx):
        self.nc, self.ctx = nc, ctx
        self.bank = ctx.enter_context(nc.psum_tensor("bank", [128, 8, CHUNK], F32))
        self.xT = self.sb("xT", [128, TOK])
        self.yT = self.sb("yT", [128, TOK])
        self.ident = self.sb("ident", [128, 128])
        self.mean_w = self.sb("mean_w", [128, 128])
        self.out = self.sb("rows_out", [128, TILES, 128])
        self.norm_sems = [self.sem(f"norm_{n}") for n in ("mean", "centred", "squared", "var", "log", "rstd", "scaled")]
        self.norms = 0
        self.eps = self.sb("eps", [128, 1])

    def sb(self, name, shape, dt=F32, ctx=None):
        return (ctx or self.ctx).enter_context(self.nc.sbuf_tensor(name, shape, dt))

    def sem(self, name):
        return self.ctx.enter_context(self.nc.semaphore(name))


def chunk(t, c):
    return t[:, c * CHUNK:(c + 1) * CHUNK]


def setup(core, xT_dram):
    nc = core.nc
    loaded, cleared, built = core.sem("x_loaded"), core.sem("const_cleared"), core.sem("const_built")
    with nc.Block() as block:

        @block.sync
        def _(sp):
            sp.dma_start(core.xT[:], xT_dram).then_inc(loaded, 16)
            sp.wait_ge(loaded, 16)

        @block.gpsimd
        def _(pool):
            nc.gpsimd.memset(core.ident[:], 0.0).then_inc(cleared, 1)
            nc.gpsimd.memset(core.mean_w[:], 1.0 / D).then_inc(built, 1)
            nc.gpsimd.memset(core.eps[:], EPS).then_inc(built, 1)
            pool.wait_ge(cleared, 1)
            nc.gpsimd.affine_select(out=core.ident[:], in_=core.ident[:], compare_op=ALU.not_equal, fill=1.0,
                                    base=0, pattern=[[-1, 128]], channel_multiplier=1).then_inc(built, 1)


def layernorm(core, name, src, dst, gamma=None, beta=None):
    nc = core.nc
    mean, var = core.bank[:, 0:4, :], core.bank[:, 4:8, :]
    with ExitStack() as own:
        sq = core.sb(f"{name}_sq", [128, TOK], ctx=own)
        rstd = core.sb(f"{name}_rstd", [128, TOK], ctx=own)
        mean_ready, centred, squared, var_ready, log_ready, rstd_ready, scaled = core.norm_sems
        before = core.norms * NCH
        core.norms += 1
        block = own.enter_context(nc.Block())

        @block.tensor
        def _(pe):
            for c in range(NCH):
                nc.tensor.matmul(mean[:, c, :], core.mean_w[:], chunk(src, c), start=True, stop=True).then_inc(mean_ready, 1)
            for c in range(NCH):
                pe.wait_ge(squared, before + c + 1)
                nc.tensor.matmul(var[:, c, :], core.mean_w[:], chunk(sq, c), start=True, stop=True).then_inc(var_ready, 1)

        @block.vector
        def _(dve):
            for c in range(NCH):
                dve.wait_ge(mean_ready, before + c + 1)
                nc.vector.tensor_tensor(chunk(dst, c), chunk(src, c), mean[:, c, :], ALU.subtract).then_inc(centred, 1)
            for c in range(NCH):
                dve.wait_ge(rstd_ready, before + c + 1)
                nc.vector.tensor_tensor(chunk(dst, c), chunk(dst, c), chunk(rstd, c), ALU.mult).then_inc(scaled, 1)
                if gamma is not None:
                    dve.wait_ge(scaled, before + c + 1)
                    nc.vector.tensor_scalar(chunk(dst, c), chunk(dst, c), gamma, beta, ALU.mult, ALU.add)

        @block.scalar
        def _(act):
            nc.scalar.preload_act_table_set("natural_log_exp_and_others")
            for c in range(NCH):
                act.wait_ge(centred, before + c + 1)
                nc.scalar.activation(chunk(sq, c), chunk(dst, c), ACT.Square).then_inc(squared, 1)
            for c in range(NCH):
                act.wait_ge(var_ready, before + c + 1)
                nc.scalar.activation(chunk(rstd, c), var[:, c, :], ACT.Ln, bias=core.eps[:, 0:1]).then_inc(log_ready, 1)
                act.wait_ge(log_ready, before + c + 1)
                nc.scalar.activation(chunk(rstd, c), chunk(rstd, c), ACT.Exp, scale=-0.5).then_inc(rstd_ready, 1)


def cross_attention_0(core, t):
    nc = core.nc
    DH = D // HEADS
    QUADS = 4
    UNITS = 2 * QUADS
    PAIRS = BATCH // 2
    layernorm(core, "ln0", core.xT, core.yT)
    with ExitStack() as own:
        sb = lambda n, s, dt=F32: core.sb(n, s, dt, own)
        sem = core.sem
        wq, wk, wv, wo = (sb(f"a_{n}", [128, 128]) for n in ("wq", "wk", "wv", "wo"))
        bias = sb("a_bias", [128, 4])
        qT = sb("a_qT", [128, TOK])
        oT = sb("a_oT", [128, TOK])
        head_of = sb("a_head_of", [128, HEADS])
        own_head = sb("a_own_head", [128, 4])
        group_of = sb("a_group_of", [4, 128])
        big = sb("a_big", [3, 128])
        ones3 = sb("a_ones3", [3, CTX])
        big_bf = sb("a_big_bf", [3, 128], BF16)
        ctT = sb("a_ctT", [128, 2, CTX])
        maskf = sb("a_maskf", [3, 2, CTX])
        maskb = sb("a_maskb", [3, 2, CTX], BF16)
        kT = sb("a_kT", [128, 2, CTX])
        v = sb("a_v", [128, 2, 2, 128])
        vlast = sb("a_vlast", [4, 2, 128])
        qb = sb("a_qb", [128, 2, HEADS, LAT])
        p = sb("a_p", [128, 2, QUADS, CTX])
        pT = sb("a_pT", [128, 2, 2, QUADS, 128])
        plast = sb("a_plast", [4, 2, 128])
        nmax = sb("a_nmax", [128, 2, QUADS])
        psum_ = sb("a_psum", [128, 2, QUADS])
        rsum = sb("a_rsum", [128, 2, QUADS])
        odiag = sb("a_odiag", [128, 4, LAT])
        S = [core.bank[:, n, 0:CTX] for n in (0, 1)]
        TP = [core.bank[:, n, 0:256] for n in (2, 3)]
        TL = core.bank[0:4, 7, 0:128]
        KP, VP = core.bank[:, 4, 0:CTX], core.bank[:, 5, :]
        OP = core.bank[:, 6, 0:128]

        w_loaded, q_made, q_copied = sem("a_w_loaded"), sem("a_q_made"), sem("a_q_copied")
        const_step = sem("a_const_step")
        ct_loaded = [sem(f"a_ct_loaded{n}") for n in (0, 1)]
        mask_loaded = [sem(f"a_mask_loaded{n}") for n in (0, 1)]
        mask_cast, qb_made = sem("a_mask_cast"), sem("a_qb_made")
        k_made, k_copied = sem("a_k_made"), sem("a_k_copied")
        v_made, v_copied = sem("a_v_made"), sem("a_v_copied")
        s_made, max_made, exp_made, recip_made, norm_made = (sem(f"a_{n}") for n in ("s_made", "max_made", "exp_made", "recip_made", "norm_made"))
        t_made, t_copied, tl_made, tl_copied = (sem(f"a_{n}") for n in ("t_made", "t_copied", "tl_made", "tl_copied"))
        o_made, o_masked, o_copied = sem("a_o_made"), sem("a_o_masked"), sem("a_o_copied")
        out_made, out_added = sem("a_out_made"), sem("a_out_added")

        with nc.Block() as block:

            @block.sync
            def _(sp):
                for dst, name in ((wq, "L0_xattn_Wq"), (wk, "L0_xattn_Wk"), (wv, "L0_xattn_Wv"), (wo, "L0_xattn_Wo")):
                    sp.dma_start(dst[:], t[name]).then_inc(w_loaded, 16)
                for n, name in enumerate(("L0_xattn_bq", "L0_xattn_bk", "L0_xattn_bv", "L0_xattn_bo")):
                    sp.dma_start(bias[:, n:n + 1], t[name]).then_inc(w_loaded, 16)
                sp.wait_ge(w_loaded, 128)

            @block.gpsimd
            def _(pool):
                nc.gpsimd.memset(head_of[:], 1.0).then_inc(const_step, 1)
                nc.gpsimd.memset(group_of[:], 1.0).then_inc(const_step, 1)
                nc.gpsimd.memset(ones3[:], 1.0)
                parts = bf16_parts(-1e9, 3)
                nc.gpsimd.memset(big[:], parts[0]).then_inc(const_step, 1)
                pool.wait_ge(const_step, 3)
                nc.gpsimd.affine_select(out=head_of[:], in_=head_of[:], compare_op=ALU.is_ge, fill=0.0, base=0,
                                        pattern=[[-DH, HEADS]], channel_multiplier=1).then_inc(const_step, 1)
                pool.wait_ge(const_step, 4)
                nc.gpsimd.affine_select(out=head_of[:], in_=head_of[:], compare_op=ALU.is_ge, fill=0.0, base=DH - 1,
                                        pattern=[[DH, HEADS]], channel_multiplier=-1).then_inc(const_step, 1)
                step = 5
                nc.gpsimd.affine_select(out=group_of[:], in_=group_of[:], compare_op=ALU.is_ge, fill=0.0, base=0,
                                        pattern=[[1, 128]], channel_multiplier=-32).then_inc(const_step, 1)
                step += 1
                pool.wait_ge(const_step, step)
                nc.gpsimd.affine_select(out=group_of[:], in_=group_of[:], compare_op=ALU.is_ge, fill=0.0, base=31,
                                        pattern=[[-1, 128]], channel_multiplier=32).then_inc(const_step, 1)
                step += 1
                for n in (1, 2):
                    nc.gpsimd.affine_select(out=big[:], in_=big[:], compare_op=ALU.is_ge, fill=parts[n], base=n - 1,
                                            pattern=[[0, 128]], channel_multiplier=-1).then_inc(const_step, 1)
                    step += 1
                    pool.wait_ge(const_step, step)
                nc.gpsimd.tensor_copy(big_bf[:], big[:]).then_inc(const_step, 1)

            @block.tensor
            def _(pe):
                pe.wait_ge(w_loaded, 128)
                for c in range(NCH):
                    nc.tensor.matmul(core.bank[:, c, :], wq[:], chunk(core.yT, c), start=True, stop=True).then_inc(q_made, 1)

            @block.vector
            def _(dve):
                dve.wait_ge(w_loaded, 128)
                dve.wait_ge(const_step, 5)
                nc.vector.tensor_reduce(own_head[:], head_of[:].rearrange("p (g h) -> p h g", g=QUADS), AXX, ALU.add)
                for c in range(NCH):
                    dve.wait_ge(q_made, c + 1)
                    nc.vector.tensor_scalar(chunk(qT, c), core.bank[:, c, :], bias[:, 0:1], DH ** -0.5,
                                            ALU.add, ALU.mult).then_inc(q_copied, 1)

        with nc.Block() as block:
            ct_dram, mask_dram = t["ctxT"], t["mask0"]

            def turns(eng, body):
                body(0, True, False)
                with eng.Fori(1, PAIRS - 1) as i:
                    body(i, False, False)
                body(PAIRS - 1, False, True)

            @block.sync
            def _(sp):
                def load(i, j, after):
                    if after is not None:
                        sp.wait_ge(v_made, after)
                        sp.wait_ge(mask_cast, after)
                    sp.dma_start(ctT[:, j, :], ct_dram[:, bass.ds((i * 2 + j) * CTX, CTX)]).then_inc(ct_loaded[j], 16)
                    sp.dma_start(maskf[:, j, :], mask_dram[:, bass.ds((i * 2 + j) * CTX, CTX)].broadcast_to([3, CTX])).then_inc(mask_loaded[j], 16)

                load(0, 0, None)
                load(0, 1, None)
                with sp.Fori(1, PAIRS) as i:
                    for j in range(2):
                        load(i, j, i * 2 + (j - 1))

            @block.gpsimd
            def _(pool):
                def prepare(i, j, first):
                    if not first:
                        pool.wait_ge(s_made, i * UNITS + QUADS * (j - 1))
                    pool.wait_ge(mask_loaded[j], i * 16 + 16)
                    nc.gpsimd.tensor_tensor(maskb[:, j, :], maskf[:, j, :], ones3[:], ALU.mult).then_inc(mask_cast, 1)
                    rows = qT[:, bass.ds((i * 2 + j) * LAT, LAT)].unsqueeze(1).broadcast_to([128, HEADS, LAT])
                    heads = head_of[:].unsqueeze(2).broadcast_to([128, HEADS, LAT])
                    nc.gpsimd.tensor_tensor(qb[:, j], rows, heads, ALU.mult).then_inc(qb_made, 1)

                prepare(0, 0, True)
                prepare(0, 1, True)
                with pool.Fori(1, PAIRS) as i:
                    for j in range(2):
                        prepare(i, j, False)

            @block.tensor
            def _(pe):
                def keys(i, j, first=False):
                    pe.wait_ge(ct_loaded[j % 2], (i + j // 2) * 16 + 16)
                    if not first:
                        pe.wait_ge(k_copied, i * 2 + j)
                    nc.tensor.matmul(KP, wk[:], ctT[:, j % 2, :], start=True, stop=True).then_inc(k_made, 1)

                def values(i, j, first=False):
                    if not first:
                        pe.wait_ge(v_copied, i * 2 + j)
                    for k in range(2):
                        nc.tensor.matmul(VP[:, 128 * k:128 * k + 128], ctT[:, j % 2, 128 * k:128 * k + 128], wv[:],
                                         start=True, stop=True)
                    nc.tensor.matmul(VP[0:4, 256:384], ctT[:, j % 2, 256:257].broadcast_to([128, 4]), wv[:],
                                     start=True, stop=True).then_inc(v_made, 1)

                def scores(i, s, first):
                    j, g = divmod(s, QUADS)
                    if g == 0:
                        pe.wait_ge(k_copied, i * 2 + j + 1)
                        pe.wait_ge(qb_made, i * 2 + j + 1)
                    if not (first and s < 2):
                        pe.wait_ge(exp_made, i * UNITS + (s - 1))
                    nc.tensor.matmul(S[s % 2], qb[:, j, 4 * g:4 * g + 4, :].rearrange("p h q -> p (h q)"), kT[:, j, :], start=True, stop=False)
                    nc.tensor.matmul(S[s % 2], big_bf[:], maskb[:, j, :], start=False, stop=True).then_inc(s_made, 1)

                def transposes(i, s, tfirst):
                    j, g = divmod(s % UNITS, QUADS)
                    pe.wait_ge(norm_made, i * UNITS + (s + 1))
                    if not tfirst:
                        pe.wait_ge(t_copied, i * UNITS + (s - 1))
                    for k in range(2):
                        ins = nc.tensor.transpose(TP[s % 2][:, 128 * k:128 * k + 128], p[:, j, g, 128 * k:128 * k + 128], core.ident[:])
                    ins.then_inc(t_made, 1)

                def output(i, j, first=False):
                    n, jj = i * 2 + j, j % 2
                    if not first:
                        pe.wait_ge(tl_copied, n)
                    nc.tensor.transpose(TL, p[:, jj, :, CTX - 1], core.ident[:]).then_inc(tl_made, 1)
                    pe.wait_ge(tl_copied, n + 1)
                    pe.wait_ge(t_copied, (n + 1) * QUADS)
                    pe.wait_ge(v_copied, n + 1)
                    if not first:
                        pe.wait_ge(o_masked, n)
                    nc.tensor.matmul(OP, vlast[:, jj, :], plast[:, jj, :], start=True, stop=False, skip_group_check=True)
                    for k in range(2):
                        for g in range(QUADS):
                            rows = slice(32 * g, 32 * g + 32)
                            ins = nc.tensor.matmul(OP[rows, :], v[:, jj, k, rows], pT[:, jj, k, g, :], start=False,
                                                   stop=(k == 1), skip_group_check=True)
                    ins.then_inc(o_made, 1)

                pe.wait_ge(w_loaded, 128)
                keys(0, 0, True)
                values(0, 0, True)

                def body(i, first, last):
                    for s in range(UNITS):
                        scores(i, s, first)
                        if not (first and s < 2):
                            transposes(i, s - 2, first and s < 4)
                        j, g = divmod(s, QUADS)
                        if g == 1 and not (last and j == 1):
                            keys(i, j + 1)
                        if g == 2:
                            if not (first and j == 0):
                                output(i, j - 1, first and j == 1)
                            if not (last and j == 1):
                                values(i, j + 1)

                turns(pe, body)
                transposes(PAIRS, -2, False)
                transposes(PAIRS, -1, False)
                output(PAIRS, -1)

            @block.scalar
            def _(act):
                def keys(i, j, first=False):
                    act.wait_ge(k_made, i * 2 + j + 1)
                    if not first:
                        act.wait_ge(s_made, (i * 2 + j - 1) * QUADS)
                    nc.scalar.activation(kT[:, j % 2, :], KP, ACT.Identity, bias=bias[:, 1:2]).then_inc(k_copied, 1)

                def transposed(i, s):
                    j, g = divmod(s % UNITS, QUADS)
                    act.wait_ge(t_made, i * UNITS + (s + 1))
                    nc.scalar.activation(pT[:, j, :, g, :], TP[s % 2].rearrange("p (k q) -> p k q", k=2), ACT.Copy).then_inc(t_copied, 1)

                def body(i, first, last):
                    for s in range(UNITS):
                        j, g = divmod(s, QUADS)
                        act.wait_ge(max_made, i * UNITS + (s + 1))
                        if g == 0 and not first:
                            act.wait_ge(tl_made, i * 2 + j - 1)
                        nc.scalar.activation(p[:, j, g, :], S[s % 2], ACT.Exp, bias=nmax[:, j, g:g + 1],
                                             accum_out=psum_[:, j, g:g + 1]).then_inc(exp_made, 1)
                        if not (first and s < 2):
                            if g == 2 and not first:
                                act.wait_ge(o_made, i * 2 + j - 1)
                            transposed(i, s - 2)
                        if g == 1 and not (last and j == 1):
                            keys(i, j + 1, first and j == 0)

                keys(0, 0, True)
                turns(act, body)
                transposed(PAIRS, -2)
                transposed(PAIRS, -1)

            @block.vector
            def _(dve):
                def values(i, j, first=False):
                    dve.wait_ge(v_made, i * 2 + j + 1)
                    if not first:
                        dve.wait_ge(o_made, i * 2 + j - 1)
                    nc.vector.tensor_copy(v[:, j % 2].rearrange("p k d -> p (k d)"), VP[:, 0:256])
                    nc.vector.tensor_tensor(vlast[:, j % 2, :], VP[0:4, 256:384], group_of[:], ALU.mult).then_inc(v_copied, 1)

                def normalise(i, s):
                    j, g = divmod(s % UNITS, QUADS)
                    dve.wait_ge(exp_made, i * UNITS + (s + 1))
                    nc.vector.reciprocal(rsum[:, j, g:g + 1], psum_[:, j, g:g + 1]).then_inc(recip_made, 1)
                    dve.wait_ge(recip_made, i * UNITS + (s + 1))
                    nc.vector.tensor_scalar(p[:, j, g, :], p[:, j, g, :], rsum[:, j, g:g + 1], None, ALU.mult).then_inc(norm_made, 1)

                def last_key(i, j):
                    n, jj = i * 2 + j, j % 2
                    dve.wait_ge(tl_made, n + 1)
                    nc.vector.tensor_copy(plast[:, jj, :], TL).then_inc(tl_copied, 1)

                def output(i, j, first=False):
                    n = i * 2 + j
                    dve.wait_ge(o_made, n + 1)
                    if not first:
                        dve.wait_ge(o_copied, n)
                    heads = own_head[:].unsqueeze(2).broadcast_to([128, 4, LAT])
                    nc.vector.tensor_tensor(odiag[:], OP.rearrange("p (h q) -> p h q", h=4), heads, ALU.mult).then_inc(o_masked, 1)
                    dve.wait_ge(o_masked, n + 1)
                    nc.vector.tensor_reduce(oT[:, bass.ds(n * LAT, LAT)], odiag[:].rearrange("p h q -> p q h"), AXX, ALU.add).then_inc(o_copied, 1)

                def body(i, first, last):
                    for s in range(UNITS):
                        j, g = divmod(s, QUADS)
                        dve.wait_ge(s_made, i * UNITS + (s + 1))
                        nc.vector.tensor_reduce(nmax[:, j, g:g + 1], S[s % 2], AXX, ALU.max, negate=True).then_inc(max_made, 1)
                        if not (first and s == 0):
                            normalise(i, s - 1)
                        if g == 2 and not (first and j == 0):
                            last_key(i, j - 1)
                        if g == 3:
                            if not (last and j == 1):
                                values(i, j + 1, first and j == 0)
                            if not (first and j == 0):
                                output(i, j - 1, first and j == 1)

                dve.wait_ge(w_loaded, 128)
                values(0, 0, True)
                turns(dve, body)
                normalise(PAIRS, -1)
                last_key(PAIRS, -1)
                output(PAIRS, -1)

        with nc.Block() as block:
            vb = sb("a_vb", [128, TOK])

            @block.vector
            def _(dve):
                for c in range(NCH):
                    nc.vector.tensor_scalar(chunk(vb, c), chunk(oT, c), bias[:, 2:3], None, ALU.add).then_inc(q_copied, 1)
                for c in range(NCH):
                    dve.wait_ge(out_made, c + 1)
                    nc.vector.scalar_tensor_tensor(chunk(core.xT, c), core.bank[:, c, :], bias[:, 3:4], chunk(core.xT, c),
                                                   ALU.add, ALU.add).then_inc(out_added, 1)

            @block.tensor
            def _(pe):
                for c in range(NCH):
                    pe.wait_ge(q_copied, NCH + c + 1)
                    nc.tensor.matmul(core.bank[:, c, :], wo[:], chunk(vb, c), start=True, stop=True).then_inc(out_made, 1)


def peeled(eng, turns, body):
    body(0, True, False)
    with eng.Fori(1, turns - 1) as i:
        body(i, False, False)
    body(turns - 1, False, True)


def memory_attention_0(core, t):
    nc = core.nc
    DH, KV = 8, 64
    GROUPS = BATCH // 4
    layernorm(core, "ln1", core.xT, core.yT)
    with ExitStack() as own:
        sb = lambda n, s, dt=F32: core.sb(n, s, dt, own)
        sem = core.sem
        wq, wk, wv = (sb(f"b_{n}", [128, 128]) for n in ("wq", "wk", "wv"))
        mem, norm = sb("b_mem", [128, 128]), sb("b_norm", [128, 128])
        norm_col, ones = sb("b_norm_col", [128, 1]), sb("b_ones", [128, KV])
        gate = sb("b_gate", [128, 4])
        qT, kT, aT = sb("b_qT", [128, TOK]), sb("b_kT", [128, TOK]), sb("b_aT", [128, TOK])
        own_head = sb("b_own_head", [128, 4])
        same_group = sb("b_same_group", [128, 128])
        w_loaded, zeroed, gate_step, mask_step = sem("b_w_loaded"), sem("b_zeroed"), sem("b_gate_step"), sem("b_mask_step")
        q_made, q_copied = sem("b_q_made"), sem("b_q_copied")

        with nc.Block() as block:

            @block.sync
            def _(sp):
                sp.wait_ge(zeroed, 1)
                sp.dma_start(wq[:], t["L0_attn_Wq"]).then_inc(w_loaded, 16)
                for dst, name in ((wk, "L0_attn_Wk"), (wv, "L0_attn_Wv")):
                    for r in range(2):
                        sp.dma_start(dst[:].rearrange("p (n r d) -> p n r d", r=2, d=DH)[:, :, r, :],
                                     t[name].rearrange("p (n d) -> p n d", d=DH)).then_inc(w_loaded, 16)
                for r in range(2):
                    rows = slice(KV * r, KV * r + KV)
                    sp.dma_start(mem[rows, rows], t["L0_attn_memory"]).then_inc(w_loaded, 16)
                    sp.dma_start(norm_col[rows, :], t["L0_attn_memory_norm"]).then_inc(w_loaded, 16)
                sp.dma_start(gate[:, 0:1], t["L0_attn_memory_weight"].broadcast_to([128, 1])).then_inc(w_loaded, 16)
                sp.wait_ge(w_loaded, 160)

            @block.gpsimd
            def _(pool):
                step = 0

                def select(m, base, pattern, by):
                    nonlocal step
                    pool.wait_ge(mask_step, step)
                    nc.gpsimd.affine_select(out=m, in_=m, compare_op=ALU.is_ge, fill=0.0, base=base, pattern=pattern,
                                            channel_multiplier=by).then_inc(mask_step, 1)
                    step += 1

                nc.gpsimd.memset(own_head[:], 1.0).then_inc(mask_step, 1)
                nc.gpsimd.memset(same_group[:], 1.0).then_inc(mask_step, 1)
                step = 2
                for g in range(4):
                    rows = own_head[32 * g:32 * g + 32, :]
                    select(rows, 0, [[-DH, 4]], 1)
                    select(rows, DH - 1, [[DH, 4]], -1)
                blocks = same_group[:].rearrange("p (g c) -> p g c", g=4)
                select(blocks, 0, [[-32, 4], [0, 32]], 1)
                select(blocks, 31, [[32, 4], [0, 32]], -1)

            @block.tensor
            def _(pe):
                pe.wait_ge(w_loaded, 160)
                for n, w in enumerate((wq, wk)):
                    for c in range(NCH):
                        nc.tensor.matmul(core.bank[:, n * NCH + c, :], w[:], chunk(core.yT, c), start=True, stop=True).then_inc(q_made, 1)

            @block.vector
            def _(dve):
                nc.vector.memset(mem[:], 0.0).then_inc(zeroed, 1)
                nc.vector.memset(norm[:], 0.0).then_inc(gate_step, 1)
                nc.vector.memset(ones[:], 1.0).then_inc(gate_step, 1)
                dve.wait_ge(w_loaded, 160)
                dve.wait_ge(gate_step, 2)
                for r in range(2):
                    rows = slice(KV * r, KV * r + KV)
                    nc.vector.tensor_scalar(norm[rows, rows], ones[rows, :], norm_col[rows, :], None, ALU.mult)
                for n, dst in enumerate((qT, kT)):
                    for c in range(NCH):
                        dve.wait_ge(q_made, n * NCH + c + 1)
                        nc.vector.tensor_copy(chunk(dst, c), core.bank[:, n * NCH + c, :]).then_inc(q_copied, 1)
                dve.wait_ge(gate_step, 3)
                nc.vector.tensor_scalar(gate[:, 2:3], gate[:, 1:2], 1.0, None, ALU.add).then_inc(gate_step, 1)
                dve.wait_ge(gate_step, 4)
                nc.vector.reciprocal(gate[:, 2:3], gate[:, 2:3]).then_inc(gate_step, 1)
                dve.wait_ge(gate_step, 5)
                nc.vector.tensor_scalar(gate[:, 3:4], gate[:, 2:3], -1.0, 1.0, ALU.mult, ALU.add)

            @block.scalar
            def _(act):
                act.wait_ge(w_loaded, 160)
                act.wait_ge(gate_step, 2)
                nc.scalar.activation(gate[:, 1:2], gate[:, 0:1], ACT.Exp, scale=-1.0).then_inc(gate_step, 1)

        with ExitStack() as loop:
            sb = lambda n, s, dt=F32: core.sb(n, s, dt, loop)
            qb = sb("b_qb", [128, 2, 4, 4, LAT])
            kg = sb("b_kg", [128, 2, 128])
            yg = sb("b_yg", [128, 2, 4, 4, LAT])
            vb = sb("b_vb", [128, 2, 4, 128])
            p = sb("b_p", [128, 2, 4, 4, LAT])
            pT = sb("b_pT", [128, 2, 4, 128])
            top, total, rtotal = sb("b_top", [128, 16]), sb("b_total", [128, 16]), sb("b_rtotal", [128, 16])
            odiag = sb("b_odiag", [128, 4, 4, LAT])
            S = core.bank[:, 0:4, 0:128].rearrange("p c (b k) -> p c b k", b=4)
            VP, TP, OP = (core.bank[:, n, :].rearrange("p (b k) -> p b k", b=4) for n in (4, 5, 6))
            qb_made, kg_made, v_made, v_copied, s_made = (sem(f"b_{n}") for n in ("qb_made", "kg_made", "v_made", "v_copied", "s_made"))
            top_made, shifted, exp_made, summed, recip, normed = (sem(f"b_{n}") for n in ("top_made", "shifted", "exp_made", "summed", "recip", "normed"))
            t_made, t_copied, o_made, o_masked, o_copied = (sem(f"b_{n}") for n in ("t_made", "t_copied", "o_made", "o_masked", "o_copied"))
            block = loop.enter_context(nc.Block())

            @block.gpsimd
            def _(pool):
                def body(i, first, last):
                    for j in range(2):
                        if not first:
                            pool.wait_ge(s_made, i * 2 + (j - 1))
                        toks = bass.ds((i * 2 + j) * 128, 128)
                        rows = qT[:, toks].rearrange("p (b q) -> p b q", b=4)
                        for b in range(4):
                            nc.gpsimd.tensor_tensor(qb[:, j, b], rows[:, b, :].unsqueeze(1).broadcast_to([128, 4, LAT]),
                                                    own_head[:].unsqueeze(2).broadcast_to([128, 4, LAT]), ALU.mult)
                        feats = core.yT[:, toks].rearrange("p (b q) -> p b q", b=4)
                        for g in range(4):
                            ins = nc.gpsimd.tensor_copy(yg[:, j, :, g, :], feats)
                        ins.then_inc(qb_made, 1)

                peeled(pool, GROUPS // 2, body)

            @block.tensor
            def _(pe):
                def scores(i, j, first):
                    n = i * 2 + j
                    pe.wait_ge(qb_made, n + 1)
                    if not first:
                        pe.wait_ge(v_copied, n)
                    for b in range(4):
                        nc.tensor.matmul(VP[:, b, :], yg[:, j, b].rearrange("p r q -> p (r q)"),
                                         wv[:], start=True, stop=True)
                    pe.wait_ge(kg_made, n + 1)
                    if not first:
                        pe.wait_ge(shifted, n)
                    for g in range(4):
                        rows = slice(32 * g, 32 * g + 32)
                        for b in range(4):
                            ins = nc.tensor.matmul(S[:, g, b, :], qb[rows, j, b].rearrange("p h q -> p (h q)"),
                                                   kg[rows, j, 32 * b:32 * b + 32], start=True, stop=True)
                    ins.then_inc(s_made, 1)

                def output(i, j, first):
                    n, jj = i * 2 + j, j % 2
                    pe.wait_ge(normed, n + 1)
                    if not first:
                        pe.wait_ge(t_copied, n)
                    for b in range(4):
                        ins = nc.tensor.transpose(TP[:, b, :], p[:, jj, b].rearrange("p c k -> p (c k)"), core.ident[:])
                    ins.then_inc(t_made, 1)
                    pe.wait_ge(t_copied, n + 1)
                    if not first:
                        pe.wait_ge(o_masked, n)
                    for b in range(4):
                        ins = nc.tensor.matmul(OP[:, b, :], vb[:, jj, b, :], pT[:, jj, b, :], start=True, stop=True)
                    ins.then_inc(o_made, 1)

                def body(i, first, last):
                    for j in range(2):
                        scores(i, j, first and j == 0)
                        if not (first and j == 0):
                            output(i, j - 1, first)

                peeled(pe, GROUPS // 2, body)
                output(GROUPS // 2, -1, False)

            @block.scalar
            def _(act):
                def transposed(i, j):
                    act.wait_ge(t_made, i * 2 + j + 1)
                    nc.scalar.activation(pT[:, j % 2], TP, ACT.Copy).then_inc(t_copied, 1)

                def body(i, first, last):
                    for j in range(2):
                        n = i * 2 + j
                        if not first:
                            act.wait_ge(s_made, n - 1)
                        nc.scalar.activation(kg[:, j, :], kT[:, bass.ds(n * 128, 128)], ACT.Copy, scale=DH ** -0.5).then_inc(kg_made, 1)
                        if not (first and j == 0):
                            transposed(i, j - 1)
                        act.wait_ge(shifted, n + 1)
                        nc.scalar.activation(p[:, j], p[:, j], ACT.Exp).then_inc(exp_made, 1)

                peeled(act, GROUPS // 2, body)
                transposed(GROUPS // 2, -1)

            @block.vector
            def _(dve):
                def output(i, j, first):
                    n = i * 2 + j
                    dve.wait_ge(o_made, n + 1)
                    if not first:
                        dve.wait_ge(o_copied, n)
                    for b in range(4):
                        ins = nc.vector.tensor_tensor(odiag[:, b], OP[:, b, :].rearrange("p (h q) -> p h q", h=4),
                                                      own_head[:].unsqueeze(2).broadcast_to([128, 4, LAT]), ALU.mult)
                    ins.then_inc(o_masked, 1)
                    dve.wait_ge(o_masked, n + 1)
                    nc.vector.tensor_reduce(aT[:, bass.ds(n * 128, 128)].rearrange("p (b q) -> p b q", b=4),
                                            odiag[:].rearrange("p b h q -> p b q h"), AXX, ALU.add).then_inc(o_copied, 1)

                def body(i, first, last):
                    for j in range(2):
                        n = i * 2 + j
                        dve.wait_ge(s_made, n + 1)
                        nc.vector.tensor_tensor(vb[:, j], VP, same_group[:].unsqueeze(1).broadcast_to([128, 4, 128]),
                                                ALU.mult).then_inc(v_copied, 1)
                        if not (first and j == 0):
                            dve.wait_ge(shifted, n)
                        nc.vector.tensor_reduce(top[:].rearrange("p (c b) -> p c b", c=4), S, AXX, ALU.max).then_inc(top_made, 1)
                        dve.wait_ge(top_made, n + 1)
                        for g in range(4):
                            ins = nc.vector.tensor_tensor(p[:, j, :, g, :], S[:, g], top[:, 4 * g:4 * g + 4].unsqueeze(2).broadcast_to([128, 4, LAT]),
                                                          ALU.subtract)
                        ins.then_inc(shifted, 1)
                        if not (first and j == 0):
                            output(i, j - 1, first)
                        dve.wait_ge(exp_made, n + 1)
                        if not (first and j == 0):
                            dve.wait_ge(normed, n)
                        nc.vector.tensor_reduce(total[:].rearrange("p (b c) -> p b c", c=4), p[:, j], AXX, ALU.add).then_inc(summed, 1)
                        dve.wait_ge(summed, n + 1)
                        nc.vector.reciprocal(rtotal[:], total[:]).then_inc(recip, 1)
                        dve.wait_ge(recip, n + 1)
                        nc.vector.tensor_tensor(p[:, j].rearrange("p b c k -> p (b c) k"), p[:, j].rearrange("p b c k -> p (b c) k"),
                                                rtotal[:].unsqueeze(2).broadcast_to([128, 16, LAT]), ALU.mult).then_inc(normed, 1)

                peeled(dve, GROUPS // 2, body)
                output(GROUPS // 2, -1, False)

        with ExitStack() as last:
            low, high = core.sb("b_low", [128, TOK], ctx=last), core.sb("b_high", [128, TOK], ctx=last)
            clipped, expd, elu_made = sem("b_clipped"), sem("b_expd"), sem("b_elu_made")
            num_made, den_made, chain = sem("b_num_made"), sem("b_den_made"), sem("b_chain")
            block = last.enter_context(nc.Block())

            @block.vector
            def _(dve):
                for c in range(NCH):
                    nc.vector.tensor_scalar(chunk(low, c), chunk(qT, c), 0.0, None, ALU.min).then_inc(clipped, 1)
                    nc.vector.tensor_scalar(chunk(high, c), chunk(qT, c), 0.0, None, ALU.max).then_inc(chain, 1)
                for c in range(NCH):
                    dve.wait_ge(expd, c + 1)
                    dve.wait_ge(chain, NCH)
                    nc.vector.scalar_tensor_tensor(chunk(high, c), chunk(low, c), -1.0, chunk(high, c), ALU.add, ALU.add).then_inc(elu_made, 1)
                done = NCH
                for c in range(NCH):
                    dve.wait_ge(den_made, c + 1)
                    nc.vector.reciprocal(chunk(low, c), core.bank[:, 4 + c, :]).then_inc(chain, 1)
                    done += 1
                    dve.wait_ge(chain, done)
                    dve.wait_ge(elu_made, NCH)
                    dve.wait_ge(num_made, NCH)
                    nc.vector.tensor_tensor(chunk(qT, c), core.bank[:, c, :], chunk(low, c), ALU.mult).then_inc(chain, 1)
                    done += 1
                    dve.wait_ge(chain, done)
                    nc.vector.scalar_tensor_tensor(chunk(core.xT, c), chunk(qT, c), gate[:, 2:3], chunk(core.xT, c), ALU.mult, ALU.add).then_inc(chain, 1)
                    done += 1
                    dve.wait_ge(chain, done)
                    nc.vector.scalar_tensor_tensor(chunk(core.xT, c), chunk(aT, c), gate[:, 3:4], chunk(core.xT, c), ALU.mult, ALU.add)

            @block.scalar
            def _(act):
                for c in range(NCH):
                    act.wait_ge(clipped, c + 1)
                    nc.scalar.activation(chunk(low, c), chunk(low, c), ACT.Exp).then_inc(expd, 1)

            @block.tensor
            def _(pe):
                for c in range(NCH):
                    pe.wait_ge(elu_made, c + 1)
                    nc.tensor.matmul(core.bank[:, c, :], mem[:], chunk(high, c), start=True, stop=True).then_inc(num_made, 1)
                    nc.tensor.matmul(core.bank[:, 4 + c, :], norm[:], chunk(high, c), start=True, stop=True).then_inc(den_made, 1)


def experts_0(core, t):
    nc = core.nc
    E, HID, KCH = 8, 512, 4
    layernorm(core, "ln2", core.xT, core.yT)
    with ExitStack() as own:
        sb = lambda n, s, dt=F32: core.sb(n, s, dt, own)
        sem = core.sem
        router, router_b = sb("c_router", [128, E]), sb("c_router_b", [128, E])
        b2 = sb("c_b2", [E, 128])
        acc = sb("c_acc", [128, TILES, 128])
        gates = sb("c_gates", [128, E, TILES])
        gT = sb("c_gT", [E, TILES, 128])
        w_loaded, logit_made, gate_step = sem("c_w_loaded"), sem("c_logit_made"), sem("c_gate_step")
        shifted, gates_made = sem("c_shifted"), sem("c_gates_made")
        rank_made, exp_made, gt_made, gt_copied, bias_made = sem("c_rank_made"), sem("c_exp_made"), sem("c_gt_made"), sem("c_gt_copied"), sem("c_bias_made")

        with ExitStack() as route:
            rb = lambda n: core.sb(n, [128, TILES, E], ctx=route)
            logit, left, rank, hit, keep, tmp = (rb(f"c_{n}") for n in ("logit", "left", "rank", "hit", "keep", "tmp"))
            best, top, pick = (core.sb(f"c_{n}", [128, TILES], ctx=route) for n in ("best", "top", "pick"))
            wide = lambda v: v[:].unsqueeze(2).broadcast_to([128, TILES, E])
            LG = core.bank[:, 0, 0:TILES * E].rearrange("p (t e) -> p t e", e=E)
            block = route.enter_context(nc.Block())

            @block.sync
            def _(sp):
                sp.dma_start(router[:], t["L0_ffn_router_w"]).then_inc(w_loaded, 16)
                sp.dma_start(router_b[:], t["L0_ffn_router_b"].broadcast_to([128, E])).then_inc(w_loaded, 16)
                sp.dma_start(b2[:], t["L0_ffn_b2"]).then_inc(w_loaded, 16)
                sp.wait_ge(w_loaded, 48)

            @block.gpsimd
            def _(pool):
                for e in range(E):
                    nc.gpsimd.memset(rank[:, :, e], float(E - e)).then_inc(rank_made, 1)

            @block.tensor
            def _(pe):
                pe.wait_ge(w_loaded, 48)
                for m in range(TILES):
                    ins = nc.tensor.matmul(LG[:, m, :], core.yT[:, 128 * m:128 * m + 128], router[:], start=True, stop=True)
                ins.then_inc(logit_made, 1)
                pe.wait_ge(gates_made, 1)
                for m in range(TILES):
                    ins = nc.tensor.transpose(core.bank[0:E, 1 + m // 4, 128 * (m % 4):128 * (m % 4) + 128], tmp[:, m, :], core.ident[:])
                ins.then_inc(gt_made, 1)
                pe.wait_ge(gt_copied, 1)
                for m in range(TILES):
                    ins = nc.tensor.matmul(core.bank[:, (5 + m // 4) % 8, 128 * (m % 4):128 * (m % 4) + 128], gT[:, m, :], b2[:], start=True, stop=True)
                    if m % 4 == 3:
                        ins.then_inc(bias_made, 1)

            @block.scalar
            def _(act):
                act.wait_ge(shifted, 1)
                nc.scalar.activation(tmp[:], tmp[:], ACT.Exp).then_inc(exp_made, 1)

            @block.vector
            def _(dve):
                step = 0

                def then(ins):
                    nonlocal step
                    ins.then_inc(gate_step, 1)
                    step += 1
                    dve.wait_ge(gate_step, step)

                v = nc.vector
                dve.wait_ge(logit_made, 1)
                dve.wait_ge(w_loaded, 48)
                dve.wait_ge(rank_made, E)
                then(v.tensor_tensor(logit[:], LG, router_b[:].unsqueeze(1).broadcast_to([128, TILES, E]), ALU.add))
                then(v.tensor_reduce(best[:], logit[:], AXX, ALU.max))
                then(v.tensor_tensor(hit[:], logit[:], wide(best), ALU.is_equal))
                then(v.tensor_tensor(hit[:], hit[:], rank[:], ALU.mult))
                then(v.tensor_reduce(pick[:], hit[:], AXX, ALU.max))
                then(v.tensor_tensor(keep[:], hit[:], wide(pick), ALU.is_equal))
                then(v.scalar_tensor_tensor(left[:], keep[:], -3e38, logit[:], ALU.mult, ALU.add))
                then(v.tensor_reduce(top[:], left[:], AXX, ALU.max))
                then(v.tensor_tensor(hit[:], left[:], wide(top), ALU.is_equal))
                then(v.tensor_tensor(hit[:], hit[:], rank[:], ALU.mult))
                then(v.tensor_reduce(pick[:], hit[:], AXX, ALU.max))
                then(v.tensor_tensor(hit[:], hit[:], wide(pick), ALU.is_equal))
                then(v.tensor_tensor(keep[:], keep[:], hit[:], ALU.add))
                v.tensor_tensor(tmp[:], logit[:], wide(best), ALU.subtract).then_inc(shifted, 1)
                dve.wait_ge(exp_made, 1)
                then(v.tensor_tensor(tmp[:], tmp[:], keep[:], ALU.mult))
                then(v.tensor_reduce(top[:], tmp[:], AXX, ALU.add))
                then(v.reciprocal(best[:], top[:]))
                then(v.tensor_tensor(tmp[:], tmp[:], wide(best), ALU.mult))
                v.tensor_copy(gates[:].rearrange("p e t -> p t e"), tmp[:]).then_inc(gates_made, 1)
                dve.wait_ge(gt_made, 1)
                v.tensor_copy(gT[:].rearrange("e (c m) k -> e c (m k)", c=NCH), core.bank[0:E, 1:5, :]).then_inc(gt_copied, 1)
                for c in range(NCH):
                    dve.wait_ge(bias_made, c + 1)
                    v.tensor_copy(acc[:, 4 * c:4 * c + 4, :].rearrange("p m d -> p (m d)"), core.bank[:, (5 + c) % 8, :])

        WIDTH = 2 * HID + KCH
        w = sb("c_w", [128, 2, WIDTH])
        hs = sb("c_hs", [128, 2, KCH, CHUNK])
        UP = [core.bank[:, k, :] for k in range(KCH)]
        Y = [core.bank[:, 4 + n, :].rearrange("p (m d) -> p m d", m=4) for n in (0, 1)]
        we_loaded = [sem(f"c_we_loaded{n}") for n in (0, 1)]
        up_made, relu_made, down_made, added = sem("c_up_made"), sem("c_relu_made"), sem("c_down_made"), sem("c_added")
        UNITS, TURNS = 2 * NCH, E // 2
        with nc.Block() as block:

            @block.sync
            def _(sp):
                def load(i, j):
                    sp.dma_start(w[:, j, :], t["L0_ffn_w"][:, bass.ds((i * 2 + j) * WIDTH, WIDTH)]).then_inc(we_loaded[j], 16)

                load(0, 0)
                load(0, 1)
                with sp.Fori(1, TURNS) as i:
                    for j in range(2):
                        sp.wait_ge(down_made, i * UNITS + NCH * (j - 1))
                        load(i, j)

            @block.tensor
            def _(pe):
                def up(i, s, first):
                    j, c = divmod(s, NCH)
                    if c == 0:
                        pe.wait_ge(we_loaded[j], i * 16 + 16)
                    for k in range(KCH):
                        if not (first and s == 0):
                            pe.wait_ge(relu_made, i * UNITS * KCH + ((s - 1) * KCH + k + 1))
                        nc.tensor.matmul(UP[k], w[:, j, 128 * k:128 * k + 128], chunk(core.yT, c), start=True, stop=True).then_inc(up_made, 1)

                def down(i, s, first):
                    j = s % UNITS // NCH
                    pe.wait_ge(relu_made, i * UNITS * KCH + (s + 1) * KCH)
                    if not first:
                        pe.wait_ge(added, i * UNITS + (s - 1))
                    for m in range(4):
                        for k in range(KCH):
                            ins = nc.tensor.matmul(Y[s % 2][:, m, :], hs[:, s % 2, k, 128 * m:128 * m + 128],
                                                   w[:, j, HID + 128 * k:HID + 128 * k + 128], start=(k == 0), stop=(k == KCH - 1))
                    ins.then_inc(down_made, 1)

                def body(i, first, last):
                    for s in range(UNITS):
                        up(i, s, first)
                        if not (first and s == 0):
                            down(i, s - 1, first and s < 3)

                peeled(pe, TURNS, body)
                down(TURNS, -1, False)

            @block.scalar
            def _(act):
                def body(i, first, last):
                    for s in range(UNITS):
                        if not (first and s < 2):
                            act.wait_ge(down_made, i * UNITS + (s - 1))
                        for k in range(KCH):
                            act.wait_ge(up_made, i * UNITS * KCH + (s * KCH + k + 1))
                            nc.scalar.activation(hs[:, s % 2, k, :], UP[k], ACT.Relu,
                                                 bias=w[:, s // NCH, 2 * HID + k:2 * HID + k + 1]).then_inc(relu_made, 1)

                peeled(act, TURNS, body)

            @block.vector
            def _(dve):
                def body(i, first, last):
                    for s in range(UNITS):
                        j, c = divmod(s, NCH)
                        dve.wait_ge(down_made, i * UNITS + (s + 1))
                        if not (first and s < NCH):
                            dve.wait_ge(added, i * UNITS + (s - NCH + 1))
                        for m in range(4):
                            tile = NCH * c + m
                            ins = nc.vector.scalar_tensor_tensor(acc[:, tile, :], Y[s % 2][:, m, :], gates[:, bass.ds(i * 2 + j, 1), tile],
                                                                 acc[:, tile, :], ALU.mult, ALU.add)
                        ins.then_inc(added, 1)

                peeled(dve, TURNS, body)

        acc_t = sem("c_acc_t")
        with nc.Block() as block:

            @block.tensor
            def _(pe):
                for m in range(TILES):
                    ins = nc.tensor.transpose(core.bank[:, m // 4, 128 * (m % 4):128 * (m % 4) + 128], acc[:, m, :], core.ident[:])
                    if m % 4 == 3:
                        ins.then_inc(acc_t, 1)

            @block.vector
            def _(dve):
                for c in range(NCH):
                    dve.wait_ge(acc_t, c + 1)
                    nc.vector.tensor_tensor(chunk(core.xT, c), chunk(core.xT, c), core.bank[:, c, :], ALU.add)


def cross_attention_1(core, t):
    nc = core.nc
    DH, KEYS = 64, CTX + LAT
    REST = KEYS - 256
    GROUPS, UNITS = BATCH // 4, 16
    layernorm(core, "ln3", core.xT, core.yT)
    with ExitStack() as own:
        sb = lambda n, s, dt=F32: core.sb(n, s, dt, own)
        sem = core.sem
        affine = sb("d_affine", [128, 5])
        latT = sb("d_latT", [128, TOK])
        keyT = sb("d_keyT", [128, BATCH, KEYS])
        wqk, wvo = sb("d_wqk", [128, HEADS, 128]), sb("d_wvo", [128, HEADS, 128])
        scratch = nc.dram_tensor("mask1_bf16", (BATCH, CTX), BF16, kind="Internal").ap()

        with ExitStack() as pre:
            w_loaded, made, mask_cast, mask_stored = sem("d_w_loaded"), sem("d_w_made"), sem("d_mask_cast"), sem("d_mask_stored")
            wqT, wkT, wvT, wout = (core.sb(f"d_{n}", [128, 8, 128], ctx=pre) for n in ("wqT", "wkT", "wvT", "wout"))
            mask8, mask16 = core.sb("d_mask8", [BATCH, CTX], mybir.dt.uint8, pre), core.sb("d_mask16", [BATCH, CTX], BF16, pre)
            block = pre.enter_context(nc.Block())

            @block.sync
            def _(sp):
                for dst, name in ((wqT, "L1_xattn_WqT"), (wkT, "L1_xattn_WkT"), (wvT, "L1_xattn_WvT"), (wout, "L1_xattn_Wout")):
                    sp.dma_start(dst[:].rearrange("p n d -> p (n d)"), t[name]).then_inc(w_loaded, 16)
                sp.dma_start(affine[:], t["L1_xattn_affine"]).then_inc(w_loaded, 16)
                sp.dma_start(mask8[:], t["mask1"]).then_inc(w_loaded, 16)
                sp.wait_ge(w_loaded, 96)
                sp.wait_ge(mask_cast, 1)
                sp.dma_start(scratch, mask16[:]).then_inc(mask_stored, 16)
                sp.wait_ge(mask_stored, 16)

            @block.tensor
            def _(pe):
                pe.wait_ge(w_loaded, 96)
                for n, (a, b) in enumerate(((wqT, wkT), (wvT, wout))):
                    for h in range(HEADS):
                        rows = slice(DH * (h % 2), DH * (h % 2) + DH)
                        at = 4 * n + 2 * (h % 2) + h // 8
                        ins = nc.tensor.matmul(core.bank[:, at, 128 * (h // 2 % 4):128 * (h // 2 % 4) + 128], a[rows, h // 2, :], b[rows, h // 2, :],
                                               start=True, stop=True)
                    ins.then_inc(made, 1)

            @block.vector
            def _(dve):
                dve.wait_ge(w_loaded, 96)
                nc.vector.tensor_copy(mask16[:], mask8[:]).then_inc(mask_cast, 1)
                for n, (dst, scale) in enumerate(((wqk, DH ** -0.5), (wvo, 1.0))):
                    dve.wait_ge(made, n + 1)
                    for odd in range(2):
                        out = dst[:].rearrange("p (m two) d -> p two m d", two=2)[:, odd]
                        src = core.bank[:, 4 * n + 2 * odd:4 * n + 2 * odd + 2, :].rearrange("p b (m d) -> p (b m) d", d=128)
                        nc.vector.tensor_scalar(out, src, scale, None, ALU.mult)

        layernorm(core, "ln4", core.yT, latT, affine[:, 2:3], affine[:, 3:4])

        with ExitStack() as norm:
            RING = 4
            ct = core.sb("d_ct", [128, RING, CTX], ctx=norm)
            xc, sq, rstd = (core.sb(f"d_{n}", [128, RING, CTX], ctx=norm) for n in ("xc", "sq", "rstd"))
            ct_loaded = [sem(f"d_ct_loaded{n}") for n in range(RING)]
            mean_made, centred, squared, var_made, logged, rooted, scaled, kept = (
                sem(f"d_{n}") for n in ("mean_made", "centred", "squared", "var_made", "logged", "rooted", "scaled", "kept"))
            MEAN = [core.bank[:, n, 0:CTX] for n in (0, 1)]
            VAR = [core.bank[:, n, 0:CTX] for n in (2, 3)]
            TURNS = BATCH // RING
            block = norm.enter_context(nc.Block())

            @block.sync
            def _(sp):
                for j in range(RING):
                    sp.dma_start(ct[:, j, :], t["ctxT"][:, j * CTX:(j + 1) * CTX]).then_inc(ct_loaded[j], 16)
                with sp.Fori(1, TURNS) as i:
                    for j in range(RING):
                        sp.wait_ge(centred, i * RING + (j - RING + 1))
                        sp.dma_start(ct[:, j, :], t["ctxT"][:, bass.ds((i * RING + j) * CTX, CTX)]).then_inc(ct_loaded[j], 16)

            @block.tensor
            def _(pe):
                def var(i, j, first):
                    pe.wait_ge(squared, i * RING + (j + 1))
                    if not first:
                        pe.wait_ge(logged, i * RING + (j - 1))
                    nc.tensor.matmul(VAR[j % 2], core.mean_w[:], sq[:, j % RING, :], start=True, stop=True).then_inc(var_made, 1)

                def body(i, first, last):
                    for j in range(RING):
                        pe.wait_ge(ct_loaded[j], i * 16 + 16)
                        if not (first and j < 2):
                            pe.wait_ge(centred, i * RING + (j - 1))
                        nc.tensor.matmul(MEAN[j % 2], core.mean_w[:], ct[:, j, :], start=True, stop=True).then_inc(mean_made, 1)
                        if not (first and j == 0):
                            var(i, j - 1, first and j < 3)

                peeled(pe, TURNS, body)
                var(TURNS, -1, False)

            @block.scalar
            def _(act):
                def root(i, j, first):
                    act.wait_ge(var_made, i * RING + (j + 1))
                    if not first:
                        act.wait_ge(scaled, i * RING + (j - RING + 1))
                    nc.scalar.activation(rstd[:, j % RING, :], VAR[j % 2], ACT.Ln, bias=core.eps[:, 0:1]).then_inc(logged, 1)
                    act.wait_ge(logged, i * RING + (j + 1))
                    nc.scalar.activation(rstd[:, j % RING, :], rstd[:, j % RING, :], ACT.Exp, scale=-0.5).then_inc(rooted, 1)

                def body(i, first, last):
                    for j in range(RING):
                        act.wait_ge(centred, i * RING + (j + 1))
                        if not first:
                            act.wait_ge(var_made, i * RING + (j - RING + 1))
                        nc.scalar.activation(sq[:, j, :], xc[:, j, :], ACT.Square).then_inc(squared, 1)
                        if not (first and j == 0):
                            root(i, j - 1, first)

                peeled(act, TURNS, body)
                root(TURNS, -1, False)

            @block.vector
            def _(dve):
                def scale(i, j):
                    dve.wait_ge(rooted, i * RING + (j + 1))
                    nc.vector.tensor_tensor(xc[:, j % RING, :], xc[:, j % RING, :], rstd[:, j % RING, :], ALU.mult).then_inc(scaled, 1)
                    dve.wait_ge(scaled, i * RING + (j + 1))
                    nc.vector.tensor_scalar(keyT[:, bass.ds(i * RING + j, 1), 0:CTX], xc[:, j % RING, :].unsqueeze(1), affine[:, 0:1], affine[:, 1:2],
                                            ALU.mult, ALU.add).then_inc(kept, 1)

                def body(i, first, last):
                    for j in range(RING):
                        dve.wait_ge(mean_made, i * RING + (j + 1))
                        if not first:
                            dve.wait_ge(kept, i * RING + (j - RING + 1))
                        nc.vector.tensor_tensor(xc[:, j, :], ct[:, j, :], MEAN[j % 2], ALU.subtract).then_inc(centred, 1)
                        if not (first and j < 2):
                            scale(i, j - 2)

                peeled(dve, TURNS, body)
                scale(TURNS, -2)
                scale(TURNS, -1)

            @block.gpsimd
            def _(pool):
                nc.gpsimd.tensor_copy(keyT[:, :, CTX:KEYS], latT[:].rearrange("p (b q) -> p b q", b=BATCH))

        key = sb("d_key", [128, 2, KEYS])
        maskb = sb("d_maskb", [1, 2, CTX], BF16)
        lowest = sb("d_lowest", [1, 128], BF16)
        xv = sb("d_xv", [128, 2, 3, 128])
        q = sb("d_q", [128, 4, HEADS, LAT])
        P = sb("d_p", [128, 4, KEYS])
        pT = sb("d_pT", [128, 2, 3, 128])
        nmax, total, rtotal = (sb(f"d_{n}", [128, 4]) for n in ("nmax", "total", "rtotal"))
        a = sb("d_a", [128, 4, HEADS, LAT])
        S = [core.bank[:, n, 0:KEYS] for n in (0, 1)]
        TP = [core.bank[:, n, 0:384] for n in (2, 3)]
        XP, OP = core.bank[:, 4, 0:384], core.bank[:, 5, :]
        Q = [core.bank[:, n, :] for n in (6, 7)]
        OUT = core.bank[:, 6, 0:128]
        key_loaded = [sem(f"d_key_loaded{n}") for n in (0, 1)]
        zeroed, low_made = sem("d_zeroed"), sem("d_low_made")
        xv_made, xv_copied, q_made, q_copied = sem("d_xv_made"), sem("d_xv_copied"), sem("d_q_made"), sem("d_q_copied")
        s_made, max_made, exp_made, recip, normed = (sem(f"d_{n}") for n in ("s_made", "max_made", "exp_made", "recip", "normed"))
        t_made, t_copied, o_made, o_copied = (sem(f"d_{n}") for n in ("t_made", "t_copied", "o_made", "o_copied"))
        out_made, out_added = sem("d_out_made"), sem("d_out_added")
        with nc.Block() as block:

            @block.sync
            def _(sp):
                def load(i, b, first):
                    n = i * 4 + b
                    if not first:
                        sp.wait_ge(s_made, (n - 1) * 4)
                        sp.wait_ge(xv_made, n - 1)
                    sp.dma_start(key[:, b % 2, :], keyT[:, bass.ds(n, 1), :].rearrange("p a k -> p (a k)")).then_inc(key_loaded[b % 2], 16)
                    sp.dma_start(maskb[:, b % 2, :], scratch[bass.ds(n, 1), :]).then_inc(key_loaded[b % 2], 16)

                load(0, 0, True)
                load(0, 1, True)
                load(0, 2, False)
                load(0, 3, False)
                with sp.Fori(1, GROUPS) as i:
                    for b in range(4):
                        load(i, b, False)

            @block.gpsimd
            def _(pool):
                nc.gpsimd.memset(lowest[:], -3.3895313892515355e38).then_inc(low_made, 1)

            @block.tensor
            def _(pe):
                def key_rows(i, b, first=False):
                    n = i * 4 + b
                    pe.wait_ge(key_loaded[b % 2], (i * 2 + b // 2) * 32 + 32)
                    if not first:
                        pe.wait_ge(xv_copied, n)
                    for k in range(3):
                        width = 128 if k < 2 else REST
                        ins = nc.tensor.transpose(XP[0:width, 128 * k:128 * k + 128], key[:, b % 2, 128 * k:128 * k + width], core.ident[:])
                    ins.then_inc(xv_made, 1)

                def queries(i, r, first=False):
                    if not (first and r < 2):
                        pe.wait_ge(q_copied, i * 4 + (r - 1))
                    if r == 0 and not first:
                        pe.wait_ge(out_added, i - 1)
                    for h in range(4):
                        ins = nc.tensor.matmul(Q[r % 2][:, 128 * h:128 * h + 128], wqk[:, 4 * r + h, :], latT[:, bass.ds(i * 128, 128)],
                                               start=True, stop=True)
                    ins.then_inc(q_made, 1)

                def scores(i, u, first):
                    b, g = divmod(u, 4)
                    if u == 0:
                        pe.wait_ge(q_copied, i * 4 + 4)
                    if g == 0:
                        pe.wait_ge(key_loaded[b % 2], (i * 2 + b // 2) * 32 + 32)
                    if not (first and u < 2):
                        pe.wait_ge(exp_made, i * UNITS + (u - 1))
                    nc.tensor.matmul(S[u % 2], q[:, b, 4 * g:4 * g + 4, :].rearrange("p h q -> p (h q)"), key[:, b % 2, :], start=True, stop=False)
                    nc.tensor.matmul(S[u % 2][:, 0:CTX], lowest[:], maskb[:, b % 2, :], start=False, stop=True).then_inc(s_made, 1)

                def transposes(i, u, first):
                    pe.wait_ge(normed, i * UNITS + (u + 1))
                    if not (first and u < 2):
                        pe.wait_ge(t_copied, i * UNITS + (u - 1))
                    for k in range(3):
                        width = 128 if k < 2 else REST
                        ins = nc.tensor.transpose(TP[u % 2][0:width, 128 * k:128 * k + 128], P[:, u % 4, 128 * k:128 * k + width], core.ident[:])
                    ins.then_inc(t_made, 1)

                def means(i, u, first):
                    b, g = divmod(u, 4)
                    if g == 0:
                        pe.wait_ge(xv_copied, i * 4 + (b + 1))
                        if not (first and b == 0):
                            pe.wait_ge(o_copied, i * 4 + b)
                    pe.wait_ge(t_copied, i * UNITS + (u + 1))
                    for k in range(3):
                        width = 128 if k < 2 else REST
                        ins = nc.tensor.matmul(OP[:, 128 * g:128 * g + 128], xv[0:width, b % 2, k, :], pT[0:width, u % 2, k, :],
                                               start=(k == 0), stop=(k == 2))
                    ins.then_inc(o_made, 1)

                def project(i):
                    pe.wait_ge(o_copied, i * 4 + 4)
                    pe.wait_ge(q_copied, i * 4 + 7)
                    for h in range(HEADS):
                        ins = nc.tensor.matmul(OUT, wvo[:, h, :], a[:, :, h, :], start=(h == 0), stop=(h == HEADS - 1))
                    ins.then_inc(out_made, 1)

                pe.wait_ge(low_made, 1)
                pe.wait_ge(zeroed, 1)
                for r in range(4):
                    queries(0, r, True)
                key_rows(0, 0, True)

                def body(i, first, last):
                    for u in range(UNITS):
                        scores(i, u, first)
                        if u >= 2:
                            transposes(i, u - 2, first)
                        if u >= 3:
                            means(i, u - 3, first)
                        if u % 4 == 1 and not (last and u // 4 == 3):
                            key_rows(i, u // 4 + 1)
                    if not last:
                        queries(i + 1, 0)
                    transposes(i, UNITS - 2, first)
                    means(i, UNITS - 3, first)
                    if not last:
                        queries(i + 1, 1)
                    transposes(i, UNITS - 1, first)
                    means(i, UNITS - 2, first)
                    if not last:
                        queries(i + 1, 2)
                        queries(i + 1, 3)
                    means(i, UNITS - 1, first)
                    if last:
                        pe.wait_ge(o_copied, i * 4 + 4)
                        for h in range(HEADS):
                            ins = nc.tensor.matmul(OUT, wvo[:, h, :], a[:, :, h, :], start=(h == 0), stop=(h == HEADS - 1))
                        ins.then_inc(out_made, 1)
                    else:
                        project(i)

                peeled(pe, GROUPS, body)

            @block.scalar
            def _(act):
                def queries(i, r):
                    act.wait_ge(q_made, i * 4 + (r + 1))
                    if r == 0:
                        act.wait_ge(s_made, i * UNITS)
                    nc.scalar.activation(q[:, :, 4 * r:4 * r + 4, :].rearrange("p b h q -> p h b q"),
                                         Q[r % 2].rearrange("p (h b q) -> p h b q", h=4, b=4), ACT.Copy).then_inc(q_copied, 1)

                def transposed(i, u, first):
                    act.wait_ge(t_made, i * UNITS + (u + 1))
                    if not (first and u < 2):
                        act.wait_ge(o_made, i * UNITS + (u - 1))
                    nc.scalar.activation(pT[:, u % 2].rearrange("p k q -> p (k q)"), TP[u % 2], ACT.Copy).then_inc(t_copied, 1)

                def body(i, first, last):
                    for u in range(UNITS):
                        act.wait_ge(max_made, i * UNITS + (u + 1))
                        if not (first and u < 4):
                            act.wait_ge(t_made, i * UNITS + (u - 3))
                        nc.scalar.activation(P[:, u % 4, :], S[u % 2], ACT.Exp, bias=nmax[:, u % 4:u % 4 + 1],
                                             accum_out=total[:, u % 4:u % 4 + 1]).then_inc(exp_made, 1)
                        if u >= 2:
                            transposed(i, u - 2, first)
                    if not last:
                        queries(i + 1, 0)
                    transposed(i, UNITS - 2, first)
                    if not last:
                        queries(i + 1, 1)
                    transposed(i, UNITS - 1, first)
                    if not last:
                        queries(i + 1, 2)
                        queries(i + 1, 3)

                for r in range(4):
                    act.wait_ge(q_made, r + 1)
                    nc.scalar.activation(q[:, :, 4 * r:4 * r + 4, :].rearrange("p b h q -> p h b q"),
                                         Q[r % 2].rearrange("p (h b q) -> p h b q", h=4, b=4), ACT.Copy).then_inc(q_copied, 1)
                peeled(act, GROUPS, body)

            @block.vector
            def _(dve):
                def key_rows(i, b, first=False):
                    n = i * 4 + b
                    dve.wait_ge(xv_made, n + 1)
                    if not first:
                        dve.wait_ge(o_made, (n - 1) * 4)
                    nc.vector.tensor_copy(xv[:, b % 2].rearrange("p k d -> p (k d)"), XP).then_inc(xv_copied, 1)

                def normalise(i, u):
                    dve.wait_ge(exp_made, i * UNITS + (u + 1))
                    nc.vector.reciprocal(rtotal[:, u % 4:u % 4 + 1], total[:, u % 4:u % 4 + 1]).then_inc(recip, 1)
                    dve.wait_ge(recip, i * UNITS + (u + 1))
                    nc.vector.tensor_scalar(P[:, u % 4, :], P[:, u % 4, :], rtotal[:, u % 4:u % 4 + 1], None, ALU.mult).then_inc(normed, 1)

                def means(i, b, first):
                    dve.wait_ge(o_made, i * UNITS + 4 * b + 4)
                    if b == 0 and not first:
                        dve.wait_ge(out_made, i)
                    nc.vector.tensor_copy(a[:, b].rearrange("p h q -> p (h q)"), OP).then_inc(o_copied, 1)

                def body(i, first, last):
                    for u in range(UNITS):
                        dve.wait_ge(s_made, i * UNITS + (u + 1))
                        nc.vector.tensor_reduce(nmax[:, u % 4:u % 4 + 1], S[u % 2], AXX, ALU.max, negate=True).then_inc(max_made, 1)
                        if u >= 1:
                            normalise(i, u - 1)
                        if u % 4 == 2:
                            if u > 4:
                                means(i, u // 4 - 1, first)
                            if not (last and u // 4 == 3):
                                key_rows(i, u // 4 + 1, first and u < 4)
                    normalise(i, UNITS - 1)
                    means(i, 3, first)
                    dve.wait_ge(out_made, i + 1)
                    toks = bass.ds(i * 128, 128)
                    nc.vector.scalar_tensor_tensor(core.xT[:, toks], OUT, affine[:, 4:5], core.xT[:, toks], ALU.add, ALU.add).then_inc(out_added, 1)

                nc.vector.memset(XP, 0.0)
                for n in range(2):
                    ins = nc.vector.memset(TP[n], 0.0)
                ins.then_inc(zeroed, 1)
                key_rows(0, 0, True)
                peeled(dve, GROUPS, body)


def recurrent_1(core, t):
    nc = core.nc
    EXP, K, KCH = 192, 4, 4
    PER = CHUNK // LAT
    layernorm(core, "ln5", core.xT, core.yT)
    with ExitStack() as own:
        sb = lambda n, s, dt=F32: core.sb(n, s, dt, own)
        sem = core.sem
        cols = sb("e_cols", [128, 17])
        fb = sb("e_fb", [128, 4])
        fneg, fhalf = sb("e_fneg", [128, 4]), sb("e_fhalf", [128, 4])
        pw, fw, dpa, dpb = sb("e_pw", [128, 128]), sb("e_fw", [128, 2 * EXP]), sb("e_dpa", [128, 128]), sb("e_dpb", [64, 128])
        w1, w2 = sb("e_w1", [128, 512]), sb("e_w2", [128, KCH, 128])
        hT = sb("e_hT", [128, TOK])
        w_loaded = sem("e_w_loaded")

        with nc.Block() as block:

            @block.sync
            def _(sp):
                for dst, name in ((cols[:], "cols"), (fb[:], "f_b"), (pw[:], "pwT"), (fw[:], "fT"), (dpa[:], "dpT"), (w1[:], "mlp_w1T"),
                                  (w2[:].rearrange("p k d -> p (k d)"), "mlp_w2T")):
                    src = t[f"L1_attn_{name}"]
                    sp.dma_start(dst, src[0:128, :]).then_inc(w_loaded, 16)
                sp.dma_start(dpb[:], t["L1_attn_dpT"][128:EXP, :]).then_inc(w_loaded, 16)
                sp.wait_ge(w_loaded, 128)

        layernorm(core, "ln6", core.yT, hT, cols[:, 0:1], cols[:, 1:2])

        with ExitStack() as part:
            cT = core.sb("e_cT", [128, TOK], ctx=part)
            tap, conv_made, pw_made, b_made = sem("e_tap"), sem("e_conv_made"), sem("e_pw_made"), sem("e_b_made")
            block = part.enter_context(nc.Block())

            @block.vector
            def _(dve):
                nc.vector.tensor_scalar(fneg[:], fb[:], -1.0, None, ALU.mult)
                nc.vector.tensor_scalar(fhalf[:], fb[:], 0.5, None, ALU.add)
                for k in range(K):
                    for c in range(NCH):
                        src, dst = (chunk(v, c).rearrange("p (b t) -> p b t", t=LAT) for v in (hT, cT))
                        weight = cols[:, 9 + K - 1 - k:9 + K - k]
                        if k == 0:
                            ins = nc.vector.tensor_scalar(dst, src, weight, cols[:, 8:9], ALU.mult, ALU.add)
                        else:
                            dve.wait_ge(tap, (k - 1) * NCH + c + 1)
                            ins = nc.vector.scalar_tensor_tensor(dst[:, :, k:], src[:, :, :LAT - k], weight, dst[:, :, k:], ALU.mult, ALU.add)
                        ins.then_inc(tap, 1)
                for c in range(NCH):
                    dve.wait_ge(pw_made, c + 1)
                    nc.vector.scalar_tensor_tensor(chunk(core.yT, c), core.bank[:, c, :], cols[:, 6:7], chunk(core.yT, c), ALU.add, ALU.add)

            @block.tensor
            def _(pe):
                for c in range(NCH):
                    pe.wait_ge(tap, (K - 1) * NCH + c + 1)
                    nc.tensor.matmul(core.bank[:, c, :], pw[:], chunk(cT, c), start=True, stop=True).then_inc(pw_made, 1)

        layernorm(core, "ln7", core.yT, hT, cols[:, 2:3], cols[:, 3:4])

        with ExitStack() as part:
            pb = lambda n: core.sb(n, [128, 2, CHUNK], ctx=part)
            kept, new, cand, seq = (
                [pb(f"e_{n}{h}") for h in (0, 1)] for n in ("kept", "new", "cand", "seq"))
            f_made, sig_made, step, scanned, dp_made, dp_added = (
                sem(f"e_{n}") for n in ("f_made", "sig_made", "step", "scanned", "dp_made", "dp_added"))
            ROWS = (128, 64)
            COLS = (0, 128, EXP, EXP + 128)
            block = part.enter_context(nc.Block())

            @block.tensor
            def _(pe):
                def gates(c):
                    if c >= 2:
                        pe.wait_ge(dp_added, c - 1)
                    for n in range(4):
                        rows = ROWS[n % 2]
                        ins = nc.tensor.matmul(core.bank[0:rows, 4 * (c % 2) + n, :], fw[:, COLS[n]:COLS[n] + rows], chunk(hT, c), start=True, stop=True)
                    ins.then_inc(f_made, 1)

                gates(0)
                gates(1)
                for c in range(NCH):
                    pe.wait_ge(scanned, 2 * c + 2)
                    out = core.bank[:, 4 * (c % 2), :]
                    nc.tensor.matmul(out, dpa[:], seq[0][:, c % 2, :], start=True, stop=False)
                    nc.tensor.matmul(out, dpb[:], seq[1][0:64, c % 2, :], start=False, stop=True).then_inc(dp_made, 1)
                    if c + 2 < NCH:
                        gates(c + 2)

            @block.scalar
            def _(act):
                for c in range(NCH):
                    act.wait_ge(f_made, c + 1)
                    if c >= 2:
                        act.wait_ge(scanned, 2 * (c - 1))
                    for h, rows in enumerate(ROWS):
                        bank = [core.bank[0:rows, 4 * (c % 2) + n, :] for n in (h, 2 + h)]
                        r = slice(0, rows)
                        nc.scalar.activation(new[h][r, c % 2, :], bank[0], ACT.Sigmoid, bias=fb[r, h:h + 1])
                        nc.scalar.activation(kept[h][r, c % 2, :], bank[0], ACT.Sigmoid, bias=fneg[r, h:h + 1], scale=-1.0)
                        nc.scalar.activation(cand[h][r, c % 2, :], bank[1], ACT.Sigmoid, bias=fb[r, 2 + h:3 + h]).then_inc(sig_made, 1)

            @block.vector
            def _(dve):
                n = 0

                def then(ins):
                    nonlocal n
                    ins.then_inc(step, 1)
                    n += 1
                    dve.wait_ge(step, n)

                for c in range(NCH):
                    for h, rows in enumerate(ROWS):
                        r = slice(0, rows)
                        k_, n_, c_, s_ = (v[h][r, c % 2, :] for v in (kept, new, cand, seq))
                        dve.wait_ge(sig_made, 2 * c + h + 1)
                        if c >= 2:
                            dve.wait_ge(dp_made, c - 1)
                        then(nc.vector.scalar_tensor_tensor(c_, core.bank[r, 4 * (c % 2) + 2 + h, :], fhalf[r, 2 + h:3 + h], c_, ALU.add, ALU.max))
                        then(nc.vector.tensor_tensor(n_, n_, c_, ALU.mult))
                        first_k, first_n = (v.rearrange("p (b t) -> p b t", t=LAT)[:, :, 0:1] for v in (k_, n_))
                        then(nc.vector.scalar_tensor_tensor(first_n, first_k, 0.5, first_n, ALU.mult, ALU.add))
                        then(nc.vector.tensor_scalar(first_k, first_k, 0.0, None, ALU.mult))
                        nc.vector.tensor_tensor_scan(s_, k_, n_, 0.0, ALU.mult, ALU.add).then_inc(scanned, 1)
                    dve.wait_ge(dp_made, c + 1)
                    nc.vector.tensor_tensor(chunk(core.yT, c), chunk(core.yT, c), core.bank[:, 4 * (c % 2), :], ALU.add).then_inc(dp_added, 1)

        layernorm(core, "ln8", core.yT, hT, cols[:, 4:5], cols[:, 5:6])

        with ExitStack() as part:
            mid = core.sb("e_mid", [128, 2, KCH, CHUNK], ctx=part)
            up_made, act_made, down_made, summed = sem("e_up_made"), sem("e_act_made"), sem("e_down_made"), sem("e_summed")
            block = part.enter_context(nc.Block())

            @block.tensor
            def _(pe):
                def up(c):
                    for k in range(KCH):
                        if c >= 1:
                            pe.wait_ge(act_made, (c - 1) * KCH + k + 1)
                        nc.tensor.matmul(core.bank[:, k, :], w1[:, 128 * k:128 * k + 128], chunk(hT, c), start=True, stop=True).then_inc(up_made, 1)

                up(0)
                for c in range(NCH):
                    if c + 1 < NCH:
                        up(c + 1)
                    pe.wait_ge(act_made, (c + 1) * KCH)
                    for k in range(KCH):
                        ins = nc.tensor.matmul(core.bank[:, 4 + c, :], w2[:, k, :], mid[:, c % 2, k, :], start=(k == 0), stop=(k == KCH - 1))
                    ins.then_inc(down_made, 1)

            @block.scalar
            def _(act):
                for c in range(NCH):
                    if c >= 2:
                        act.wait_ge(down_made, c - 1)
                    for k in range(KCH):
                        act.wait_ge(up_made, c * KCH + k + 1)
                        nc.scalar.activation(mid[:, c % 2, k, :], core.bank[:, k, :], ACT.Gelu, bias=cols[:, 13 + k:14 + k]).then_inc(act_made, 1)

            @block.vector
            def _(dve):
                for c in range(NCH):
                    nc.vector.tensor_tensor(chunk(core.xT, c), chunk(core.xT, c), chunk(core.yT, c), ALU.add).then_inc(summed, 1)
                for c in range(NCH):
                    dve.wait_ge(down_made, c + 1)
                    dve.wait_ge(summed, c + 1)
                    nc.vector.scalar_tensor_tensor(chunk(core.xT, c), core.bank[:, 4 + c, :], cols[:, 7:8], chunk(core.xT, c), ALU.add, ALU.add)


def quantised_ffn_1(core, t):
    nc = core.nc
    INNER, KCH = 512, 4
    ROUND = 1.5 * 2.0 ** 23
    QMAX, QMIN, TINY = 127.0, -128.0, 1e-5
    layernorm(core, "ln9", core.xT, core.yT)
    with ExitStack() as own:
        sb = lambda n, s, dt=F32: core.sb(n, s, dt, own)
        sem = core.sem
        wq = sb("f_wq", [128, 3, INNER], BF16)
        wmean, winv = sb("f_wmean", [128, 3]), sb("f_winv", [128, 3])
        xqT = sb("f_xqT", [128, TOK], BF16)
        rows_in = sb("f_rows_in", [128, TILES])
        sg, su = sb("f_sg", [128, TILES]), sb("f_su", [128, TILES])
        bias_round, wdown = sb("f_bias_round", [128, 1]), sb("f_wdown", [128, 1])

        with ExitStack() as pre:
            w = core.sb("f_w", [128, 3, INNER], ctx=pre)
            q = core.sb("f_q", [128, TILES, 128], ctx=pre)
            inv = core.sb("f_inv", [128, TILES], ctx=pre)
            w_loaded, wsum, wmean_made, step = sem("f_w_loaded"), sem("f_wsum"), sem("f_wmean_made"), sem("f_step")
            x_turned, y_turned, x_kept, q_made, q_turned = (sem(f"f_{n}") for n in ("x_turned", "y_turned", "x_kept", "q_made", "q_turned"))
            block = pre.enter_context(nc.Block())

            @block.sync
            def _(sp):
                sp.dma_start(w[:].rearrange("p n d -> p (n d)"), t["L1_ffn_w"]).then_inc(w_loaded, 16)
                sp.wait_ge(w_loaded, 16)

            @block.tensor
            def _(pe):
                for v, base, done in ((core.yT, 0, y_turned), (core.xT, 4, x_turned)):
                    for m in range(TILES):
                        ins = nc.tensor.transpose(core.bank[:, base + m // 4, 128 * (m % 4):128 * (m % 4) + 128], v[:, 128 * m:128 * m + 128], core.ident[:])
                    ins.then_inc(done, 1)
                pe.wait_ge(wsum, 1)
                pe.wait_ge(x_kept, 1)
                nc.tensor.matmul(core.bank[:, 4, 0:3], core.mean_w[:], wmean[:], start=True, stop=True).then_inc(wmean_made, 1)
                pe.wait_ge(q_made, 1)
                for m in range(TILES):
                    ins = nc.tensor.transpose(core.bank[:, m // 4, 128 * (m % 4):128 * (m % 4) + 128], q[:, m, :], core.ident[:])
                ins.then_inc(q_turned, 1)

            @block.scalar
            def _(act):
                act.wait_ge(x_turned, 1)
                nc.scalar.activation(core.out[:].rearrange("p m d -> p (m d)"), core.bank[:, 4:8, :].rearrange("p c n -> p (c n)"), ACT.Copy).then_inc(x_kept, 1)

            @block.vector
            def _(dve):
                n = 0

                def then(ins):
                    nonlocal n
                    ins.then_inc(step, 1)
                    n += 1
                    dve.wait_ge(step, n)

                v = nc.vector
                v.memset(bias_round[:], -ROUND)
                dve.wait_ge(w_loaded, 16)
                v.tensor_reduce(wmean[:], w[:], AXX, ALU.add, apply_absolute_value=True).then_inc(wsum, 1)
                turned = core.bank[:, 0:4, :].rearrange("p c (m d) -> p (c m) d", d=128)
                dve.wait_ge(y_turned, 1)
                then(v.tensor_reduce(rows_in[:], turned, AXX, ALU.max, apply_absolute_value=True))
                then(v.tensor_scalar(rows_in[:], rows_in[:], TINY, None, ALU.max))
                then(v.reciprocal(inv[:], rows_in[:]))
                then(v.tensor_scalar(inv[:], inv[:], QMAX, None, ALU.mult))
                then(v.tensor_tensor(q[:], turned, inv[:].unsqueeze(2).broadcast_to([128, TILES, 128]), ALU.mult))
                then(v.tensor_scalar(q[:], q[:], ROUND, -ROUND, ALU.add, ALU.add))
                v.tensor_scalar(q[:], q[:], QMAX, QMIN, ALU.min, ALU.max).then_inc(q_made, 1)
                dve.wait_ge(wmean_made, 1)
                then(v.tensor_scalar(wmean[:], core.bank[:, 4, 0:3], 1.0 / INNER, TINY, ALU.mult, ALU.max))
                then(v.reciprocal(winv[:], wmean[:]))
                for m in range(3):
                    then(v.tensor_scalar(w[:, m, :], w[:, m, :], winv[:, m:m + 1], ROUND, ALU.mult, ALU.add))
                then(v.tensor_scalar(w[:], w[:], -ROUND, 1.0, ALU.add, ALU.min))
                v.tensor_scalar(wq[:], w[:], -1.0, None, ALU.max)
                then(v.tensor_scalar(rows_in[:], rows_in[:], 1.0 / QMAX, None, ALU.mult))
                v.tensor_scalar(wdown[:], wmean[:, 2:3], 1.0 / QMAX, None, ALU.mult)
                v.tensor_scalar(sg[:], rows_in[:], wmean[:, 0:1], None, ALU.mult)
                v.tensor_scalar(su[:], rows_in[:], wmean[:, 1:2], None, ALU.mult)
                dve.wait_ge(q_turned, 1)
                v.tensor_copy(xqT[:].rearrange("p (c n) -> p c n", c=NCH), core.bank[:, 0:4, :])

        gs, h = sb("f_gs", [128, 2, INNER]), sb("f_h", [128, 2, INNER])
        hT = sb("f_hT", [128, 2, KCH, 128], BF16)
        alpha = sb("f_alpha", [128, 2])
        most, mult, sd = sb("f_most", [128, 2]), sb("f_mult", [128, 2]), sb("f_sd", [128, 2])
        G, U = [core.bank[:, n, :] for n in (0, 1)], [core.bank[:, n, :] for n in (2, 3)]
        T, DN = [core.bank[:, n, :] for n in (4, 5)], [core.bank[:, n, 0:128] for n in (6, 7)]
        TURNS = TILES // 2
        alpha_made, g_made, silu_made, rounded, t_made, t_copied, d_made = (
            sem(f"f_{n}") for n in ("alpha_made", "g_made", "silu_made", "rounded", "t_made", "t_copied", "d_made"))
        gu_free, finished, quant = (sem(f"f_{n}") for n in ("gu_free", "finished", "quant"))
        QUANT = 5
        with nc.Block() as block:

            @block.tensor
            def _(pe):
                def turn(i, j):
                    n = i * 2 + j
                    pe.wait_ge(rounded, n + 1)
                    pe.wait_ge(t_copied, n + 1)
                    for k in range(KCH):
                        ins = nc.tensor.transpose(T[j % 2][:, 128 * k:128 * k + 128], h[:, j % 2, 128 * k:128 * k + 128], core.ident[:])
                    ins.then_inc(t_made, 1)

                def down(i, j):
                    n = i * 2 + j
                    pe.wait_ge(t_copied, n + 3)
                    pe.wait_ge(finished, n + 1)
                    for k in range(KCH):
                        ins = nc.tensor.matmul(DN[j % 2], hT[:, j % 2, k, :], wq[:, 2, 128 * k:128 * k + 128], start=(k == 0), stop=(k == KCH - 1))
                    ins.then_inc(d_made, 1)

                def body(i, first, last):
                    for j in range(2):
                        pe.wait_ge(gu_free, i * 2 + (j + 1))
                        src = xqT[:, bass.ds((i * 2 + j) * 128, 128)]
                        nc.tensor.matmul(G[j], src, wq[:, 0, :], start=True, stop=True)
                        nc.tensor.matmul(U[j], src, wq[:, 1, :], start=True, stop=True).then_inc(g_made, 1)
                        if not (first and j == 0):
                            turn(i, j - 1)
                        if not first:
                            down(i, j - 2)

                pe.sem_inc(d_made, 2)
                peeled(pe, TURNS, body)
                turn(TURNS, -1)
                down(TURNS, -2)
                down(TURNS, -1)

            @block.scalar
            def _(act):
                def turned(i, j):
                    n = i * 2 + j
                    act.wait_ge(t_made, n + 1)
                    act.wait_ge(d_made, n + 1)
                    nc.scalar.activation(hT[:, j % 2].rearrange("p k q -> p (k q)"), T[j % 2], ACT.Identity,
                                         bias=bias_round[:, 0:1]).then_inc(t_copied, 1)

                def body(i, first, last):
                    for j in range(2):
                        act.wait_ge(alpha_made, i * 2 + (j + 1))
                        act.wait_ge(g_made, i * 2 + (j + 1))
                        nc.scalar.activation(gs[:, j, :], G[j], ACT.Silu, scale=alpha[:, j:j + 1]).then_inc(silu_made, 1)
                        if not (first and j == 0):
                            turned(i, j - 1)

                act.sem_inc(t_copied, 2)
                peeled(act, TURNS, body)
                turned(TURNS, -1)

            @block.vector
            def _(dve):
                v = nc.vector

                def finish(i, j):
                    n = i * 2 + j
                    dve.wait_ge(d_made, n + 3)
                    row = core.out[:, bass.ds(n, 1), :].rearrange("p a d -> p (a d)")
                    v.scalar_tensor_tensor(row, DN[j % 2], sd[:, j % 2:j % 2 + 1], row, ALU.mult, ALU.add).then_inc(finished, 1)

                def body(i, first, last):
                    for j in range(2):
                        n = i * 2 + j
                        J = slice(j, j + 1)
                        v.tensor_copy(alpha[:, J], sg[:, bass.ds(n, 1)]).then_inc(alpha_made, 1)
                        if not first:
                            finish(i, j - 2)
                        dve.wait_ge(silu_made, n + 1)
                        v.scalar_tensor_tensor(h[:, j, :], U[j], su[:, bass.ds(n, 1)], gs[:, j, :], ALU.mult, ALU.mult).then_inc(gu_free, 1)
                        dve.wait_ge(gu_free, n + 3)
                        v.tensor_reduce(most[:, J], h[:, j, :], AXX, ALU.max, apply_absolute_value=True).then_inc(quant, 1)
                        dve.wait_ge(quant, n * QUANT + 1)
                        v.tensor_scalar(most[:, J], most[:, J], TINY, None, ALU.max).then_inc(quant, 1)
                        dve.wait_ge(quant, n * QUANT + 2)
                        v.reciprocal(mult[:, J], most[:, J]).then_inc(quant, 1)
                        dve.wait_ge(quant, n * QUANT + 3)
                        v.tensor_scalar(mult[:, J], mult[:, J], QMAX, None, ALU.mult).then_inc(quant, 1)
                        dve.wait_ge(finished, n + 1)
                        v.tensor_scalar(sd[:, J], most[:, J], wdown[:, 0:1], None, ALU.mult)
                        dve.wait_ge(quant, n * QUANT + 4)
                        v.tensor_scalar(h[:, j, :], h[:, j, :], mult[:, J], ROUND, ALU.mult, ALU.add).then_inc(quant, 1)
                        dve.wait_ge(quant, n * QUANT + 5)
                        v.tensor_scalar(h[:, j, :], h[:, j, :], ROUND + QMAX, ROUND + QMIN, ALU.min, ALU.max).then_inc(rounded, 1)

                dve.sem_inc(gu_free, 2)
                dve.sem_inc(finished, 2)
                peeled(dve, TURNS, body)
                finish(TURNS, -2)
                finish(TURNS, -1)


def perceiver(nc, t, out):
    with ExitStack() as ctx:
        core = Core(nc, ctx)
        setup(core, t["xT"])
        for stage in STAGES:
            stage(core, t)
        stored = core.sem("stored")
        with nc.Block() as block:

            @block.sync
            def _(sp):
                sp.dma_start(out.rearrange("(m p) d -> p m d", p=128), core.out[:]).then_inc(stored, 16)
                sp.wait_ge(stored, 16)


STAGES = [cross_attention_0, memory_attention_0, experts_0, cross_attention_1, recurrent_1, quantised_ffn_1]


def layouts(inputs):
    import numpy as np

    a = {k: np.asarray(v) for k, v in inputs.items()}
    put = {"xT": a["x"].reshape(TOK, D).T, "ctxT": a["ctx_1024"].reshape(BATCH * CTX, D).T,
           "mask0": a["mask_Bx1x1xS2_fk0"].reshape(1, BATCH * CTX)}
    for n in ("Wq", "Wk", "Wv", "Wo"):
        put[f"L0_xattn_{n}"] = a[f"L0_xattn_{n}"]
    for n in ("bq", "bk", "bv", "bo"):
        put[f"L0_xattn_{n}"] = a[f"L0_xattn_{n}"].reshape(D, 1)
    for n in ("Wq", "Wk", "Wv", "memory"):
        put[f"L0_attn_{n}"] = a[f"L0_attn_{n}"]
    put["L0_attn_memory_norm"] = a["L0_attn_memory_norm"].reshape(64, 1)
    put["L0_attn_memory_weight"] = a["L0_attn_memory_weight"].reshape(1, 1)
    put["L0_ffn_router_w"], put["L0_ffn_b2"] = a["L0_ffn_router_w"], a["L0_ffn_b2"]
    put["L0_ffn_router_b"] = a["L0_ffn_router_b"].reshape(1, 8)
    put["L0_ffn_w"] = np.concatenate([a["L0_ffn_w1"].transpose(1, 0, 2),
                                      a["L0_ffn_w2"].reshape(8, 4, 128, 128).transpose(2, 0, 1, 3).reshape(128, 8, 512),
                                      a["L0_ffn_b1"].reshape(8, 4, 128).transpose(2, 0, 1)], axis=2).reshape(128, -1)
    pairs = lambda w: w.reshape(8, 128, 128).transpose(1, 0, 2).reshape(128, 1024)
    put["L1_xattn_WqT"] = pairs(a["L1_xattn_Wq"].T)
    put["L1_xattn_WkT"] = pairs(a["L1_xattn_Wkv"][:, :1024].T)
    put["L1_xattn_WvT"] = pairs(a["L1_xattn_Wkv"][:, 1024:].T)
    put["L1_xattn_Wout"] = pairs(a["L1_xattn_Wout"])
    put["L1_xattn_affine"] = np.stack([a[f"L1_xattn_{n}"] for n in ("g_media", "b_media", "g_latent", "b_latent", "bout")], axis=1)
    cols = [a[f"L1_attn_{n}"] for n in ("ln1_g", "ln1_b", "ln2_g", "ln2_b", "ln3_g", "ln3_b", "pw_b", "mlp_b2", "dw_b")]
    cols += list(a["L1_attn_dw_w"][:, 0, :].T) + list(a["L1_attn_mlp_b1"].reshape(4, 128))
    put["L1_attn_cols"] = np.stack(cols, axis=1)
    fb = a["L1_attn_f_b"]
    put["L1_attn_f_b"] = np.stack([fb[0:128], np.concatenate([fb[128:192]] * 2), fb[192:320], np.concatenate([fb[320:384]] * 2)], axis=1)
    put["L1_attn_pwT"], put["L1_attn_fT"], put["L1_attn_dpT"] = a["L1_attn_pw_w"].T, a["L1_attn_f_w"].T, a["L1_attn_dp_w"].T
    put["L1_attn_mlp_w1T"] = a["L1_attn_mlp_w1"].T
    put["L1_attn_mlp_w2T"] = a["L1_attn_mlp_w2"].T.reshape(4, 128, 128).transpose(1, 0, 2).reshape(128, 512)
    put["L1_ffn_w"] = np.concatenate([a["L1_ffn_w_gate"].T, a["L1_ffn_w_up"].T,
                                      a["L1_ffn_w_down"].T.reshape(4, 128, 128).transpose(1, 0, 2).reshape(128, 512)], axis=1)
    put["mask1"] = a["mask_BxS2_bk0"]
    return {k: np.ascontiguousarray(v) for k, v in put.items()}


def kernel(**inputs):
    import concourse.bacc as bacc
    import numpy as np
    from concourse.bass_utils import run_bass_kernel_spmd

    nc = bacc.Bacc("TRN2", target_bir_lowering=False, num_devices=1)
    arrays = layouts(inputs)
    t = {k: nc.dram_tensor(f"in_{k}", v.shape, mybir.dt.from_np(v.dtype), kind="ExternalInput").ap() for k, v in arrays.items()}
    out = nc.dram_tensor("out_rows", (TOK, D), F32, kind="ExternalOutput").ap()
    perceiver(nc, t, out)
    r = run_bass_kernel_spmd(nc, [{f"in_{k}": v for k, v in arrays.items()}], core_ids=[0])
    return np.ascontiguousarray(r.results[0]["out_rows"]).reshape(BATCH, LAT, D)
```

```python
import concourse.bass as bass
from concourse import mybir
from contextlib import ExitStack

F32 = mybir.dt.float32
BF16 = mybir.dt.bfloat16
ALU = mybir.AluOpType
ACT = mybir.ActivationFunctionType
AXX = mybir.AxisListType.X

BATCH, LAT, D, CTX = 64, 32, 128, 257
TOK = BATCH * LAT
HEADS = 16
CHUNK = 512
NCH = TOK // CHUNK
TILES = TOK // 128
EPS = 1e-5


def bf16_parts(value, count):
    import numpy as np

    parts = []
    rest = np.float32(value)
    for _ in range(count):
        part = (rest.view(np.uint32) & np.uint32(0xFFFF0000)).view(np.float32)
        parts.append(float(part))
        rest = np.float32(rest - part)
    return parts


class Core:

    def __init__(self, nc, ctx):
        self.nc, self.ctx = nc, ctx
        self.bank = ctx.enter_context(nc.psum_tensor("bank", [128, 8, CHUNK], F32))
        self.xT = self.sb("xT", [128, TOK])
        self.yT = self.sb("yT", [128, TOK])
        self.ident = self.sb("ident", [128, 128])
        self.mean_w = self.sb("mean_w", [128, 128])
        self.out = self.sb("rows_out", [128, TILES, 128])
        self.norm_sems = [self.sem(f"norm_{n}") for n in ("mean", "centred", "squared", "var", "log", "rstd", "scaled")]
        self.norms = 0
        self.eps = self.sb("eps", [128, 1])

    def sb(self, name, shape, dt=F32, ctx=None):
        return (ctx or self.ctx).enter_context(self.nc.sbuf_tensor(name, shape, dt))

    def sem(self, name):
        return self.ctx.enter_context(self.nc.semaphore(name))


def chunk(t, c):
    return t[:, c * CHUNK:(c + 1) * CHUNK]


def peeled(eng, turns, body):
    body(0, True, False)
    with eng.Fori(1, turns - 1) as i:
        body(i, False, False)
    body(turns - 1, False, True)


def setup(core, xT_dram):
    nc = core.nc
    loaded, cleared, built = core.sem("x_loaded"), core.sem("const_cleared"), core.sem("const_built")
    with nc.Block() as block:

        @block.sync
        def _(sp):
            sp.dma_start(core.xT[:], xT_dram).then_inc(loaded, 16)
            sp.wait_ge(loaded, 16)

        @block.gpsimd
        def _(pool):
            nc.gpsimd.memset(core.ident[:], 0.0).then_inc(cleared, 1)
            nc.gpsimd.memset(core.mean_w[:], 1.0 / D).then_inc(built, 1)
            nc.gpsimd.memset(core.eps[:], EPS).then_inc(built, 1)
            pool.wait_ge(cleared, 1)
            nc.gpsimd.affine_select(out=core.ident[:], in_=core.ident[:], compare_op=ALU.not_equal, fill=1.0,
                                    base=0, pattern=[[-1, 128]], channel_multiplier=1).then_inc(built, 1)


def layernorm(core, name, src, dst, gamma=None, beta=None):
    nc = core.nc
    mean, var = core.bank[:, 0:4, :], core.bank[:, 4:8, :]
    with ExitStack() as own:
        sq = core.sb(f"{name}_sq", [128, TOK], ctx=own)
        rstd = core.sb(f"{name}_rstd", [128, TOK], ctx=own)
        mean_ready, centred, squared, var_ready, log_ready, rstd_ready, scaled = core.norm_sems
        before = core.norms * NCH
        core.norms += 1
        block = own.enter_context(nc.Block())

        @block.tensor
        def _(pe):
            for c in range(NCH):
                nc.tensor.matmul(mean[:, c, :], core.mean_w[:], chunk(src, c), start=True, stop=True).then_inc(mean_ready, 1)
            for c in range(NCH):
                pe.wait_ge(squared, before + c + 1)
                nc.tensor.matmul(var[:, c, :], core.mean_w[:], chunk(sq, c), start=True, stop=True).then_inc(var_ready, 1)

        @block.vector
        def _(dve):
            for c in range(NCH):
                dve.wait_ge(mean_ready, before + c + 1)
                nc.vector.tensor_tensor(chunk(dst, c), chunk(src, c), mean[:, c, :], ALU.subtract).then_inc(centred, 1)
            for c in range(NCH):
                dve.wait_ge(rstd_ready, before + c + 1)
                nc.vector.tensor_tensor(chunk(dst, c), chunk(dst, c), chunk(rstd, c), ALU.mult).then_inc(scaled, 1)
                if gamma is not None:
                    dve.wait_ge(scaled, before + c + 1)
                    nc.vector.tensor_scalar(chunk(dst, c), chunk(dst, c), gamma, beta, ALU.mult, ALU.add)

        @block.scalar
        def _(act):
            nc.scalar.preload_act_table_set("natural_log_exp_and_others")
            for c in range(NCH):
                act.wait_ge(centred, before + c + 1)
                nc.scalar.activation(chunk(sq, c), chunk(dst, c), ACT.Square).then_inc(squared, 1)
            for c in range(NCH):
                act.wait_ge(var_ready, before + c + 1)
                nc.scalar.activation(chunk(rstd, c), var[:, c, :], ACT.Ln, bias=core.eps[:, 0:1]).then_inc(log_ready, 1)
                act.wait_ge(log_ready, before + c + 1)
                nc.scalar.activation(chunk(rstd, c), chunk(rstd, c), ACT.Exp, scale=-0.5).then_inc(rstd_ready, 1)


def cross_attention_0(core, t):
    nc = core.nc
    DH = D // HEADS
    QUADS = 4
    UNITS = 2 * QUADS
    PAIRS = BATCH // 2
    layernorm(core, "ln0", core.xT, core.yT)
    with ExitStack() as own:
        sb = lambda n, s, dt=F32: core.sb(n, s, dt, own)
        sem = core.sem
        wq, wk, wv, wo = (sb(f"a_{n}", [128, 128]) for n in ("wq", "wk", "wv", "wo"))
        bias = sb("a_bias", [128, 4])
        qT = sb("a_qT", [128, TOK])
        oT = sb("a_oT", [128, TOK])
        head_of = sb("a_head_of", [128, HEADS])
        own_head = sb("a_own_head", [128, 4])
        group_of = sb("a_group_of", [4, 128])
        big = sb("a_big", [3, 128])
        ones3 = sb("a_ones3", [3, CTX])
        big_bf = sb("a_big_bf", [3, 128], BF16)
        ctT = sb("a_ctT", [128, 2, CTX])
        maskf = sb("a_maskf", [3, 2, CTX])
        maskb = sb("a_maskb", [3, 2, CTX], BF16)
        kT = sb("a_kT", [128, 2, CTX])
        v = sb("a_v", [128, 2, 2, 128])
        vlast = sb("a_vlast", [4, 2, 128])
        qb = sb("a_qb", [128, 2, HEADS, LAT])
        p = sb("a_p", [128, 2, QUADS, CTX])
        pT = sb("a_pT", [128, 2, 2, QUADS, 128])
        plast = sb("a_plast", [4, 2, 128])
        nmax = sb("a_nmax", [128, 2, QUADS])
        psum_ = sb("a_psum", [128, 2, QUADS])
        rsum = sb("a_rsum", [128, 2, QUADS])
        odiag = sb("a_odiag", [128, 4, LAT])
        RING, LAG = 4, 3
        S = [core.bank[:, n, 0:CTX] for n in range(RING)]
        TP = [core.bank[:, n, 0:256] for n in (4, 5)]
        KP, VP = core.bank[:, 6, 0:CTX], core.bank[:, 6, :]
        TL, OP = core.bank[0:4, 7, 0:128], core.bank[:, 7, 0:128]

        w_loaded, q_made, q_copied = sem("a_w_loaded"), sem("a_q_made"), sem("a_q_copied")
        const_step = sem("a_const_step")
        ct_loaded = [sem(f"a_ct_loaded{n}") for n in (0, 1)]
        mask_loaded = [sem(f"a_mask_loaded{n}") for n in (0, 1)]
        mask_cast, qb_made = sem("a_mask_cast"), sem("a_qb_made")
        k_made, k_copied = sem("a_k_made"), sem("a_k_copied")
        v_made, v_copied = sem("a_v_made"), sem("a_v_copied")
        s_made, max_made, exp_made, recip_made, norm_made = (sem(f"a_{n}") for n in ("s_made", "max_made", "exp_made", "recip_made", "norm_made"))
        t_made, t_copied, tl_made, tl_copied = (sem(f"a_{n}") for n in ("t_made", "t_copied", "tl_made", "tl_copied"))
        o_made, o_masked, o_copied = sem("a_o_made"), sem("a_o_masked"), sem("a_o_copied")
        out_made, out_added = sem("a_out_made"), sem("a_out_added")

        with nc.Block() as block:

            @block.sync
            def _(sp):
                for dst, name in ((wq, "L0_xattn_Wq"), (wk, "L0_xattn_Wk"), (wv, "L0_xattn_Wv"), (wo, "L0_xattn_Wo")):
                    sp.dma_start(dst[:], t[name]).then_inc(w_loaded, 16)
                for n, name in enumerate(("L0_xattn_bq", "L0_xattn_bk", "L0_xattn_bv", "L0_xattn_bo")):
                    sp.dma_start(bias[:, n:n + 1], t[name]).then_inc(w_loaded, 16)
                sp.wait_ge(w_loaded, 128)

            @block.gpsimd
            def _(pool):
                nc.gpsimd.memset(head_of[:], 1.0).then_inc(const_step, 1)
                nc.gpsimd.memset(group_of[:], 1.0).then_inc(const_step, 1)
                nc.gpsimd.memset(ones3[:], 1.0)
                parts = bf16_parts(-1e9, 3)
                nc.gpsimd.memset(big[:], parts[0]).then_inc(const_step, 1)
                pool.wait_ge(const_step, 3)
                nc.gpsimd.affine_select(out=head_of[:], in_=head_of[:], compare_op=ALU.is_ge, fill=0.0, base=0,
                                        pattern=[[-DH, HEADS]], channel_multiplier=1).then_inc(const_step, 1)
                pool.wait_ge(const_step, 4)
                nc.gpsimd.affine_select(out=head_of[:], in_=head_of[:], compare_op=ALU.is_ge, fill=0.0, base=DH - 1,
                                        pattern=[[DH, HEADS]], channel_multiplier=-1).then_inc(const_step, 1)
                step = 5
                nc.gpsimd.affine_select(out=group_of[:], in_=group_of[:], compare_op=ALU.is_ge, fill=0.0, base=0,
                                        pattern=[[1, 128]], channel_multiplier=-32).then_inc(const_step, 1)
                step += 1
                pool.wait_ge(const_step, step)
                nc.gpsimd.affine_select(out=group_of[:], in_=group_of[:], compare_op=ALU.is_ge, fill=0.0, base=31,
                                        pattern=[[-1, 128]], channel_multiplier=32).then_inc(const_step, 1)
                step += 1
                for n in (1, 2):
                    nc.gpsimd.affine_select(out=big[:], in_=big[:], compare_op=ALU.is_ge, fill=parts[n], base=n - 1,
                                            pattern=[[0, 128]], channel_multiplier=-1).then_inc(const_step, 1)
                    step += 1
                    pool.wait_ge(const_step, step)
                nc.gpsimd.tensor_copy(big_bf[:], big[:]).then_inc(const_step, 1)

            @block.tensor
            def _(pe):
                pe.wait_ge(w_loaded, 128)
                for c in range(NCH):
                    nc.tensor.matmul(core.bank[:, c, :], wq[:], chunk(core.yT, c), start=True, stop=True).then_inc(q_made, 1)

            @block.vector
            def _(dve):
                dve.wait_ge(w_loaded, 128)
                dve.wait_ge(const_step, 5)
                nc.vector.tensor_reduce(own_head[:], head_of[:].rearrange("p (g h) -> p h g", g=QUADS), AXX, ALU.add)
                for c in range(NCH):
                    dve.wait_ge(q_made, c + 1)
                    nc.vector.tensor_scalar(chunk(qT, c), core.bank[:, c, :], bias[:, 0:1], DH ** -0.5,
                                            ALU.add, ALU.mult).then_inc(q_copied, 1)

        with nc.Block() as block:
            ct_dram, mask_dram = t["ctxT"], t["mask0"]

            @block.sync
            def _(sp):
                def load(i, j, after):
                    if after is not None:
                        sp.wait_ge(v_made, after)
                        sp.wait_ge(mask_cast, after)
                    sp.dma_start(ctT[:, j, :], ct_dram[:, bass.ds((i * 2 + j) * CTX, CTX)]).then_inc(ct_loaded[j], 16)
                    sp.dma_start(maskf[:, j, :], mask_dram[:, bass.ds((i * 2 + j) * CTX, CTX)].broadcast_to([3, CTX])).then_inc(mask_loaded[j], 16)

                load(0, 0, None)
                load(0, 1, None)
                with sp.Fori(1, PAIRS) as i:
                    for j in range(2):
                        load(i, j, i * 2 + (j - 1))

            @block.gpsimd
            def _(pool):
                def prepare(i, j, first):
                    if not first:
                        pool.wait_ge(s_made, i * UNITS + QUADS * (j - 1))
                    pool.wait_ge(mask_loaded[j], i * 16 + 16)
                    nc.gpsimd.tensor_tensor(maskb[:, j, :], maskf[:, j, :], ones3[:], ALU.mult).then_inc(mask_cast, 1)
                    rows = qT[:, bass.ds((i * 2 + j) * LAT, LAT)].unsqueeze(1).broadcast_to([128, HEADS, LAT])
                    heads = head_of[:].unsqueeze(2).broadcast_to([128, HEADS, LAT])
                    nc.gpsimd.tensor_tensor(qb[:, j], rows, heads, ALU.mult).then_inc(qb_made, 1)

                prepare(0, 0, True)
                prepare(0, 1, True)
                with pool.Fori(1, PAIRS) as i:
                    for j in range(2):
                        prepare(i, j, False)

            @block.tensor
            def _(pe):
                def keys(i, j, first=False):
                    pe.wait_ge(ct_loaded[j % 2], (i + j // 2) * 16 + 16)
                    if not first:
                        pe.wait_ge(v_copied, i * 2 + j)
                    nc.tensor.matmul(KP, wk[:], ctT[:, j % 2, :], start=True, stop=True).then_inc(k_made, 1)

                def values(i, j):
                    pe.wait_ge(k_copied, i * 2 + j + 1)
                    for k in range(2):
                        nc.tensor.matmul(VP[:, 128 * k:128 * k + 128], ctT[:, j, 128 * k:128 * k + 128], wv[:],
                                         start=True, stop=True)
                    nc.tensor.matmul(VP[0:4, 256:384], ctT[:, j, 256:257].broadcast_to([128, 4]), wv[:],
                                     start=True, stop=True).then_inc(v_made, 1)

                def scores(i, s, first):
                    j, g = divmod(s, QUADS)
                    if g == 0:
                        pe.wait_ge(k_copied, i * 2 + j + 1)
                        pe.wait_ge(qb_made, i * 2 + j + 1)
                    if not (first and s < RING):
                        pe.wait_ge(exp_made, i * UNITS + (s - RING + 1))
                    nc.tensor.matmul(S[s % RING], qb[:, j, 4 * g:4 * g + 4, :].rearrange("p h q -> p (h q)"), kT[:, j, :], start=True, stop=False)
                    nc.tensor.matmul(S[s % RING], big_bf[:], maskb[:, j, :], start=False, stop=True).then_inc(s_made, 1)

                def transposes(i, s, tfirst):
                    j, g = divmod(s % UNITS, QUADS)
                    pe.wait_ge(norm_made, i * UNITS + (s + 1))
                    if not tfirst:
                        pe.wait_ge(t_copied, i * UNITS + (s - 1))
                    for k in range(2):
                        ins = nc.tensor.transpose(TP[s % 2][:, 128 * k:128 * k + 128], p[:, j, g, 128 * k:128 * k + 128], core.ident[:])
                    ins.then_inc(t_made, 1)

                def last_key(i, j, first=False):
                    if not first:
                        pe.wait_ge(o_masked, i * 2 + j)
                    nc.tensor.transpose(TL, p[:, j % 2, :, CTX - 1], core.ident[:]).then_inc(tl_made, 1)

                def output(i, j):
                    n, jj = i * 2 + j, j % 2
                    pe.wait_ge(tl_copied, n + 1)
                    pe.wait_ge(t_copied, (n + 1) * QUADS)
                    pe.wait_ge(v_copied, n + 1)
                    nc.tensor.matmul(OP, vlast[:, jj, :], plast[:, jj, :], start=True, stop=False, skip_group_check=True)
                    for k in range(2):
                        for g in range(QUADS):
                            rows = slice(32 * g, 32 * g + 32)
                            ins = nc.tensor.matmul(OP[rows, :], v[:, jj, k, rows], pT[:, jj, k, g, :], start=False,
                                                   stop=(k == 1), skip_group_check=True)
                    ins.then_inc(o_made, 1)

                pe.wait_ge(w_loaded, 128)
                keys(0, 0, True)

                def body(i, first, last):
                    for s in range(UNITS):
                        scores(i, s, first)
                        if not (first and s < LAG):
                            transposes(i, s - LAG, first and s < LAG + 2)
                        j, g = divmod(s, QUADS)
                        if g == 0:
                            values(i, j)
                        if g == 2 and not (first and j == 0):
                            last_key(i, j - 1, first and j == 1)
                        if g == 3:
                            if not (last and j == 1):
                                keys(i, j + 1)
                            if not (first and j == 0):
                                output(i, j - 1)

                peeled(pe, PAIRS, body)
                for s in range(-LAG, 0):
                    transposes(PAIRS, s, False)
                last_key(PAIRS, -1)
                output(PAIRS, -1)

            @block.scalar
            def _(act):
                def keys(i, j, first=False):
                    act.wait_ge(k_made, i * 2 + j + 1)
                    if not first:
                        act.wait_ge(s_made, (i * 2 + j - 1) * QUADS)
                    nc.scalar.activation(kT[:, j % 2, :], KP, ACT.Identity, bias=bias[:, 1:2]).then_inc(k_copied, 1)

                def transposed(i, s, first=False):
                    j, g = divmod(s % UNITS, QUADS)
                    act.wait_ge(t_made, i * UNITS + (s + 1))
                    if g == 0 and not first:
                        act.wait_ge(o_made, i * 2 + (s // QUADS - 1))
                    nc.scalar.activation(pT[:, j, :, g, :], TP[s % 2].rearrange("p (k q) -> p k q", k=2), ACT.Copy).then_inc(t_copied, 1)

                def body(i, first, last):
                    for s in range(UNITS):
                        j, g = divmod(s, QUADS)
                        if not (first and s < LAG):
                            transposed(i, s - LAG, first)
                        if g == 3 and not (last and j == 1):
                            keys(i, j + 1, first and j == 0)
                        act.wait_ge(max_made, i * UNITS + (s + 1))
                        if g == 0 and not first:
                            act.wait_ge(tl_made, i * 2 + j - 1)
                        nc.scalar.activation(p[:, j, g, :], S[s % RING], ACT.Exp, bias=nmax[:, j, g:g + 1],
                                             accum_out=psum_[:, j, g:g + 1]).then_inc(exp_made, 1)

                keys(0, 0, True)
                peeled(act, PAIRS, body)
                for s in range(-LAG, 0):
                    transposed(PAIRS, s)

            @block.vector
            def _(dve):
                def values(i, j, first=False):
                    dve.wait_ge(v_made, i * 2 + j + 1)
                    if not first:
                        dve.wait_ge(o_made, i * 2 + j - 1)
                    nc.vector.tensor_copy(v[:, j % 2].rearrange("p k d -> p (k d)"), VP[:, 0:256])
                    nc.vector.tensor_tensor(vlast[:, j % 2, :], VP[0:4, 256:384], group_of[:], ALU.mult).then_inc(v_copied, 1)

                def normalise(i, s):
                    j, g = divmod(s % UNITS, QUADS)
                    dve.wait_ge(exp_made, i * UNITS + (s + 1))
                    nc.vector.reciprocal(rsum[:, j, g:g + 1], psum_[:, j, g:g + 1]).then_inc(recip_made, 1)
                    dve.wait_ge(recip_made, i * UNITS + (s + 1))
                    nc.vector.tensor_scalar(p[:, j, g, :], p[:, j, g, :], rsum[:, j, g:g + 1], None, ALU.mult).then_inc(norm_made, 1)

                def last_key(i, j):
                    n, jj = i * 2 + j, j % 2
                    dve.wait_ge(tl_made, n + 1)
                    nc.vector.tensor_copy(plast[:, jj, :], TL).then_inc(tl_copied, 1)

                def output(i, j, first=False):
                    n = i * 2 + j
                    dve.wait_ge(o_made, n + 1)
                    if not first:
                        dve.wait_ge(o_copied, n)
                    heads = own_head[:].unsqueeze(2).broadcast_to([128, 4, LAT])
                    nc.vector.tensor_tensor(odiag[:], OP.rearrange("p (h q) -> p h q", h=4), heads, ALU.mult).then_inc(o_masked, 1)
                    dve.wait_ge(o_masked, n + 1)
                    nc.vector.tensor_reduce(oT[:, bass.ds(n * LAT, LAT)], odiag[:].rearrange("p h q -> p q h"), AXX, ALU.add).then_inc(o_copied, 1)

                def body(i, first, last):
                    for s in range(UNITS):
                        j, g = divmod(s, QUADS)
                        if not (first and s < 2):
                            normalise(i, s - 2)
                        dve.wait_ge(s_made, i * UNITS + (s + 1))
                        nc.vector.tensor_reduce(nmax[:, j, g:g + 1], S[s % RING], AXX, ALU.max, negate=True).then_inc(max_made, 1)
                        if g == 1:
                            values(i, j, first)
                        if g == 2 and not (first and j == 0):
                            last_key(i, j - 1)
                        if g == 3 and not (first and j == 0):
                            output(i, j - 1, first)

                dve.wait_ge(w_loaded, 128)
                peeled(dve, PAIRS, body)
                normalise(PAIRS, -2)
                normalise(PAIRS, -1)
                last_key(PAIRS, -1)
                output(PAIRS, -1)

        with nc.Block() as block:
            vb = sb("a_vb", [128, TOK])

            @block.vector
            def _(dve):
                for c in range(NCH):
                    nc.vector.tensor_scalar(chunk(vb, c), chunk(oT, c), bias[:, 2:3], None, ALU.add).then_inc(q_copied, 1)
                for c in range(NCH):
                    dve.wait_ge(out_made, c + 1)
                    nc.vector.scalar_tensor_tensor(chunk(core.xT, c), core.bank[:, c, :], bias[:, 3:4], chunk(core.xT, c),
                                                   ALU.add, ALU.add).then_inc(out_added, 1)

            @block.tensor
            def _(pe):
                for c in range(NCH):
                    pe.wait_ge(q_copied, NCH + c + 1)
                    nc.tensor.matmul(core.bank[:, c, :], wo[:], chunk(vb, c), start=True, stop=True).then_inc(out_made, 1)


def memory_attention_0(core, t):
    nc = core.nc
    DH, KV = 8, 64
    GROUPS = BATCH // 4
    layernorm(core, "ln1", core.xT, core.yT)
    with ExitStack() as own:
        sb = lambda n, s, dt=F32: core.sb(n, s, dt, own)
        sem = core.sem
        wq, wk, wv = (sb(f"b_{n}", [128, 128]) for n in ("wq", "wk", "wv"))
        mem, norm = sb("b_mem", [128, 128]), sb("b_norm", [128, 128])
        norm_col, ones = sb("b_norm_col", [128, 1]), sb("b_ones", [128, KV])
        gate = sb("b_gate", [128, 4])
        qT, kT, aT = sb("b_qT", [128, TOK]), sb("b_kT", [128, TOK]), sb("b_aT", [128, TOK])
        own_head = sb("b_own_head", [128, 4])
        same_group = sb("b_same_group", [128, 128])
        w_loaded, zeroed, gate_step, mask_step = sem("b_w_loaded"), sem("b_zeroed"), sem("b_gate_step"), sem("b_mask_step")
        q_made, q_copied = sem("b_q_made"), sem("b_q_copied")

        with nc.Block() as block:

            @block.sync
            def _(sp):
                sp.wait_ge(zeroed, 1)
                sp.dma_start(wq[:], t["L0_attn_Wq"]).then_inc(w_loaded, 16)
                for dst, name in ((wk, "L0_attn_Wk"), (wv, "L0_attn_Wv")):
                    for r in range(2):
                        sp.dma_start(dst[:].rearrange("p (n r d) -> p n r d", r=2, d=DH)[:, :, r, :],
                                     t[name].rearrange("p (n d) -> p n d", d=DH)).then_inc(w_loaded, 16)
                for r in range(2):
                    rows = slice(KV * r, KV * r + KV)
                    sp.dma_start(mem[rows, rows], t["L0_attn_memory"]).then_inc(w_loaded, 16)
                    sp.dma_start(norm_col[rows, :], t["L0_attn_memory_norm"]).then_inc(w_loaded, 16)
                sp.dma_start(gate[:, 0:1], t["L0_attn_memory_weight"].broadcast_to([128, 1])).then_inc(w_loaded, 16)
                sp.wait_ge(w_loaded, 160)

            @block.gpsimd
            def _(pool):
                step = 0

                def select(m, base, pattern, by):
                    nonlocal step
                    pool.wait_ge(mask_step, step)
                    nc.gpsimd.affine_select(out=m, in_=m, compare_op=ALU.is_ge, fill=0.0, base=base, pattern=pattern,
                                            channel_multiplier=by).then_inc(mask_step, 1)
                    step += 1

                nc.gpsimd.memset(own_head[:], 1.0).then_inc(mask_step, 1)
                nc.gpsimd.memset(same_group[:], 1.0).then_inc(mask_step, 1)
                step = 2
                for g in range(4):
                    rows = own_head[32 * g:32 * g + 32, :]
                    select(rows, 0, [[-DH, 4]], 1)
                    select(rows, DH - 1, [[DH, 4]], -1)
                blocks = same_group[:].rearrange("p (g c) -> p g c", g=4)
                select(blocks, 0, [[-32, 4], [0, 32]], 1)
                select(blocks, 31, [[32, 4], [0, 32]], -1)

            @block.tensor
            def _(pe):
                pe.wait_ge(w_loaded, 160)
                for n, w in enumerate((wq, wk)):
                    for c in range(NCH):
                        nc.tensor.matmul(core.bank[:, n * NCH + c, :], w[:], chunk(core.yT, c), start=True, stop=True).then_inc(q_made, 1)

            @block.vector
            def _(dve):
                nc.vector.memset(mem[:], 0.0).then_inc(zeroed, 1)
                nc.vector.memset(norm[:], 0.0).then_inc(gate_step, 1)
                nc.vector.memset(ones[:], 1.0).then_inc(gate_step, 1)
                dve.wait_ge(w_loaded, 160)
                dve.wait_ge(gate_step, 2)
                for r in range(2):
                    rows = slice(KV * r, KV * r + KV)
                    nc.vector.tensor_scalar(norm[rows, rows], ones[rows, :], norm_col[rows, :], None, ALU.mult)
                for n, dst in enumerate((qT, kT)):
                    for c in range(NCH):
                        dve.wait_ge(q_made, n * NCH + c + 1)
                        nc.vector.tensor_copy(chunk(dst, c), core.bank[:, n * NCH + c, :]).then_inc(q_copied, 1)
                dve.wait_ge(gate_step, 3)
                nc.vector.tensor_scalar(gate[:, 2:3], gate[:, 1:2], 1.0, None, ALU.add).then_inc(gate_step, 1)
                dve.wait_ge(gate_step, 4)
                nc.vector.reciprocal(gate[:, 2:3], gate[:, 2:3]).then_inc(gate_step, 1)
                dve.wait_ge(gate_step, 5)
                nc.vector.tensor_scalar(gate[:, 3:4], gate[:, 2:3], -1.0, 1.0, ALU.mult, ALU.add)

            @block.scalar
            def _(act):
                act.wait_ge(w_loaded, 160)
                act.wait_ge(gate_step, 2)
                nc.scalar.activation(gate[:, 1:2], gate[:, 0:1], ACT.Exp, scale=-1.0).then_inc(gate_step, 1)

        with ExitStack() as loop:
            sb = lambda n, s, dt=F32: core.sb(n, s, dt, loop)
            qb = sb("b_qb", [128, 2, 4, 4, LAT])
            kg = sb("b_kg", [128, 2, 128])
            yg = sb("b_yg", [128, 2, 4, 4, LAT])
            vb = sb("b_vb", [128, 2, 4, 128])
            p = sb("b_p", [128, 2, 4, 4, LAT])
            pT = sb("b_pT", [128, 2, 4, 128])
            top, total, rtotal = sb("b_top", [128, 16]), sb("b_total", [128, 16]), sb("b_rtotal", [128, 16])
            odiag = sb("b_odiag", [128, 4, 4, LAT])
            S = core.bank[:, 0:4, 0:128].rearrange("p c (b k) -> p c b k", b=4)
            VP, TP, OP = (core.bank[:, n, :].rearrange("p (b k) -> p b k", b=4) for n in (4, 5, 6))
            qb_made, kg_made, v_made, v_copied, s_made = (sem(f"b_{n}") for n in ("qb_made", "kg_made", "v_made", "v_copied", "s_made"))
            top_made, shifted, exp_made, summed, recip, normed = (sem(f"b_{n}") for n in ("top_made", "shifted", "exp_made", "summed", "recip", "normed"))
            t_made, t_copied, o_made, o_masked, o_copied = (sem(f"b_{n}") for n in ("t_made", "t_copied", "o_made", "o_masked", "o_copied"))
            block = loop.enter_context(nc.Block())

            @block.gpsimd
            def _(pool):
                def body(i, first, last):
                    for j in range(2):
                        if not first:
                            pool.wait_ge(s_made, i * 2 + (j - 1))
                        toks = bass.ds((i * 2 + j) * 128, 128)
                        rows = qT[:, toks].rearrange("p (b q) -> p b q", b=4)
                        for b in range(4):
                            nc.gpsimd.tensor_tensor(qb[:, j, b], rows[:, b, :].unsqueeze(1).broadcast_to([128, 4, LAT]),
                                                    own_head[:].unsqueeze(2).broadcast_to([128, 4, LAT]), ALU.mult)
                        feats = core.yT[:, toks].rearrange("p (b q) -> p b q", b=4)
                        for g in range(4):
                            ins = nc.gpsimd.tensor_copy(yg[:, j, :, g, :], feats)
                        ins.then_inc(qb_made, 1)

                peeled(pool, GROUPS // 2, body)

            @block.tensor
            def _(pe):
                def scores(i, j, first):
                    n = i * 2 + j
                    pe.wait_ge(qb_made, n + 1)
                    if not first:
                        pe.wait_ge(v_copied, n)
                    for b in range(4):
                        nc.tensor.matmul(VP[:, b, :], yg[:, j, b].rearrange("p r q -> p (r q)"),
                                         wv[:], start=True, stop=True)
                    pe.wait_ge(kg_made, n + 1)
                    if not first:
                        pe.wait_ge(shifted, n)
                    for g in range(4):
                        rows = slice(32 * g, 32 * g + 32)
                        for b in range(4):
                            ins = nc.tensor.matmul(S[:, g, b, :], qb[rows, j, b].rearrange("p h q -> p (h q)"),
                                                   kg[rows, j, 32 * b:32 * b + 32], start=True, stop=True)
                    ins.then_inc(s_made, 1)

                def output(i, j, first):
                    n, jj = i * 2 + j, j % 2
                    pe.wait_ge(normed, n + 1)
                    if not first:
                        pe.wait_ge(t_copied, n)
                    for b in range(4):
                        ins = nc.tensor.transpose(TP[:, b, :], p[:, jj, b].rearrange("p c k -> p (c k)"), core.ident[:])
                    ins.then_inc(t_made, 1)
                    pe.wait_ge(t_copied, n + 1)
                    if not first:
                        pe.wait_ge(o_masked, n)
                    for b in range(4):
                        ins = nc.tensor.matmul(OP[:, b, :], vb[:, jj, b, :], pT[:, jj, b, :], start=True, stop=True)
                    ins.then_inc(o_made, 1)

                def body(i, first, last):
                    for j in range(2):
                        scores(i, j, first and j == 0)
                        if not (first and j == 0):
                            output(i, j - 1, first)

                peeled(pe, GROUPS // 2, body)
                output(GROUPS // 2, -1, False)

            @block.scalar
            def _(act):
                def transposed(i, j):
                    act.wait_ge(t_made, i * 2 + j + 1)
                    nc.scalar.activation(pT[:, j % 2], TP, ACT.Copy).then_inc(t_copied, 1)

                def body(i, first, last):
                    for j in range(2):
                        n = i * 2 + j
                        if not first:
                            act.wait_ge(s_made, n - 1)
                        nc.scalar.activation(kg[:, j, :], kT[:, bass.ds(n * 128, 128)], ACT.Copy, scale=DH ** -0.5).then_inc(kg_made, 1)
                        if not (first and j == 0):
                            transposed(i, j - 1)
                        act.wait_ge(shifted, n + 1)
                        nc.scalar.activation(p[:, j], p[:, j], ACT.Exp).then_inc(exp_made, 1)

                peeled(act, GROUPS // 2, body)
                transposed(GROUPS // 2, -1)

            @block.vector
            def _(dve):
                def output(i, j, first):
                    n = i * 2 + j
                    dve.wait_ge(o_made, n + 1)
                    if not first:
                        dve.wait_ge(o_copied, n)
                    for b in range(4):
                        ins = nc.vector.tensor_tensor(odiag[:, b], OP[:, b, :].rearrange("p (h q) -> p h q", h=4),
                                                      own_head[:].unsqueeze(2).broadcast_to([128, 4, LAT]), ALU.mult)
                    ins.then_inc(o_masked, 1)
                    dve.wait_ge(o_masked, n + 1)
                    nc.vector.tensor_reduce(aT[:, bass.ds(n * 128, 128)].rearrange("p (b q) -> p b q", b=4),
                                            odiag[:].rearrange("p b h q -> p b q h"), AXX, ALU.add).then_inc(o_copied, 1)

                def body(i, first, last):
                    for j in range(2):
                        n = i * 2 + j
                        dve.wait_ge(s_made, n + 1)
                        nc.vector.tensor_tensor(vb[:, j], VP, same_group[:].unsqueeze(1).broadcast_to([128, 4, 128]),
                                                ALU.mult).then_inc(v_copied, 1)
                        if not (first and j == 0):
                            dve.wait_ge(shifted, n)
                        nc.vector.tensor_reduce(top[:].rearrange("p (c b) -> p c b", c=4), S, AXX, ALU.max).then_inc(top_made, 1)
                        dve.wait_ge(top_made, n + 1)
                        for g in range(4):
                            ins = nc.vector.tensor_tensor(p[:, j, :, g, :], S[:, g], top[:, 4 * g:4 * g + 4].unsqueeze(2).broadcast_to([128, 4, LAT]),
                                                          ALU.subtract)
                        ins.then_inc(shifted, 1)
                        if not (first and j == 0):
                            output(i, j - 1, first)
                        dve.wait_ge(exp_made, n + 1)
                        if not (first and j == 0):
                            dve.wait_ge(normed, n)
                        nc.vector.tensor_reduce(total[:].rearrange("p (b c) -> p b c", c=4), p[:, j], AXX, ALU.add).then_inc(summed, 1)
                        dve.wait_ge(summed, n + 1)
                        nc.vector.reciprocal(rtotal[:], total[:]).then_inc(recip, 1)
                        dve.wait_ge(recip, n + 1)
                        nc.vector.tensor_tensor(p[:, j].rearrange("p b c k -> p (b c) k"), p[:, j].rearrange("p b c k -> p (b c) k"),
                                                rtotal[:].unsqueeze(2).broadcast_to([128, 16, LAT]), ALU.mult).then_inc(normed, 1)

                peeled(dve, GROUPS // 2, body)
                output(GROUPS // 2, -1, False)

        with ExitStack() as last:
            low, high = core.sb("b_low", [128, TOK], ctx=last), core.sb("b_high", [128, TOK], ctx=last)
            clipped, expd, elu_made = sem("b_clipped"), sem("b_expd"), sem("b_elu_made")
            num_made, den_made, chain = sem("b_num_made"), sem("b_den_made"), sem("b_chain")
            block = last.enter_context(nc.Block())

            @block.vector
            def _(dve):
                for c in range(NCH):
                    nc.vector.tensor_scalar(chunk(low, c), chunk(qT, c), 0.0, None, ALU.min).then_inc(clipped, 1)
                    nc.vector.tensor_scalar(chunk(high, c), chunk(qT, c), 0.0, None, ALU.max).then_inc(chain, 1)
                for c in range(NCH):
                    dve.wait_ge(expd, c + 1)
                    dve.wait_ge(chain, NCH)
                    nc.vector.scalar_tensor_tensor(chunk(high, c), chunk(low, c), -1.0, chunk(high, c), ALU.add, ALU.add).then_inc(elu_made, 1)
                done = NCH
                for c in range(NCH):
                    dve.wait_ge(den_made, c + 1)
                    nc.vector.reciprocal(chunk(low, c), core.bank[:, 4 + c, :]).then_inc(chain, 1)
                    done += 1
                    dve.wait_ge(chain, done)
                    dve.wait_ge(elu_made, NCH)
                    dve.wait_ge(num_made, NCH)
                    nc.vector.tensor_tensor(chunk(qT, c), core.bank[:, c, :], chunk(low, c), ALU.mult).then_inc(chain, 1)
                    done += 1
                    dve.wait_ge(chain, done)
                    nc.vector.scalar_tensor_tensor(chunk(core.xT, c), chunk(qT, c), gate[:, 2:3], chunk(core.xT, c), ALU.mult, ALU.add).then_inc(chain, 1)
                    done += 1
                    dve.wait_ge(chain, done)
                    nc.vector.scalar_tensor_tensor(chunk(core.xT, c), chunk(aT, c), gate[:, 3:4], chunk(core.xT, c), ALU.mult, ALU.add)

            @block.scalar
            def _(act):
                for c in range(NCH):
                    act.wait_ge(clipped, c + 1)
                    nc.scalar.activation(chunk(low, c), chunk(low, c), ACT.Exp).then_inc(expd, 1)

            @block.tensor
            def _(pe):
                for c in range(NCH):
                    pe.wait_ge(elu_made, c + 1)
                    nc.tensor.matmul(core.bank[:, c, :], mem[:], chunk(high, c), start=True, stop=True).then_inc(num_made, 1)
                    nc.tensor.matmul(core.bank[:, 4 + c, :], norm[:], chunk(high, c), start=True, stop=True).then_inc(den_made, 1)


class Context:

    def __init__(self, core, own):
        sb = lambda n, s, dt=F32: core.sb(n, s, dt, own)
        self.keyT = sb("x_keyT", [128, BATCH, CTX + LAT])
        self.affine = sb("x_affine", [128, 5])
        self.wqT, self.wkT, self.wvT, self.wout = (sb(f"x_{n}", [128, 8, 128]) for n in ("wqT", "wkT", "wvT", "wout"))
        self.mask8, self.mask16 = sb("x_mask8", [BATCH, CTX], mybir.dt.uint8), sb("x_mask16", [BATCH, CTX], BF16)
        self.mask_dram = core.nc.dram_tensor("mask1_bf16", (BATCH, CTX), BF16, kind="Internal").ap()
        self.affine_loaded, self.w_loaded = core.sem("x_affine_loaded"), core.sem("x_w_loaded")
        self.mask_loaded, self.mask_cast, self.mask_stored = (core.sem(f"x_mask_{n}") for n in ("loaded", "cast", "stored"))


def experts_0(core, t, cx):
    nc = core.nc
    E, HID, KCH = 8, 512, 4
    layernorm(core, "ln2", core.xT, core.yT)
    with ExitStack() as own:
        sb = lambda n, s, dt=F32: core.sb(n, s, dt, own)
        sem = core.sem
        router, router_b = sb("c_router", [128, E]), sb("c_router_b", [128, E])
        b2 = sb("c_b2", [E, 128])
        acc = sb("c_acc", [128, TILES, 128])
        gates = sb("c_gates", [128, E, TILES])
        gT = sb("c_gT", [E, TILES, 128])
        w_loaded, logit_made, gate_step = sem("c_w_loaded"), sem("c_logit_made"), sem("c_gate_step")
        shifted, gates_made = sem("c_shifted"), sem("c_gates_made")
        rank_made, exp_made, gt_made, gt_copied, bias_made = sem("c_rank_made"), sem("c_exp_made"), sem("c_gt_made"), sem("c_gt_copied"), sem("c_bias_made")

        with ExitStack() as route:
            rb = lambda n: core.sb(n, [128, TILES, E], ctx=route)
            logit, left, rank, hit, keep, tmp = (rb(f"c_{n}") for n in ("logit", "left", "rank", "hit", "keep", "tmp"))
            best, top, pick = (core.sb(f"c_{n}", [128, TILES], ctx=route) for n in ("best", "top", "pick"))
            wide = lambda v: v[:].unsqueeze(2).broadcast_to([128, TILES, E])
            LG = core.bank[:, 0, 0:TILES * E].rearrange("p (t e) -> p t e", e=E)
            block = route.enter_context(nc.Block())

            @block.sync
            def _(sp):
                sp.dma_start(router[:], t["L0_ffn_router_w"]).then_inc(w_loaded, 16)
                sp.dma_start(router_b[:], t["L0_ffn_router_b"].broadcast_to([128, E])).then_inc(w_loaded, 16)
                sp.dma_start(b2[:], t["L0_ffn_b2"]).then_inc(w_loaded, 16)
                sp.dma_start(cx.affine[:], t["L1_xattn_affine"]).then_inc(cx.affine_loaded, 16)
                sp.dma_start(cx.mask8[:], t["mask1"]).then_inc(cx.mask_loaded, 16)
                sp.wait_ge(w_loaded, 48)

            @block.gpsimd
            def _(pool):
                for e in range(E):
                    nc.gpsimd.memset(rank[:, :, e], float(E - e)).then_inc(rank_made, 1)

            @block.tensor
            def _(pe):
                pe.wait_ge(w_loaded, 48)
                for m in range(TILES):
                    ins = nc.tensor.matmul(LG[:, m, :], core.yT[:, 128 * m:128 * m + 128], router[:], start=True, stop=True)
                ins.then_inc(logit_made, 1)
                pe.wait_ge(gates_made, 1)
                for m in range(TILES):
                    ins = nc.tensor.transpose(core.bank[0:E, 1 + m // 4, 128 * (m % 4):128 * (m % 4) + 128], tmp[:, m, :], core.ident[:])
                ins.then_inc(gt_made, 1)
                pe.wait_ge(gt_copied, 1)
                for m in range(TILES):
                    ins = nc.tensor.matmul(core.bank[:, (5 + m // 4) % 8, 128 * (m % 4):128 * (m % 4) + 128], gT[:, m, :], b2[:], start=True, stop=True)
                    if m % 4 == 3:
                        ins.then_inc(bias_made, 1)

            @block.scalar
            def _(act):
                act.wait_ge(shifted, 1)
                nc.scalar.activation(tmp[:], tmp[:], ACT.Exp).then_inc(exp_made, 1)

            @block.vector
            def _(dve):
                step = 0

                def then(ins):
                    nonlocal step
                    ins.then_inc(gate_step, 1)
                    step += 1
                    dve.wait_ge(gate_step, step)

                v = nc.vector
                dve.wait_ge(logit_made, 1)
                dve.wait_ge(w_loaded, 48)
                dve.wait_ge(rank_made, E)
                then(v.tensor_tensor(logit[:], LG, router_b[:].unsqueeze(1).broadcast_to([128, TILES, E]), ALU.add))
                then(v.tensor_reduce(best[:], logit[:], AXX, ALU.max))
                then(v.tensor_tensor(hit[:], logit[:], wide(best), ALU.is_equal))
                then(v.tensor_tensor(hit[:], hit[:], rank[:], ALU.mult))
                then(v.tensor_reduce(pick[:], hit[:], AXX, ALU.max))
                then(v.tensor_tensor(keep[:], hit[:], wide(pick), ALU.is_equal))
                then(v.scalar_tensor_tensor(left[:], keep[:], -3e38, logit[:], ALU.mult, ALU.add))
                then(v.tensor_reduce(top[:], left[:], AXX, ALU.max))
                then(v.tensor_tensor(hit[:], left[:], wide(top), ALU.is_equal))
                then(v.tensor_tensor(hit[:], hit[:], rank[:], ALU.mult))
                then(v.tensor_reduce(pick[:], hit[:], AXX, ALU.max))
                then(v.tensor_tensor(hit[:], hit[:], wide(pick), ALU.is_equal))
                then(v.tensor_tensor(keep[:], keep[:], hit[:], ALU.add))
                v.tensor_tensor(tmp[:], logit[:], wide(best), ALU.subtract).then_inc(shifted, 1)
                dve.wait_ge(exp_made, 1)
                then(v.tensor_tensor(tmp[:], tmp[:], keep[:], ALU.mult))
                then(v.tensor_reduce(top[:], tmp[:], AXX, ALU.add))
                then(v.reciprocal(best[:], top[:]))
                then(v.tensor_tensor(tmp[:], tmp[:], wide(best), ALU.mult))
                v.tensor_copy(gates[:].rearrange("p e t -> p t e"), tmp[:]).then_inc(gates_made, 1)
                dve.wait_ge(gt_made, 1)
                v.tensor_copy(gT[:].rearrange("e (c m) k -> e c (m k)", c=NCH), core.bank[0:E, 1:5, :]).then_inc(gt_copied, 1)
                dve.wait_ge(cx.mask_loaded, 16)
                v.tensor_copy(cx.mask16[:], cx.mask8[:]).then_inc(cx.mask_cast, 1)
                for c in range(NCH):
                    dve.wait_ge(bias_made, c + 1)
                    v.tensor_copy(acc[:, 4 * c:4 * c + 4, :].rearrange("p m d -> p (m d)"), core.bank[:, (5 + c) % 8, :])

        WIDTH = 2 * HID + KCH
        w = sb("c_w", [128, 2, WIDTH])
        hs = sb("c_hs", [128, 2, KCH, CHUNK])
        RING, EDGE = 4, 4
        ct = sb("c_ct", [128, RING + 1, 4, 128])
        stats, moments, rstd = sb("c_stats", [128, RING + 1, 4, 6]), sb("c_moments", [128, RING + 1, 4, 2]), sb("c_rstd", [128, RING + 1, 4])
        UP = [core.bank[:, k, :] for k in range(KCH)]
        Y = [core.bank[:, 4 + n, :].rearrange("p (m d) -> p m d", m=4) for n in (0, 1)]
        TC = [core.bank[:, n, :] for n in (6, 7)]
        we_loaded = [sem(f"c_we_loaded{n}") for n in (0, 1)]
        up_made, relu_made, down_made, added = sem("c_up_made"), sem("c_relu_made"), sem("c_down_made"), sem("c_added")
        ct_loaded = [sem(f"c_ct_loaded{n}") for n in range(RING + 1)]
        minus_half, half_made, padded = sb("c_minus_half", [128, 4]), sem("c_half_made"), sem("c_padded")
        measured, gathered, rooted, normed, turned, kept = (sem(f"c_{n}") for n in ("measured", "gathered", "rooted", "normed", "turned", "kept"))
        UNITS, TURNS = 2 * NCH, E // 2
        with nc.Block() as block:

            @block.sync
            def _(sp):
                def load(i, j):
                    sp.dma_start(w[:, j, :], t["L0_ffn_w"][:, bass.ds((i * 2 + j) * WIDTH, WIDTH)]).then_inc(we_loaded[j], 16)

                def load_pair(i, s):
                    for b in range(2):
                        rows = t["ctx"][bass.ds((i * (2 * UNITS) + (2 * s + b)) * CTX, 256), :].rearrange("(k p) d -> p k d", p=128)
                        sp.dma_start(ct[:, s % RING, 2 * b:2 * b + 2, :], rows).then_inc(ct_loaded[s % RING], 16)

                load(0, 0)
                sp.dma_start(ct[0:BATCH, EDGE, 0, :], t["ctx_last"]).then_inc(ct_loaded[EDGE], 16)
                for s in range(RING):
                    load_pair(0, s)
                load(0, 1)
                for dst, name in ((cx.wqT, "L1_xattn_WqT"), (cx.wkT, "L1_xattn_WkT"), (cx.wvT, "L1_xattn_WvT"), (cx.wout, "L1_xattn_Wout")):
                    sp.dma_start(dst[:].rearrange("p n d -> p (n d)"), t[name]).then_inc(cx.w_loaded, 16)
                sp.wait_ge(cx.mask_cast, 1)
                sp.dma_start(cx.mask_dram, cx.mask16[:]).then_inc(cx.mask_stored, 16)
                for s in range(RING, UNITS):
                    sp.wait_ge(turned, s - RING + 2)
                    load_pair(0, s)
                with sp.Fori(1, TURNS) as i:
                    for s in range(UNITS):
                        if s % NCH == 1:
                            sp.wait_ge(down_made, i * UNITS + NCH * (s // NCH - 1))
                            load(i, s // NCH)
                        sp.wait_ge(turned, i * UNITS + (s - RING + 2))
                        load_pair(i, s)

            @block.gpsimd
            def _(pool):
                def root(i, s):
                    pool.wait_ge(gathered, i * UNITS + (s + 2))
                    at = EDGE if s < 0 else s % RING
                    rows, tiles = (BATCH, 1) if s < 0 else (128, 4)
                    root = rstd[0:rows, at, 0:tiles]
                    nc.gpsimd.tensor_tensor(root, moments[0:rows, at, 0:tiles, 1], core.eps[0:rows, :].broadcast_to([rows, tiles]), ALU.add).then_inc(padded, 1)
                    pool.wait_ge(padded, i * UNITS + (s + 2))
                    nc.gpsimd.tensor_tensor(root, root, minus_half[0:rows, 0:tiles], ALU.pow).then_inc(rooted, 1)

                nc.gpsimd.memset(minus_half[:], -0.5).then_inc(half_made, 1)
                pool.wait_ge(half_made, 1)
                root(0, -1)

                def body(i, first, last):
                    for s in range(UNITS):
                        root(i, s)

                peeled(pool, TURNS, body)

            @block.tensor
            def _(pe):
                def up(i, s, first):
                    j, c = divmod(s, NCH)
                    if c == 0:
                        pe.wait_ge(we_loaded[j], i * 16 + 16)
                    for k in range(KCH):
                        if not (first and s == 0):
                            pe.wait_ge(relu_made, i * UNITS * KCH + ((s - 1) * KCH + k + 1))
                        nc.tensor.matmul(UP[k], w[:, j, 128 * k:128 * k + 128], chunk(core.yT, c), start=True, stop=True).then_inc(up_made, 1)

                def down(i, s, first):
                    j = s % UNITS // NCH
                    pe.wait_ge(relu_made, i * UNITS * KCH + (s + 1) * KCH)
                    if not first:
                        pe.wait_ge(added, i * UNITS + (s - 1))
                    for m in range(4):
                        for k in range(KCH):
                            ins = nc.tensor.matmul(Y[s % 2][:, m, :], hs[:, s % 2, k, 128 * m:128 * m + 128],
                                                   w[:, j, HID + 128 * k:HID + 128 * k + 128], start=(k == 0), stop=(k == KCH - 1))
                    ins.then_inc(down_made, 1)

                def turn(i, s, first):
                    pe.wait_ge(normed, i * UNITS + (s + 2))
                    if first and s < 0:
                        nc.tensor.transpose(TC[s % 2][:, 0:BATCH], ct[0:BATCH, EDGE, 0, :], core.ident[0:BATCH, 0:BATCH]).then_inc(turned, 1)
                        return
                    if not (first and s == 0):
                        pe.wait_ge(kept, i * UNITS + s)
                    for m in range(4):
                        ins = nc.tensor.transpose(TC[s % 2][:, 128 * m:128 * m + 128], ct[:, s % RING, m, :], core.ident[:])
                    ins.then_inc(turned, 1)

                def body(i, first, last):
                    for s in range(UNITS):
                        up(i, s, first)
                        if not (first and s < 1):
                            turn(i, s - 2, first)
                        if not (first and s == 0):
                            down(i, s - 1, first and s < 3)

                peeled(pe, TURNS, body)
                turn(TURNS, -2, False)
                down(TURNS, -1, False)
                turn(TURNS, -1, False)

            @block.scalar
            def _(act):
                def keep(i, s, first=False):
                    act.wait_ge(turned, i * UNITS + (s + 2))
                    if first and s < 0:
                        act.wait_ge(cx.affine_loaded, 16)
                        keys, src = cx.keyT[:, :, CTX - 1], TC[s % 2][:, 0:BATCH]
                    else:
                        keys = cx.keyT[:, bass.ds(i * (2 * UNITS) + 2 * s, 2), 0:256]
                        src = TC[s % 2].rearrange("p (b k) -> p b k", b=2)
                    nc.scalar.activation(keys, src, ACT.Identity, scale=cx.affine[:, 0:1], bias=cx.affine[:, 1:2]).then_inc(kept, 1)

                def body(i, first, last):
                    for s in range(UNITS):
                        if not (first and s < 2):
                            act.wait_ge(down_made, i * UNITS + (s - 1))
                        for k in range(KCH):
                            act.wait_ge(up_made, i * UNITS * KCH + (s * KCH + k + 1))
                            nc.scalar.activation(hs[:, s % 2, k, :], UP[k], ACT.Relu,
                                                 bias=w[:, s // NCH, 2 * HID + k:2 * HID + k + 1]).then_inc(relu_made, 1)

                        if not (first and s < 1):
                            keep(i, s - 2, first)

                peeled(act, TURNS, body)
                keep(TURNS, -2)
                keep(TURNS, -1)

            @block.vector
            def _(dve):
                def measure(i, s):
                    edge = isinstance(i, int) and s < 0
                    at = EDGE if edge else s % RING
                    rows, tiles = (BATCH, 1) if edge else (128, 4)
                    dve.wait_ge(ct_loaded[at], 16 if edge else (i * (UNITS // RING) + s // RING) * 32 + 32)
                    for m in range(tiles):
                        ins = nc.vector.bn_stats(stats[0:rows, at, m, :], ct[0:rows, at, m, :])
                    ins.then_inc(measured, 1)

                def gather(i, s):
                    edge = isinstance(i, int) and s < 0
                    at = EDGE if edge else s % RING
                    rows, tiles = (BATCH, 1) if edge else (128, 4)
                    for m in range(tiles):
                        ins = nc.vector.bn_aggr(moments[0:rows, at, m, :], stats[0:rows, at, m, :])
                    ins.then_inc(gathered, 1)

                def normalise(i, s, first=False, measuring=True):
                    edge = first and s < 0
                    at = EDGE if edge else s % RING
                    rows, tiles = (BATCH, 1) if edge else (128, 4)
                    dve.wait_ge(rooted, i * UNITS + (s + 2))
                    if measuring:
                        dve.wait_ge(measured, i * UNITS + (s + 3))
                    for m in range(tiles):
                        ins = nc.vector.tensor_scalar(ct[0:rows, at, m, :], ct[0:rows, at, m, :], moments[0:rows, at, m, 0:1],
                                                      rstd[0:rows, at, m:m + 1], ALU.subtract, ALU.mult)
                    ins.then_inc(normed, 1)

                measure(0, -1)
                dve.wait_ge(measured, 1)
                gather(0, -1)

                def body(i, first, last):
                    for s in range(UNITS):
                        measure(i, s)
                        normalise(i, s - 1, first)
                        gather(i, s)
                        j, c = divmod(s, NCH)
                        dve.wait_ge(down_made, i * UNITS + (s + 1))
                        if not (first and s < NCH):
                            dve.wait_ge(added, i * UNITS + (s - NCH + 1))
                        for m in range(4):
                            tile = NCH * c + m
                            ins = nc.vector.scalar_tensor_tensor(acc[:, tile, :], Y[s % 2][:, m, :], gates[:, bass.ds(i * 2 + j, 1), tile],
                                                                 acc[:, tile, :], ALU.mult, ALU.add)
                        ins.then_inc(added, 1)

                peeled(dve, TURNS, body)
                normalise(TURNS, -1, measuring=False)

        acc_t = sem("c_acc_t")
        with nc.Block() as block:

            @block.tensor
            def _(pe):
                for m in range(TILES):
                    ins = nc.tensor.transpose(core.bank[:, m // 4, 128 * (m % 4):128 * (m % 4) + 128], acc[:, m, :], core.ident[:])
                    if m % 4 == 3:
                        ins.then_inc(acc_t, 1)

            @block.vector
            def _(dve):
                for c in range(NCH):
                    dve.wait_ge(acc_t, c + 1)
                    nc.vector.tensor_tensor(chunk(core.xT, c), chunk(core.xT, c), core.bank[:, c, :], ALU.add)


def cross_attention_1(core, t, cx):
    nc = core.nc
    DH, KEYS = 64, CTX + LAT
    REST = KEYS - 256
    GROUPS, UNITS = BATCH // 4, 16
    layernorm(core, "ln3", core.xT, core.yT)
    with ExitStack() as own:
        sb = lambda n, s, dt=F32: core.sb(n, s, dt, own)
        sem = core.sem
        affine, keyT = cx.affine, cx.keyT
        latT = sb("d_latT", [128, TOK])
        wqk, wvo = sb("d_wqk", [128, HEADS, 128]), sb("d_wvo", [128, HEADS, 128])

        made = sem("d_w_made")
        with nc.Block() as block:

            @block.tensor
            def _(pe):
                pe.wait_ge(cx.w_loaded, 64)
                for n, (a, b) in enumerate(((cx.wqT, cx.wkT), (cx.wvT, cx.wout))):
                    for h in range(HEADS):
                        rows = slice(DH * (h % 2), DH * (h % 2) + DH)
                        at = 4 * n + 2 * (h % 2) + h // 8
                        ins = nc.tensor.matmul(core.bank[:, at, 128 * (h // 2 % 4):128 * (h // 2 % 4) + 128], a[rows, h // 2, :], b[rows, h // 2, :],
                                               start=True, stop=True)
                    ins.then_inc(made, 1)

            @block.vector
            def _(dve):
                for n, (dst, scale) in enumerate(((wqk, DH ** -0.5), (wvo, 1.0))):
                    dve.wait_ge(made, n + 1)
                    for odd in range(2):
                        out = dst[:].rearrange("p (m two) d -> p two m d", two=2)[:, odd]
                        src = core.bank[:, 4 * n + 2 * odd:4 * n + 2 * odd + 2, :].rearrange("p b (m d) -> p (b m) d", d=128)
                        nc.vector.tensor_scalar(out, src, scale, None, ALU.mult)

        layernorm(core, "ln4", core.yT, latT, affine[:, 2:3], affine[:, 3:4])

        key = sb("d_key", [128, 2, KEYS])
        maskb = sb("d_maskb", [1, 2, CTX], BF16)
        lowest = sb("d_lowest", [1, 128], BF16)
        xv = sb("d_xv", [128, 2, 3, 128])
        q = sb("d_q", [128, 4, HEADS, LAT])
        P = sb("d_p", [128, 4, KEYS])
        pT = sb("d_pT", [128, 2, 3, 128])
        nmax, total, rtotal = (sb(f"d_{n}", [128, 4]) for n in ("nmax", "total", "rtotal"))
        a = sb("d_a", [128, 4, HEADS, LAT])
        S = [core.bank[:, n, 0:KEYS] for n in (0, 1)]
        TP = [core.bank[:, n, 0:384] for n in (2, 3)]
        XP, OP = core.bank[:, 4, 0:384], core.bank[:, 5, :]
        Q = [core.bank[:, n, :] for n in (6, 7)]
        OUT = core.bank[:, 6, 0:128]
        key_loaded = [sem(f"d_key_loaded{n}") for n in (0, 1)]
        zeroed, low_made, latents_placed = sem("d_zeroed"), sem("d_low_made"), sem("d_latents_placed")
        xv_made, xv_copied, q_made, q_copied = sem("d_xv_made"), sem("d_xv_copied"), sem("d_q_made"), sem("d_q_copied")
        s_made, max_made, exp_made, recip, normed = (sem(f"d_{n}") for n in ("s_made", "max_made", "exp_made", "recip", "normed"))
        t_made, t_copied, o_made, o_copied = (sem(f"d_{n}") for n in ("t_made", "t_copied", "o_made", "o_copied"))
        out_made, out_added = sem("d_out_made"), sem("d_out_added")
        with nc.Block() as block:

            @block.sync
            def _(sp):
                def load(i, b, first):
                    n = i * 4 + b
                    if not first:
                        sp.wait_ge(s_made, (n - 1) * 4)
                        sp.wait_ge(xv_made, n - 1)
                    sp.dma_start(key[:, b % 2, :], keyT[:, bass.ds(n, 1), :].rearrange("p a k -> p (a k)")).then_inc(key_loaded[b % 2], 16)
                    sp.dma_start(maskb[:, b % 2, :], cx.mask_dram[bass.ds(n, 1), :]).then_inc(key_loaded[b % 2], 16)

                sp.wait_ge(cx.mask_stored, 16)
                sp.wait_ge(latents_placed, 1)
                load(0, 0, True)
                load(0, 1, True)
                load(0, 2, False)
                load(0, 3, False)
                with sp.Fori(1, GROUPS) as i:
                    for b in range(4):
                        load(i, b, False)

            @block.gpsimd
            def _(pool):
                nc.gpsimd.memset(lowest[:], -3.3895313892515355e38).then_inc(low_made, 1)
                nc.gpsimd.tensor_copy(keyT[:, :, CTX:KEYS], latT[:].rearrange("p (b q) -> p b q", b=BATCH)).then_inc(latents_placed, 1)

            @block.tensor
            def _(pe):
                def key_rows(i, b, first=False):
                    n = i * 4 + b
                    pe.wait_ge(key_loaded[b % 2], (i * 2 + b // 2) * 32 + 32)
                    if not first:
                        pe.wait_ge(xv_copied, n)
                    for k in range(3):
                        width = 128 if k < 2 else REST
                        ins = nc.tensor.transpose(XP[0:width, 128 * k:128 * k + 128], key[:, b % 2, 128 * k:128 * k + width], core.ident[:])
                    ins.then_inc(xv_made, 1)

                def queries(i, r, first=False):
                    if not (first and r < 2):
                        pe.wait_ge(q_copied, i * 4 + (r - 1))
                    if r == 0 and not first:
                        pe.wait_ge(out_added, i - 1)
                    for h in range(4):
                        ins = nc.tensor.matmul(Q[r % 2][:, 128 * h:128 * h + 128], wqk[:, 4 * r + h, :], latT[:, bass.ds(i * 128, 128)],
                                               start=True, stop=True)
                    ins.then_inc(q_made, 1)

                def scores(i, u, first):
                    b, g = divmod(u, 4)
                    if u == 0:
                        pe.wait_ge(q_copied, i * 4 + 4)
                    if g == 0:
                        pe.wait_ge(key_loaded[b % 2], (i * 2 + b // 2) * 32 + 32)
                    if not (first and u < 2):
                        pe.wait_ge(exp_made, i * UNITS + (u - 1))
                    nc.tensor.matmul(S[u % 2], q[:, b, 4 * g:4 * g + 4, :].rearrange("p h q -> p (h q)"), key[:, b % 2, :], start=True, stop=False)
                    nc.tensor.matmul(S[u % 2][:, 0:CTX], lowest[:], maskb[:, b % 2, :], start=False, stop=True).then_inc(s_made, 1)

                def transposes(i, u, first):
                    pe.wait_ge(normed, i * UNITS + (u + 1))
                    if not (first and u < 2):
                        pe.wait_ge(t_copied, i * UNITS + (u - 1))
                    for k in range(3):
                        width = 128 if k < 2 else REST
                        ins = nc.tensor.transpose(TP[u % 2][0:width, 128 * k:128 * k + 128], P[:, u % 4, 128 * k:128 * k + width], core.ident[:])
                    ins.then_inc(t_made, 1)

                def means(i, u, first):
                    b, g = divmod(u, 4)
                    if g == 0:
                        pe.wait_ge(xv_copied, i * 4 + (b + 1))
                        if not (first and b == 0):
                            pe.wait_ge(o_copied, i * 4 + b)
                    pe.wait_ge(t_copied, i * UNITS + (u + 1))
                    for k in range(3):
                        width = 128 if k < 2 else REST
                        ins = nc.tensor.matmul(OP[:, 128 * g:128 * g + 128], xv[0:width, b % 2, k, :], pT[0:width, u % 2, k, :],
                                               start=(k == 0), stop=(k == 2))
                    ins.then_inc(o_made, 1)

                def project(i):
                    pe.wait_ge(o_copied, i * 4 + 4)
                    pe.wait_ge(q_copied, i * 4 + 7)
                    for h in range(HEADS):
                        ins = nc.tensor.matmul(OUT, wvo[:, h, :], a[:, :, h, :], start=(h == 0), stop=(h == HEADS - 1))
                    ins.then_inc(out_made, 1)

                pe.wait_ge(low_made, 1)
                pe.wait_ge(zeroed, 1)
                for r in range(4):
                    queries(0, r, True)
                key_rows(0, 0, True)

                def body(i, first, last):
                    for u in range(UNITS):
                        scores(i, u, first)
                        if u >= 2:
                            transposes(i, u - 2, first)
                        if u >= 3:
                            means(i, u - 3, first)
                        if u % 4 == 1 and not (last and u // 4 == 3):
                            key_rows(i, u // 4 + 1)
                    if not last:
                        queries(i + 1, 0)
                    transposes(i, UNITS - 2, first)
                    means(i, UNITS - 3, first)
                    if not last:
                        queries(i + 1, 1)
                    transposes(i, UNITS - 1, first)
                    means(i, UNITS - 2, first)
                    if not last:
                        queries(i + 1, 2)
                        queries(i + 1, 3)
                    means(i, UNITS - 1, first)
                    if last:
                        pe.wait_ge(o_copied, i * 4 + 4)
                        for h in range(HEADS):
                            ins = nc.tensor.matmul(OUT, wvo[:, h, :], a[:, :, h, :], start=(h == 0), stop=(h == HEADS - 1))
                        ins.then_inc(out_made, 1)
                    else:
                        project(i)

                peeled(pe, GROUPS, body)

            @block.scalar
            def _(act):
                def queries(i, r):
                    act.wait_ge(q_made, i * 4 + (r + 1))
                    if r == 0:
                        act.wait_ge(s_made, i * UNITS)
                    nc.scalar.activation(q[:, :, 4 * r:4 * r + 4, :].rearrange("p b h q -> p h b q"),
                                         Q[r % 2].rearrange("p (h b q) -> p h b q", h=4, b=4), ACT.Copy).then_inc(q_copied, 1)

                def transposed(i, u, first):
                    act.wait_ge(t_made, i * UNITS + (u + 1))
                    if not (first and u < 2):
                        act.wait_ge(o_made, i * UNITS + (u - 1))
                    nc.scalar.activation(pT[:, u % 2].rearrange("p k q -> p (k q)"), TP[u % 2], ACT.Copy).then_inc(t_copied, 1)

                def body(i, first, last):
                    for u in range(UNITS):
                        act.wait_ge(max_made, i * UNITS + (u + 1))
                        if not (first and u < 4):
                            act.wait_ge(t_made, i * UNITS + (u - 3))
                        nc.scalar.activation(P[:, u % 4, :], S[u % 2], ACT.Exp, bias=nmax[:, u % 4:u % 4 + 1],
                                             accum_out=total[:, u % 4:u % 4 + 1]).then_inc(exp_made, 1)
                        if u >= 2:
                            transposed(i, u - 2, first)
                    if not last:
                        queries(i + 1, 0)
                    transposed(i, UNITS - 2, first)
                    if not last:
                        queries(i + 1, 1)
                    transposed(i, UNITS - 1, first)
                    if not last:
                        queries(i + 1, 2)
                        queries(i + 1, 3)

                for r in range(4):
                    act.wait_ge(q_made, r + 1)
                    nc.scalar.activation(q[:, :, 4 * r:4 * r + 4, :].rearrange("p b h q -> p h b q"),
                                         Q[r % 2].rearrange("p (h b q) -> p h b q", h=4, b=4), ACT.Copy).then_inc(q_copied, 1)
                peeled(act, GROUPS, body)

            @block.vector
            def _(dve):
                def key_rows(i, b, first=False):
                    n = i * 4 + b
                    dve.wait_ge(xv_made, n + 1)
                    if not first:
                        dve.wait_ge(o_made, (n - 1) * 4)
                    nc.vector.tensor_copy(xv[:, b % 2].rearrange("p k d -> p (k d)"), XP).then_inc(xv_copied, 1)

                def normalise(i, u):
                    dve.wait_ge(exp_made, i * UNITS + (u + 1))
                    nc.vector.reciprocal(rtotal[:, u % 4:u % 4 + 1], total[:, u % 4:u % 4 + 1]).then_inc(recip, 1)
                    dve.wait_ge(recip, i * UNITS + (u + 1))
                    nc.vector.tensor_scalar(P[:, u % 4, :], P[:, u % 4, :], rtotal[:, u % 4:u % 4 + 1], None, ALU.mult).then_inc(normed, 1)

                def means(i, b, first):
                    dve.wait_ge(o_made, i * UNITS + 4 * b + 4)
                    if b == 0 and not first:
                        dve.wait_ge(out_made, i)
                    nc.vector.tensor_copy(a[:, b].rearrange("p h q -> p (h q)"), OP).then_inc(o_copied, 1)

                def body(i, first, last):
                    for u in range(UNITS):
                        dve.wait_ge(s_made, i * UNITS + (u + 1))
                        nc.vector.tensor_reduce(nmax[:, u % 4:u % 4 + 1], S[u % 2], AXX, ALU.max, negate=True).then_inc(max_made, 1)
                        if u >= 1:
                            normalise(i, u - 1)
                        if u % 4 == 2:
                            if u > 4:
                                means(i, u // 4 - 1, first)
                            if not (last and u // 4 == 3):
                                key_rows(i, u // 4 + 1, first and u < 4)
                    normalise(i, UNITS - 1)
                    means(i, 3, first)
                    dve.wait_ge(out_made, i + 1)
                    toks = bass.ds(i * 128, 128)
                    nc.vector.scalar_tensor_tensor(core.xT[:, toks], OUT, affine[:, 4:5], core.xT[:, toks], ALU.add, ALU.add).then_inc(out_added, 1)

                nc.vector.memset(XP, 0.0)
                for n in range(2):
                    ins = nc.vector.memset(TP[n], 0.0)
                ins.then_inc(zeroed, 1)
                key_rows(0, 0, True)
                peeled(dve, GROUPS, body)


def recurrent_1(core, t):
    nc = core.nc
    EXP, K, KCH = 192, 4, 4
    PER = CHUNK // LAT
    layernorm(core, "ln5", core.xT, core.yT)
    with ExitStack() as own:
        sb = lambda n, s, dt=F32: core.sb(n, s, dt, own)
        sem = core.sem
        cols = sb("e_cols", [128, 17])
        fb = sb("e_fb", [128, 4])
        fneg, fhalf = sb("e_fneg", [128, 4]), sb("e_fhalf", [128, 4])
        pw, fw, dpa, dpb = sb("e_pw", [128, 128]), sb("e_fw", [128, 2 * EXP]), sb("e_dpa", [128, 128]), sb("e_dpb", [64, 128])
        w1, w2 = sb("e_w1", [128, 512]), sb("e_w2", [128, KCH, 128])
        hT = sb("e_hT", [128, TOK])
        w_loaded = sem("e_w_loaded")

        with nc.Block() as block:

            @block.sync
            def _(sp):
                for dst, name in ((cols[:], "cols"), (fb[:], "f_b"), (pw[:], "pwT"), (fw[:], "fT"), (dpa[:], "dpT"), (w1[:], "mlp_w1T"),
                                  (w2[:].rearrange("p k d -> p (k d)"), "mlp_w2T")):
                    src = t[f"L1_attn_{name}"]
                    sp.dma_start(dst, src[0:128, :]).then_inc(w_loaded, 16)
                sp.dma_start(dpb[:], t["L1_attn_dpT"][128:EXP, :]).then_inc(w_loaded, 16)
                sp.wait_ge(w_loaded, 128)

        layernorm(core, "ln6", core.yT, hT, cols[:, 0:1], cols[:, 1:2])

        with ExitStack() as part:
            cT = core.sb("e_cT", [128, TOK], ctx=part)
            tap, conv_made, pw_made, b_made = sem("e_tap"), sem("e_conv_made"), sem("e_pw_made"), sem("e_b_made")
            block = part.enter_context(nc.Block())

            @block.vector
            def _(dve):
                nc.vector.tensor_scalar(fneg[:], fb[:], -1.0, None, ALU.mult)
                nc.vector.tensor_scalar(fhalf[:], fb[:], 0.5, None, ALU.add)
                for k in range(K):
                    for c in range(NCH):
                        src, dst = (chunk(v, c).rearrange("p (b t) -> p b t", t=LAT) for v in (hT, cT))
                        weight = cols[:, 9 + K - 1 - k:9 + K - k]
                        if k == 0:
                            ins = nc.vector.tensor_scalar(dst, src, weight, cols[:, 8:9], ALU.mult, ALU.add)
                        else:
                            dve.wait_ge(tap, (k - 1) * NCH + c + 1)
                            ins = nc.vector.scalar_tensor_tensor(dst[:, :, k:], src[:, :, :LAT - k], weight, dst[:, :, k:], ALU.mult, ALU.add)
                        ins.then_inc(tap, 1)
                for c in range(NCH):
                    dve.wait_ge(pw_made, c + 1)
                    nc.vector.scalar_tensor_tensor(chunk(core.yT, c), core.bank[:, c, :], cols[:, 6:7], chunk(core.yT, c), ALU.add, ALU.add)

            @block.tensor
            def _(pe):
                for c in range(NCH):
                    pe.wait_ge(tap, (K - 1) * NCH + c + 1)
                    nc.tensor.matmul(core.bank[:, c, :], pw[:], chunk(cT, c), start=True, stop=True).then_inc(pw_made, 1)

        layernorm(core, "ln7", core.yT, hT, cols[:, 2:3], cols[:, 3:4])

        with ExitStack() as part:
            pb = lambda n: core.sb(n, [128, 2, CHUNK], ctx=part)
            kept, new, cand, seq = (
                [pb(f"e_{n}{h}") for h in (0, 1)] for n in ("kept", "new", "cand", "seq"))
            f_made, sig_made, step, scanned, dp_made, dp_added = (
                sem(f"e_{n}") for n in ("f_made", "sig_made", "step", "scanned", "dp_made", "dp_added"))
            ROWS = (128, 64)
            COLS = (0, 128, EXP, EXP + 128)
            block = part.enter_context(nc.Block())

            @block.tensor
            def _(pe):
                def gates(c):
                    if c >= 2:
                        pe.wait_ge(dp_added, c - 1)
                    for n in range(4):
                        rows = ROWS[n % 2]
                        ins = nc.tensor.matmul(core.bank[0:rows, 4 * (c % 2) + n, :], fw[:, COLS[n]:COLS[n] + rows], chunk(hT, c), start=True, stop=True)
                    ins.then_inc(f_made, 1)

                gates(0)
                gates(1)
                for c in range(NCH):
                    pe.wait_ge(scanned, 2 * c + 2)
                    out = core.bank[:, 4 * (c % 2), :]
                    nc.tensor.matmul(out, dpa[:], seq[0][:, c % 2, :], start=True, stop=False)
                    nc.tensor.matmul(out, dpb[:], seq[1][0:64, c % 2, :], start=False, stop=True).then_inc(dp_made, 1)
                    if c + 2 < NCH:
                        gates(c + 2)

            @block.scalar
            def _(act):
                for c in range(NCH):
                    act.wait_ge(f_made, c + 1)
                    if c >= 2:
                        act.wait_ge(scanned, 2 * (c - 1))
                    for h, rows in enumerate(ROWS):
                        bank = [core.bank[0:rows, 4 * (c % 2) + n, :] for n in (h, 2 + h)]
                        r = slice(0, rows)
                        nc.scalar.activation(new[h][r, c % 2, :], bank[0], ACT.Sigmoid, bias=fb[r, h:h + 1])
                        nc.scalar.activation(kept[h][r, c % 2, :], bank[0], ACT.Sigmoid, bias=fneg[r, h:h + 1], scale=-1.0)
                        nc.scalar.activation(cand[h][r, c % 2, :], bank[1], ACT.Sigmoid, bias=fb[r, 2 + h:3 + h]).then_inc(sig_made, 1)

            @block.vector
            def _(dve):
                n = 0

                def then(ins):
                    nonlocal n
                    ins.then_inc(step, 1)
                    n += 1
                    dve.wait_ge(step, n)

                for c in range(NCH):
                    for h, rows in enumerate(ROWS):
                        r = slice(0, rows)
                        k_, n_, c_, s_ = (v[h][r, c % 2, :] for v in (kept, new, cand, seq))
                        dve.wait_ge(sig_made, 2 * c + h + 1)
                        if c >= 2:
                            dve.wait_ge(dp_made, c - 1)
                        then(nc.vector.scalar_tensor_tensor(c_, core.bank[r, 4 * (c % 2) + 2 + h, :], fhalf[r, 2 + h:3 + h], c_, ALU.add, ALU.max))
                        then(nc.vector.tensor_tensor(n_, n_, c_, ALU.mult))
                        first_k, first_n = (v.rearrange("p (b t) -> p b t", t=LAT)[:, :, 0:1] for v in (k_, n_))
                        then(nc.vector.scalar_tensor_tensor(first_n, first_k, 0.5, first_n, ALU.mult, ALU.add))
                        then(nc.vector.tensor_scalar(first_k, first_k, 0.0, None, ALU.mult))
                        nc.vector.tensor_tensor_scan(s_, k_, n_, 0.0, ALU.mult, ALU.add).then_inc(scanned, 1)
                    dve.wait_ge(dp_made, c + 1)
                    nc.vector.tensor_tensor(chunk(core.yT, c), chunk(core.yT, c), core.bank[:, 4 * (c % 2), :], ALU.add).then_inc(dp_added, 1)

        layernorm(core, "ln8", core.yT, hT, cols[:, 4:5], cols[:, 5:6])

        with ExitStack() as part:
            mid = core.sb("e_mid", [128, 2, KCH, CHUNK], ctx=part)
            up_made, act_made, down_made, summed = sem("e_up_made"), sem("e_act_made"), sem("e_down_made"), sem("e_summed")
            block = part.enter_context(nc.Block())

            @block.tensor
            def _(pe):
                def up(c):
                    for k in range(KCH):
                        if c >= 1:
                            pe.wait_ge(act_made, (c - 1) * KCH + k + 1)
                        nc.tensor.matmul(core.bank[:, k, :], w1[:, 128 * k:128 * k + 128], chunk(hT, c), start=True, stop=True).then_inc(up_made, 1)

                up(0)
                for c in range(NCH):
                    if c + 1 < NCH:
                        up(c + 1)
                    pe.wait_ge(act_made, (c + 1) * KCH)
                    for k in range(KCH):
                        ins = nc.tensor.matmul(core.bank[:, 4 + c, :], w2[:, k, :], mid[:, c % 2, k, :], start=(k == 0), stop=(k == KCH - 1))
                    ins.then_inc(down_made, 1)

            @block.scalar
            def _(act):
                for c in range(NCH):
                    if c >= 2:
                        act.wait_ge(down_made, c - 1)
                    for k in range(KCH):
                        act.wait_ge(up_made, c * KCH + k + 1)
                        nc.scalar.activation(mid[:, c % 2, k, :], core.bank[:, k, :], ACT.Gelu, bias=cols[:, 13 + k:14 + k]).then_inc(act_made, 1)

            @block.vector
            def _(dve):
                for c in range(NCH):
                    nc.vector.tensor_tensor(chunk(core.xT, c), chunk(core.xT, c), chunk(core.yT, c), ALU.add).then_inc(summed, 1)
                for c in range(NCH):
                    dve.wait_ge(down_made, c + 1)
                    dve.wait_ge(summed, c + 1)
                    nc.vector.scalar_tensor_tensor(chunk(core.xT, c), core.bank[:, 4 + c, :], cols[:, 7:8], chunk(core.xT, c), ALU.add, ALU.add)


def quantised_ffn_1(core, t):
    nc = core.nc
    INNER, KCH = 512, 4
    ROUND = 1.5 * 2.0 ** 23
    QMAX, QMIN, TINY = 127.0, -128.0, 1e-5
    layernorm(core, "ln9", core.xT, core.yT)
    with ExitStack() as own:
        sb = lambda n, s, dt=F32: core.sb(n, s, dt, own)
        sem = core.sem
        wq = sb("f_wq", [128, 3, INNER], BF16)
        wmean, winv = sb("f_wmean", [128, 3]), sb("f_winv", [128, 3])
        xqT = sb("f_xqT", [128, TOK], BF16)
        rows_in = sb("f_rows_in", [128, TILES])
        sg, su = sb("f_sg", [128, TILES]), sb("f_su", [128, TILES])
        bias_round, wdown = sb("f_bias_round", [128, 1]), sb("f_wdown", [128, 1])

        with ExitStack() as pre:
            w = core.sb("f_w", [128, 3, INNER], ctx=pre)
            q = core.sb("f_q", [128, TILES, 128], ctx=pre)
            inv = core.sb("f_inv", [128, TILES], ctx=pre)
            w_loaded, wsum, wmean_made, step = sem("f_w_loaded"), sem("f_wsum"), sem("f_wmean_made"), sem("f_step")
            x_turned, y_turned, x_kept, q_made, q_turned = (sem(f"f_{n}") for n in ("x_turned", "y_turned", "x_kept", "q_made", "q_turned"))
            block = pre.enter_context(nc.Block())

            @block.sync
            def _(sp):
                sp.dma_start(w[:].rearrange("p n d -> p (n d)"), t["L1_ffn_w"]).then_inc(w_loaded, 16)
                sp.wait_ge(w_loaded, 16)

            @block.tensor
            def _(pe):
                for v, base, done in ((core.yT, 0, y_turned), (core.xT, 4, x_turned)):
                    for m in range(TILES):
                        ins = nc.tensor.transpose(core.bank[:, base + m // 4, 128 * (m % 4):128 * (m % 4) + 128], v[:, 128 * m:128 * m + 128], core.ident[:])
                    ins.then_inc(done, 1)
                pe.wait_ge(wsum, 1)
                pe.wait_ge(x_kept, 1)
                nc.tensor.matmul(core.bank[:, 4, 0:3], core.mean_w[:], wmean[:], start=True, stop=True).then_inc(wmean_made, 1)
                pe.wait_ge(q_made, 1)
                for m in range(TILES):
                    ins = nc.tensor.transpose(core.bank[:, m // 4, 128 * (m % 4):128 * (m % 4) + 128], q[:, m, :], core.ident[:])
                ins.then_inc(q_turned, 1)

            @block.scalar
            def _(act):
                act.wait_ge(x_turned, 1)
                nc.scalar.activation(core.out[:].rearrange("p m d -> p (m d)"), core.bank[:, 4:8, :].rearrange("p c n -> p (c n)"), ACT.Copy).then_inc(x_kept, 1)

            @block.vector
            def _(dve):
                n = 0

                def then(ins):
                    nonlocal n
                    ins.then_inc(step, 1)
                    n += 1
                    dve.wait_ge(step, n)

                v = nc.vector
                v.memset(bias_round[:], -ROUND)
                dve.wait_ge(w_loaded, 16)
                v.tensor_reduce(wmean[:], w[:], AXX, ALU.add, apply_absolute_value=True).then_inc(wsum, 1)
                turned = core.bank[:, 0:4, :].rearrange("p c (m d) -> p (c m) d", d=128)
                dve.wait_ge(y_turned, 1)
                then(v.tensor_reduce(rows_in[:], turned, AXX, ALU.max, apply_absolute_value=True))
                then(v.tensor_scalar(rows_in[:], rows_in[:], TINY, None, ALU.max))
                then(v.reciprocal(inv[:], rows_in[:]))
                then(v.tensor_scalar(inv[:], inv[:], QMAX, None, ALU.mult))
                then(v.tensor_tensor(q[:], turned, inv[:].unsqueeze(2).broadcast_to([128, TILES, 128]), ALU.mult))
                then(v.tensor_scalar(q[:], q[:], ROUND, -ROUND, ALU.add, ALU.add))
                v.tensor_scalar(q[:], q[:], QMAX, QMIN, ALU.min, ALU.max).then_inc(q_made, 1)
                dve.wait_ge(wmean_made, 1)
                then(v.tensor_scalar(wmean[:], core.bank[:, 4, 0:3], 1.0 / INNER, TINY, ALU.mult, ALU.max))
                then(v.reciprocal(winv[:], wmean[:]))
                for m in range(3):
                    then(v.tensor_scalar(w[:, m, :], w[:, m, :], winv[:, m:m + 1], ROUND, ALU.mult, ALU.add))
                then(v.tensor_scalar(w[:], w[:], -ROUND, 1.0, ALU.add, ALU.min))
                v.tensor_scalar(wq[:], w[:], -1.0, None, ALU.max)
                then(v.tensor_scalar(rows_in[:], rows_in[:], 1.0 / QMAX, None, ALU.mult))
                v.tensor_scalar(wdown[:], wmean[:, 2:3], 1.0 / QMAX, None, ALU.mult)
                v.tensor_scalar(sg[:], rows_in[:], wmean[:, 0:1], None, ALU.mult)
                v.tensor_scalar(su[:], rows_in[:], wmean[:, 1:2], None, ALU.mult)
                dve.wait_ge(q_turned, 1)
                v.tensor_copy(xqT[:].rearrange("p (c n) -> p c n", c=NCH), core.bank[:, 0:4, :])

        gs, h = sb("f_gs", [128, 2, INNER]), sb("f_h", [128, 2, INNER])
        hT = sb("f_hT", [128, 2, KCH, 128], BF16)
        alpha = sb("f_alpha", [128, 2])
        most, mult, sd = sb("f_most", [128, 2]), sb("f_mult", [128, 2]), sb("f_sd", [128, 2])
        G, U = [core.bank[:, n, :] for n in (0, 1)], [core.bank[:, n, :] for n in (2, 3)]
        T, DN = [core.bank[:, n, :] for n in (4, 5)], [core.bank[:, n, 0:128] for n in (6, 7)]
        TURNS = TILES // 2
        alpha_made, g_made, silu_made, rounded, t_made, t_copied, d_made = (
            sem(f"f_{n}") for n in ("alpha_made", "g_made", "silu_made", "rounded", "t_made", "t_copied", "d_made"))
        gu_free, finished, quant = (sem(f"f_{n}") for n in ("gu_free", "finished", "quant"))
        QUANT = 5
        with nc.Block() as block:

            @block.tensor
            def _(pe):
                def turn(i, j):
                    n = i * 2 + j
                    pe.wait_ge(rounded, n + 1)
                    pe.wait_ge(t_copied, n + 1)
                    for k in range(KCH):
                        ins = nc.tensor.transpose(T[j % 2][:, 128 * k:128 * k + 128], h[:, j % 2, 128 * k:128 * k + 128], core.ident[:])
                    ins.then_inc(t_made, 1)

                def down(i, j):
                    n = i * 2 + j
                    pe.wait_ge(t_copied, n + 3)
                    pe.wait_ge(finished, n + 1)
                    for k in range(KCH):
                        ins = nc.tensor.matmul(DN[j % 2], hT[:, j % 2, k, :], wq[:, 2, 128 * k:128 * k + 128], start=(k == 0), stop=(k == KCH - 1))
                    ins.then_inc(d_made, 1)

                def body(i, first, last):
                    for j in range(2):
                        pe.wait_ge(gu_free, i * 2 + (j + 1))
                        src = xqT[:, bass.ds((i * 2 + j) * 128, 128)]
                        nc.tensor.matmul(G[j], src, wq[:, 0, :], start=True, stop=True)
                        nc.tensor.matmul(U[j], src, wq[:, 1, :], start=True, stop=True).then_inc(g_made, 1)
                        if not (first and j == 0):
                            turn(i, j - 1)
                        if not first:
                            down(i, j - 2)

                pe.sem_inc(d_made, 2)
                peeled(pe, TURNS, body)
                turn(TURNS, -1)
                down(TURNS, -2)
                down(TURNS, -1)

            @block.scalar
            def _(act):
                def turned(i, j):
                    n = i * 2 + j
                    act.wait_ge(t_made, n + 1)
                    act.wait_ge(d_made, n + 1)
                    nc.scalar.activation(hT[:, j % 2].rearrange("p k q -> p (k q)"), T[j % 2], ACT.Identity,
                                         bias=bias_round[:, 0:1]).then_inc(t_copied, 1)

                def body(i, first, last):
                    for j in range(2):
                        act.wait_ge(alpha_made, i * 2 + (j + 1))
                        act.wait_ge(g_made, i * 2 + (j + 1))
                        nc.scalar.activation(gs[:, j, :], G[j], ACT.Silu, scale=alpha[:, j:j + 1]).then_inc(silu_made, 1)
                        if not (first and j == 0):
                            turned(i, j - 1)

                act.sem_inc(t_copied, 2)
                peeled(act, TURNS, body)
                turned(TURNS, -1)

            @block.vector
            def _(dve):
                v = nc.vector

                def finish(i, j):
                    n = i * 2 + j
                    dve.wait_ge(d_made, n + 3)
                    row = core.out[:, bass.ds(n, 1), :].rearrange("p a d -> p (a d)")
                    v.scalar_tensor_tensor(row, DN[j % 2], sd[:, j % 2:j % 2 + 1], row, ALU.mult, ALU.add).then_inc(finished, 1)

                def body(i, first, last):
                    for j in range(2):
                        n = i * 2 + j
                        J = slice(j, j + 1)
                        v.tensor_copy(alpha[:, J], sg[:, bass.ds(n, 1)]).then_inc(alpha_made, 1)
                        if not first:
                            finish(i, j - 2)
                        dve.wait_ge(silu_made, n + 1)
                        v.scalar_tensor_tensor(h[:, j, :], U[j], su[:, bass.ds(n, 1)], gs[:, j, :], ALU.mult, ALU.mult).then_inc(gu_free, 1)
                        dve.wait_ge(gu_free, n + 3)
                        v.tensor_reduce(most[:, J], h[:, j, :], AXX, ALU.max, apply_absolute_value=True).then_inc(quant, 1)
                        dve.wait_ge(quant, n * QUANT + 1)
                        v.tensor_scalar(most[:, J], most[:, J], TINY, None, ALU.max).then_inc(quant, 1)
                        dve.wait_ge(quant, n * QUANT + 2)
                        v.reciprocal(mult[:, J], most[:, J]).then_inc(quant, 1)
                        dve.wait_ge(quant, n * QUANT + 3)
                        v.tensor_scalar(mult[:, J], mult[:, J], QMAX, None, ALU.mult).then_inc(quant, 1)
                        dve.wait_ge(finished, n + 1)
                        v.tensor_scalar(sd[:, J], most[:, J], wdown[:, 0:1], None, ALU.mult)
                        dve.wait_ge(quant, n * QUANT + 4)
                        v.tensor_scalar(h[:, j, :], h[:, j, :], mult[:, J], ROUND, ALU.mult, ALU.add).then_inc(quant, 1)
                        dve.wait_ge(quant, n * QUANT + 5)
                        v.tensor_scalar(h[:, j, :], h[:, j, :], ROUND + QMAX, ROUND + QMIN, ALU.min, ALU.max).then_inc(rounded, 1)

                dve.sem_inc(gu_free, 2)
                dve.sem_inc(finished, 2)
                peeled(dve, TURNS, body)
                finish(TURNS, -2)
                finish(TURNS, -1)


def perceiver(nc, t, out):
    with ExitStack() as ctx:
        core = Core(nc, ctx)
        setup(core, t["xT"])
        cross_attention_0(core, t)
        memory_attention_0(core, t)
        with ExitStack() as own:
            cx = Context(core, own)
            experts_0(core, t, cx)
            cross_attention_1(core, t, cx)
        recurrent_1(core, t)
        quantised_ffn_1(core, t)
        stored = core.sem("stored")
        with nc.Block() as block:

            @block.sync
            def _(sp):
                sp.dma_start(out.rearrange("(m p) d -> p m d", p=128), core.out[:]).then_inc(stored, 16)
                sp.wait_ge(stored, 16)


def layouts(inputs):
    import numpy as np

    a = {k: np.asarray(v) for k, v in inputs.items()}
    put = {"xT": a["x"].reshape(TOK, D).T, "ctxT": a["ctx_1024"].reshape(BATCH * CTX, D).T,
           "ctx": a["ctx_1024"].reshape(BATCH * CTX, D), "ctx_last": a["ctx_1024"][:, CTX - 1, :],
           "mask0": a["mask_Bx1x1xS2_fk0"].reshape(1, BATCH * CTX)}
    for n in ("Wq", "Wk", "Wv", "Wo"):
        put[f"L0_xattn_{n}"] = a[f"L0_xattn_{n}"]
    for n in ("bq", "bk", "bv", "bo"):
        put[f"L0_xattn_{n}"] = a[f"L0_xattn_{n}"].reshape(D, 1)
    for n in ("Wq", "Wk", "Wv", "memory"):
        put[f"L0_attn_{n}"] = a[f"L0_attn_{n}"]
    put["L0_attn_memory_norm"] = a["L0_attn_memory_norm"].reshape(64, 1)
    put["L0_attn_memory_weight"] = a["L0_attn_memory_weight"].reshape(1, 1)
    put["L0_ffn_router_w"], put["L0_ffn_b2"] = a["L0_ffn_router_w"], a["L0_ffn_b2"]
    put["L0_ffn_router_b"] = a["L0_ffn_router_b"].reshape(1, 8)
    put["L0_ffn_w"] = np.concatenate([a["L0_ffn_w1"].transpose(1, 0, 2),
                                      a["L0_ffn_w2"].reshape(8, 4, 128, 128).transpose(2, 0, 1, 3).reshape(128, 8, 512),
                                      a["L0_ffn_b1"].reshape(8, 4, 128).transpose(2, 0, 1)], axis=2).reshape(128, -1)
    pairs = lambda w: w.reshape(8, 128, 128).transpose(1, 0, 2).reshape(128, 1024)
    put["L1_xattn_WqT"] = pairs(a["L1_xattn_Wq"].T)
    put["L1_xattn_WkT"] = pairs(a["L1_xattn_Wkv"][:, :1024].T)
    put["L1_xattn_WvT"] = pairs(a["L1_xattn_Wkv"][:, 1024:].T)
    put["L1_xattn_Wout"] = pairs(a["L1_xattn_Wout"])
    put["L1_xattn_affine"] = np.stack([a[f"L1_xattn_{n}"] for n in ("g_media", "b_media", "g_latent", "b_latent", "bout")], axis=1)
    cols = [a[f"L1_attn_{n}"] for n in ("ln1_g", "ln1_b", "ln2_g", "ln2_b", "ln3_g", "ln3_b", "pw_b", "mlp_b2", "dw_b")]
    cols += list(a["L1_attn_dw_w"][:, 0, :].T) + list(a["L1_attn_mlp_b1"].reshape(4, 128))
    put["L1_attn_cols"] = np.stack(cols, axis=1)
    fb = a["L1_attn_f_b"]
    put["L1_attn_f_b"] = np.stack([fb[0:128], np.concatenate([fb[128:192]] * 2), fb[192:320], np.concatenate([fb[320:384]] * 2)], axis=1)
    put["L1_attn_pwT"], put["L1_attn_fT"], put["L1_attn_dpT"] = a["L1_attn_pw_w"].T, a["L1_attn_f_w"].T, a["L1_attn_dp_w"].T
    put["L1_attn_mlp_w1T"] = a["L1_attn_mlp_w1"].T
    put["L1_attn_mlp_w2T"] = a["L1_attn_mlp_w2"].T.reshape(4, 128, 128).transpose(1, 0, 2).reshape(128, 512)
    put["L1_ffn_w"] = np.concatenate([a["L1_ffn_w_gate"].T, a["L1_ffn_w_up"].T,
                                      a["L1_ffn_w_down"].T.reshape(4, 128, 128).transpose(1, 0, 2).reshape(128, 512)], axis=1)
    put["mask1"] = a["mask_BxS2_bk0"]
    return {k: np.ascontiguousarray(v) for k, v in put.items()}


def kernel(**inputs):
    import concourse.bacc as bacc
    import numpy as np
    from concourse.bass_utils import run_bass_kernel_spmd

    nc = bacc.Bacc("TRN2", target_bir_lowering=False, num_devices=1)
    arrays = layouts(inputs)
    t = {k: nc.dram_tensor(f"in_{k}", v.shape, mybir.dt.from_np(v.dtype), kind="ExternalInput").ap() for k, v in arrays.items()}
    out = nc.dram_tensor("out_rows", (TOK, D), F32, kind="ExternalOutput").ap()
    perceiver(nc, t, out)
    r = run_bass_kernel_spmd(nc, [{f"in_{k}": v for k, v in arrays.items()}], core_ids=[0])
    return np.ascontiguousarray(r.results[0]["out_rows"]).reshape(BATCH, LAT, D)
```

```python
import concourse.bass as bass
from concourse import mybir
from contextlib import ExitStack

F32 = mybir.dt.float32
BF16 = mybir.dt.bfloat16
ALU = mybir.AluOpType
ACT = mybir.ActivationFunctionType
AXX = mybir.AxisListType.X

BATCH, LAT, D, CTX = 64, 32, 128, 257
TOK = BATCH * LAT
HEADS = 16
CHUNK = 512
NCH = TOK // CHUNK
TILES = TOK // 128
EPS = 1e-5


def bf16_parts(value, count):
    import numpy as np

    parts = []
    rest = np.float32(value)
    for _ in range(count):
        part = (rest.view(np.uint32) & np.uint32(0xFFFF0000)).view(np.float32)
        parts.append(float(part))
        rest = np.float32(rest - part)
    return parts


class Core:

    def __init__(self, nc, ctx):
        self.nc, self.ctx = nc, ctx
        self.bank = ctx.enter_context(nc.psum_tensor("bank", [128, 8, CHUNK], F32))
        self.xT = self.sb("xT", [128, TOK])
        self.yT = self.sb("yT", [128, TOK])
        self.ident = self.sb("ident", [128, 128])
        self.mean_w = self.sb("mean_w", [128, 128])
        self.out = self.sb("rows_out", [128, TILES, 128])
        self.norm_sems = [self.sem(f"norm_{n}") for n in ("mean", "centred", "squared", "var", "log", "rstd", "scaled")]
        self.norms = 0
        self.rows_moved = self.sem("rows_moved")
        self.eps = self.sb("eps", [128, 1])

    def sb(self, name, shape, dt=F32, ctx=None):
        return (ctx or self.ctx).enter_context(self.nc.sbuf_tensor(name, shape, dt))

    def sem(self, name):
        return self.ctx.enter_context(self.nc.semaphore(name))


def chunk(t, c):
    return t[:, c * CHUNK:(c + 1) * CHUNK]


def peeled(eng, turns, body):
    body(0, True, False)
    with eng.Fori(1, turns - 1) as i:
        body(i, False, False)
    body(turns - 1, False, True)


class Weights:

    def __init__(self, core):
        def sb(prefix, shapes, dt=F32):
            return {n: core.sb(f"{prefix}_{n}", shape, dt) for n, shape in shapes.items()}

        square = [128, 128]
        self.a = sb("wa", {"wq": square, "wk": square, "wv": square, "wo": square, "bias": [128, 4]})
        self.b = sb("wb", {"wq": square, "wk": square, "wv": square, "mem": square, "norm_col": [128, 1], "gate": [128, 4]})
        self.c = sb("wc", {"router": [128, 8], "router_b": [128, 8], "b2": [8, 128]})
        self.e = sb("we", {"cols": [128, 17], "fb": [128, 4], "pw": square, "fw": [128, 384], "dpa": square, "dpb": [64, 128],
                           "w1": [128, 512], "w2": [128, 4, 128]})
        self.a_loaded, self.b_loaded, self.rest_loaded = (core.sem(f"w{n}_loaded") for n in ("a", "b", "rest"))
        self.zeroed = core.sem("wb_zeroed")

    def load(self, sp, t):
        for n, name in (("wq", "Wq"), ("wk", "Wk"), ("wv", "Wv"), ("wo", "Wo")):
            sp.dma_start(self.a[n][:], t[f"L0_xattn_{name}"]).then_inc(self.a_loaded, 16)
        for n, name in enumerate(("bq", "bk", "bv", "bo")):
            sp.dma_start(self.a["bias"][:, n:n + 1], t[f"L0_xattn_{name}"]).then_inc(self.a_loaded, 16)

    def load_rest(self, sp, t):
        sp.wait_ge(self.zeroed, 1)
        sp.dma_start(self.b["wq"][:], t["L0_attn_Wq"]).then_inc(self.b_loaded, 16)
        for dst, name in ((self.b["wk"], "L0_attn_Wk"), (self.b["wv"], "L0_attn_Wv")):
            for r in range(2):
                sp.dma_start(dst[:].rearrange("p (n r d) -> p n r d", r=2, d=8)[:, :, r, :],
                             t[name].rearrange("p (n d) -> p n d", d=8)).then_inc(self.b_loaded, 16)
        for r in range(2):
            rows = slice(64 * r, 64 * r + 64)
            sp.dma_start(self.b["mem"][rows, rows], t["L0_attn_memory"]).then_inc(self.b_loaded, 16)
            sp.dma_start(self.b["norm_col"][rows, :], t["L0_attn_memory_norm"]).then_inc(self.b_loaded, 16)
        sp.dma_start(self.b["gate"][:, 0:1], t["L0_attn_memory_weight"].broadcast_to([128, 1])).then_inc(self.b_loaded, 16)
        sp.dma_start(self.c["router"][:], t["L0_ffn_router_w"]).then_inc(self.rest_loaded, 16)
        sp.dma_start(self.c["router_b"][:], t["L0_ffn_router_b"].broadcast_to([128, 8])).then_inc(self.rest_loaded, 16)
        sp.dma_start(self.c["b2"][:], t["L0_ffn_b2"]).then_inc(self.rest_loaded, 16)
        e = self.e
        for dst, name in ((e["cols"][:], "cols"), (e["fb"][:], "f_b"), (e["pw"][:], "pwT"), (e["fw"][:], "fT"), (e["dpa"][:], "dpT"),
                          (e["w1"][:], "mlp_w1T"), (e["w2"][:].rearrange("p k d -> p (k d)"), "mlp_w2T")):
            sp.dma_start(dst, t[f"L1_attn_{name}"][0:128, :]).then_inc(self.rest_loaded, 16)
        sp.dma_start(e["dpb"][:], t["L1_attn_dpT"][128:192, :]).then_inc(self.rest_loaded, 16)

    def wait(self, sp):
        for loaded, count in ((self.a_loaded, 128), (self.b_loaded, 160), (self.rest_loaded, 176)):
            sp.wait_ge(loaded, count)


def setup(core, t):
    nc = core.nc
    loaded, built = core.rows_moved, core.sem("const_built")
    with nc.Block() as block:

        @block.sync
        def _(sp):
            for c in range(NCH):
                sp.dma_start(chunk(core.xT, c), chunk(t["xT"], c)).then_inc(loaded, 16)
            core.weights.load(sp, t)
            sp.wait_ge(loaded, NCH * 16)

        @block.vector
        def _(dve):
            nc.vector.memset(core.weights.b["mem"][:], 0.0).then_inc(core.weights.zeroed, 1)

        @block.gpsimd
        def _(pool):
            nc.gpsimd.memset(core.ident[:], 0.0).then_inc(built, 1)
            nc.gpsimd.memset(core.mean_w[:], 1.0 / D).then_inc(built, 1)
            nc.gpsimd.memset(core.eps[:], EPS).then_inc(built, 1)
            pool.wait_ge(built, 1)
            nc.gpsimd.affine_select(out=core.ident[:], in_=core.ident[:], compare_op=ALU.not_equal, fill=1.0,
                                    base=0, pattern=[[-1, 128]], channel_multiplier=1).then_inc(built, 1)


def layernorm(core, name, src, dst, gamma=None, beta=None):
    nc = core.nc
    mean, var = core.bank[:, 0:4, :], core.bank[:, 4:8, :]
    with ExitStack() as own:
        sq = core.sb(f"{name}_sq", [128, TOK], ctx=own)
        rstd = core.sb(f"{name}_rstd", [128, TOK], ctx=own)
        mean_ready, centred, squared, var_ready, log_ready, rstd_ready, scaled = core.norm_sems
        before = core.norms * NCH
        core.norms += 1
        block = own.enter_context(nc.Block())

        @block.tensor
        def _(pe):
            for s in range(NCH + 1):
                if s < NCH:
                    nc.tensor.matmul(mean[:, s, :], core.mean_w[:], chunk(src, s), start=True, stop=True).then_inc(mean_ready, 1)
                if s >= 1:
                    pe.wait_ge(squared, before + s)
                    nc.tensor.matmul(var[:, s - 1, :], core.mean_w[:], chunk(sq, s - 1), start=True, stop=True).then_inc(var_ready, 1)

        @block.vector
        def _(dve):
            for s in range(NCH + 2):
                if s < NCH:
                    dve.wait_ge(mean_ready, before + s + 1)
                    nc.vector.tensor_tensor(chunk(dst, s), chunk(src, s), mean[:, s, :], ALU.subtract).then_inc(centred, 1)
                if s >= 2:
                    c = s - 2
                    dve.wait_ge(rstd_ready, before + c + 1)
                    nc.vector.tensor_tensor(chunk(dst, c), chunk(dst, c), chunk(rstd, c), ALU.mult).then_inc(scaled, 1)
                    if gamma is not None:
                        dve.wait_ge(scaled, before + c + 1)
                        nc.vector.tensor_scalar(chunk(dst, c), chunk(dst, c), gamma, beta, ALU.mult, ALU.add)

        @block.scalar
        def _(act):
            nc.scalar.preload_act_table_set("natural_log_exp_and_others")
            for s in range(NCH + 1):
                if s < NCH:
                    act.wait_ge(centred, before + s + 1)
                    nc.scalar.activation(chunk(sq, s), chunk(dst, s), ACT.Square).then_inc(squared, 1)
                if s >= 1:
                    act.wait_ge(var_ready, before + s)
                    nc.scalar.activation(chunk(rstd, s - 1), var[:, s - 1, :], ACT.Ln, bias=core.eps[:, 0:1]).then_inc(log_ready, 1)
                    act.wait_ge(log_ready, before + s)
                    nc.scalar.activation(chunk(rstd, s - 1), chunk(rstd, s - 1), ACT.Exp, scale=-0.5).then_inc(rstd_ready, 1)


def cross_attention_0(core, t):
    nc = core.nc
    DH = D // HEADS
    QUADS = 4
    UNITS = 2 * QUADS
    PAIRS = BATCH // 2
    layernorm(core, "ln0", core.xT, core.yT)
    with ExitStack() as own:
        sb = lambda n, s, dt=F32: core.sb(n, s, dt, own)
        sem = core.sem
        wq, wk, wv, wo, bias = (core.weights.a[n] for n in ("wq", "wk", "wv", "wo", "bias"))
        w_loaded = core.weights.a_loaded
        qT = sb("a_qT", [128, TOK])
        oT = sb("a_oT", [128, TOK])
        head_of = sb("a_head_of", [128, HEADS])
        own_head = sb("a_own_head", [128, 4])
        group_of = sb("a_group_of", [4, 128])
        big = sb("a_big", [3, 128])
        ones3 = sb("a_ones3", [3, CTX])
        big_bf = sb("a_big_bf", [3, 128], BF16)
        ctT = sb("a_ctT", [128, 2, CTX])
        maskf = sb("a_maskf", [3, 2, CTX])
        maskb = sb("a_maskb", [3, 2, CTX], BF16)
        kT = sb("a_kT", [128, 2, CTX])
        v = sb("a_v", [128, 2, 2, 128])
        vlast = sb("a_vlast", [4, 2, 128])
        qb = sb("a_qb", [128, 2, HEADS, LAT])
        p = sb("a_p", [128, 2, QUADS, CTX])
        pT = sb("a_pT", [128, 2, 2, QUADS, 128])
        plast = sb("a_plast", [4, 2, 128])
        nmax = sb("a_nmax", [128, 2, QUADS])
        psum_ = sb("a_psum", [128, 2, QUADS])
        rsum = sb("a_rsum", [128, 2, QUADS])
        odiag = sb("a_odiag", [128, 4, LAT])
        RING, LAG = 4, 3
        S = [core.bank[:, n, 0:CTX] for n in range(RING)]
        TP = [core.bank[:, n, 0:256] for n in (4, 5)]
        KP, VP = core.bank[:, 6, 0:CTX], core.bank[:, 6, :]
        TL, OP = core.bank[0:4, 7, 0:128], core.bank[:, 7, 0:128]

        q_made, q_copied = sem("a_q_made"), sem("a_q_copied")
        const_step = sem("a_const_step")
        ct_loaded = [sem(f"a_ct_loaded{n}") for n in (0, 1)]
        mask_cast, qb_made = sem("a_mask_cast"), sem("a_qb_made")
        k_made, k_copied = sem("a_k_made"), sem("a_k_copied")
        v_made, v_copied = sem("a_v_made"), sem("a_v_copied")
        s_made, max_made, exp_made, recip_made, norm_made = (sem(f"a_{n}") for n in ("s_made", "max_made", "exp_made", "recip_made", "norm_made"))
        t_made, t_copied, tl_made, tl_copied = (sem(f"a_{n}") for n in ("t_made", "t_copied", "tl_made", "tl_copied"))
        o_made, o_masked, o_copied = sem("a_o_made"), sem("a_o_masked"), sem("a_o_copied")
        out_made = sem("a_out_made")

        with nc.Block() as block:

            @block.gpsimd
            def _(pool):
                nc.gpsimd.memset(head_of[:], 1.0).then_inc(const_step, 1)
                nc.gpsimd.memset(group_of[:], 1.0).then_inc(const_step, 1)
                nc.gpsimd.memset(ones3[:], 1.0)
                parts = bf16_parts(-1e9, 3)
                nc.gpsimd.memset(big[:], parts[0]).then_inc(const_step, 1)
                pool.wait_ge(const_step, 3)
                nc.gpsimd.affine_select(out=head_of[:], in_=head_of[:], compare_op=ALU.is_ge, fill=0.0, base=0,
                                        pattern=[[-DH, HEADS]], channel_multiplier=1).then_inc(const_step, 1)
                pool.wait_ge(const_step, 4)
                nc.gpsimd.affine_select(out=head_of[:], in_=head_of[:], compare_op=ALU.is_ge, fill=0.0, base=DH - 1,
                                        pattern=[[DH, HEADS]], channel_multiplier=-1).then_inc(const_step, 1)
                step = 5
                nc.gpsimd.affine_select(out=group_of[:], in_=group_of[:], compare_op=ALU.is_ge, fill=0.0, base=0,
                                        pattern=[[1, 128]], channel_multiplier=-32).then_inc(const_step, 1)
                step += 1
                pool.wait_ge(const_step, step)
                nc.gpsimd.affine_select(out=group_of[:], in_=group_of[:], compare_op=ALU.is_ge, fill=0.0, base=31,
                                        pattern=[[-1, 128]], channel_multiplier=32).then_inc(const_step, 1)
                step += 1
                for n in (1, 2):
                    nc.gpsimd.affine_select(out=big[:], in_=big[:], compare_op=ALU.is_ge, fill=parts[n], base=n - 1,
                                            pattern=[[0, 128]], channel_multiplier=-1).then_inc(const_step, 1)
                    step += 1
                    pool.wait_ge(const_step, step)
                nc.gpsimd.tensor_copy(big_bf[:], big[:]).then_inc(const_step, 1)

            @block.tensor
            def _(pe):
                pe.wait_ge(w_loaded, 128)
                for c in range(NCH):
                    nc.tensor.matmul(core.bank[:, c, :], wq[:], chunk(core.yT, c), start=True, stop=True).then_inc(q_made, 1)

            @block.vector
            def _(dve):
                dve.wait_ge(w_loaded, 128)
                dve.wait_ge(const_step, 5)
                nc.vector.tensor_reduce(own_head[:], head_of[:].rearrange("p (g h) -> p h g", g=QUADS), AXX, ALU.add)
                for c in range(NCH):
                    dve.wait_ge(q_made, c + 1)
                    nc.vector.tensor_scalar(chunk(qT, c), core.bank[:, c, :], bias[:, 0:1], DH ** -0.5,
                                            ALU.add, ALU.mult).then_inc(q_copied, 1)

        with nc.Block() as block:
            ct_dram, mask_dram = t["ctxT"], t["mask0"]

            @block.sync
            def _(sp):
                def load(i, j, after):
                    if after is not None:
                        sp.wait_ge(v_made, after)
                        sp.wait_ge(mask_cast, after)
                    sp.dma_start(ctT[:, j, :], ct_dram[:, bass.ds((i * 2 + j) * CTX, CTX)]).then_inc(ct_loaded[j], 16)
                    sp.dma_start(maskf[:, j, :], mask_dram[:, bass.ds((i * 2 + j) * CTX, CTX)].broadcast_to([3, CTX])).then_inc(ct_loaded[j], 16)

                load(0, 0, None)
                load(0, 1, None)
                core.weights.load_rest(sp, t)
                with sp.Fori(1, PAIRS) as i:
                    for j in range(2):
                        load(i, j, i * 2 + (j - 1))
                core.weights.wait(sp)

            @block.gpsimd
            def _(pool):
                def prepare(i, j, first):
                    if not first:
                        pool.wait_ge(s_made, i * UNITS + QUADS * (j - 1))
                    pool.wait_ge(ct_loaded[j], i * 32 + 32)
                    nc.gpsimd.tensor_tensor(maskb[:, j, :], maskf[:, j, :], ones3[:], ALU.mult).then_inc(mask_cast, 1)
                    rows = qT[:, bass.ds((i * 2 + j) * LAT, LAT)].unsqueeze(1).broadcast_to([128, HEADS, LAT])
                    heads = head_of[:].unsqueeze(2).broadcast_to([128, HEADS, LAT])
                    nc.gpsimd.tensor_tensor(qb[:, j], rows, heads, ALU.mult).then_inc(qb_made, 1)

                prepare(0, 0, True)
                prepare(0, 1, True)
                with pool.Fori(1, PAIRS) as i:
                    for j in range(2):
                        prepare(i, j, False)

            @block.tensor
            def _(pe):
                def keys(i, j, first=False):
                    pe.wait_ge(ct_loaded[j % 2], (i + j // 2) * 32 + 32)
                    if not first:
                        pe.wait_ge(v_copied, i * 2 + j)
                    nc.tensor.matmul(KP, wk[:], ctT[:, j % 2, :], start=True, stop=True).then_inc(k_made, 1)

                def values(i, j):
                    pe.wait_ge(k_copied, i * 2 + j + 1)
                    for k in range(2):
                        nc.tensor.matmul(VP[:, 128 * k:128 * k + 128], ctT[:, j, 128 * k:128 * k + 128], wv[:],
                                         start=True, stop=True)
                    nc.tensor.matmul(VP[0:4, 256:384], ctT[:, j, 256:257].broadcast_to([128, 4]), wv[:],
                                     start=True, stop=True).then_inc(v_made, 1)

                def scores(i, s, first):
                    j, g = divmod(s, QUADS)
                    if g == 0:
                        pe.wait_ge(k_copied, i * 2 + j + 1)
                        pe.wait_ge(qb_made, i * 2 + j + 1)
                    if not (first and s < RING):
                        pe.wait_ge(exp_made, i * UNITS + (s - RING + 1))
                    nc.tensor.matmul(S[s % RING], qb[:, j, 4 * g:4 * g + 4, :].rearrange("p h q -> p (h q)"), kT[:, j, :], start=True, stop=False)
                    nc.tensor.matmul(S[s % RING], big_bf[:], maskb[:, j, :], start=False, stop=True).then_inc(s_made, 1)

                def transposes(i, s, tfirst):
                    j, g = divmod(s % UNITS, QUADS)
                    pe.wait_ge(norm_made, i * UNITS + (s + 1))
                    if not tfirst:
                        pe.wait_ge(t_copied, i * UNITS + (s - 1))
                    for k in range(2):
                        ins = nc.tensor.transpose(TP[s % 2][:, 128 * k:128 * k + 128], p[:, j, g, 128 * k:128 * k + 128], core.ident[:])
                    ins.then_inc(t_made, 1)

                def last_key(i, j, first=False):
                    if not first:
                        pe.wait_ge(o_masked, i * 2 + j)
                    nc.tensor.transpose(TL, p[:, j % 2, :, CTX - 1], core.ident[:]).then_inc(tl_made, 1)

                def output(i, j):
                    n, jj = i * 2 + j, j % 2
                    pe.wait_ge(tl_copied, n + 1)
                    pe.wait_ge(t_copied, (n + 1) * QUADS)
                    pe.wait_ge(v_copied, n + 1)
                    nc.tensor.matmul(OP, vlast[:, jj, :], plast[:, jj, :], start=True, stop=False, skip_group_check=True)
                    for k in range(2):
                        for g in range(QUADS):
                            rows = slice(32 * g, 32 * g + 32)
                            ins = nc.tensor.matmul(OP[rows, :], v[:, jj, k, rows], pT[:, jj, k, g, :], start=False,
                                                   stop=(k == 1), skip_group_check=True)
                    ins.then_inc(o_made, 1)

                pe.wait_ge(w_loaded, 128)
                keys(0, 0, True)

                def body(i, first, last):
                    for s in range(UNITS):
                        scores(i, s, first)
                        if not (first and s < LAG):
                            transposes(i, s - LAG, first and s < LAG + 2)
                        j, g = divmod(s, QUADS)
                        if g == 0:
                            values(i, j)
                        if g == 2 and not (first and j == 0):
                            last_key(i, j - 1, first and j == 1)
                        if g == 3:
                            if not (last and j == 1):
                                keys(i, j + 1)
                            if not (first and j == 0):
                                output(i, j - 1)

                peeled(pe, PAIRS, body)
                for s in range(-LAG, 0):
                    transposes(PAIRS, s, False)
                last_key(PAIRS, -1)
                output(PAIRS, -1)

            @block.scalar
            def _(act):
                def keys(i, j, first=False):
                    act.wait_ge(k_made, i * 2 + j + 1)
                    if not first:
                        act.wait_ge(s_made, (i * 2 + j - 1) * QUADS)
                    nc.scalar.activation(kT[:, j % 2, :], KP, ACT.Identity, bias=bias[:, 1:2]).then_inc(k_copied, 1)

                def transposed(i, s, first=False):
                    j, g = divmod(s % UNITS, QUADS)
                    act.wait_ge(t_made, i * UNITS + (s + 1))
                    if g == 0 and not first:
                        act.wait_ge(o_made, i * 2 + (s // QUADS - 1))
                    nc.scalar.activation(pT[:, j, :, g, :], TP[s % 2].rearrange("p (k q) -> p k q", k=2), ACT.Copy).then_inc(t_copied, 1)

                def body(i, first, last):
                    for s in range(UNITS):
                        j, g = divmod(s, QUADS)
                        if not (first and s < LAG):
                            transposed(i, s - LAG, first)
                        if g == 3 and not (last and j == 1):
                            keys(i, j + 1, first and j == 0)
                        act.wait_ge(max_made, i * UNITS + (s + 1))
                        if g == 0 and not first:
                            act.wait_ge(tl_made, i * 2 + j - 1)
                        nc.scalar.activation(p[:, j, g, :], S[s % RING], ACT.Exp, bias=nmax[:, j, g:g + 1],
                                             accum_out=psum_[:, j, g:g + 1]).then_inc(exp_made, 1)

                keys(0, 0, True)
                peeled(act, PAIRS, body)
                for s in range(-LAG, 0):
                    transposed(PAIRS, s)

            @block.vector
            def _(dve):
                def values(i, j, first=False):
                    dve.wait_ge(v_made, i * 2 + j + 1)
                    if not first:
                        dve.wait_ge(o_made, i * 2 + j - 1)
                    nc.vector.tensor_copy(v[:, j % 2].rearrange("p k d -> p (k d)"), VP[:, 0:256])
                    nc.vector.tensor_tensor(vlast[:, j % 2, :], VP[0:4, 256:384], group_of[:], ALU.mult).then_inc(v_copied, 1)

                def normalise(i, s):
                    j, g = divmod(s % UNITS, QUADS)
                    dve.wait_ge(exp_made, i * UNITS + (s + 1))
                    nc.vector.reciprocal(rsum[:, j, g:g + 1], psum_[:, j, g:g + 1]).then_inc(recip_made, 1)
                    dve.wait_ge(recip_made, i * UNITS + (s + 1))
                    nc.vector.tensor_scalar(p[:, j, g, :], p[:, j, g, :], rsum[:, j, g:g + 1], None, ALU.mult).then_inc(norm_made, 1)

                def last_key(i, j):
                    n, jj = i * 2 + j, j % 2
                    dve.wait_ge(tl_made, n + 1)
                    nc.vector.tensor_copy(plast[:, jj, :], TL).then_inc(tl_copied, 1)

                def output(i, j, first=False):
                    n = i * 2 + j
                    dve.wait_ge(o_made, n + 1)
                    if not first:
                        dve.wait_ge(o_copied, n)
                    heads = own_head[:].unsqueeze(2).broadcast_to([128, 4, LAT])
                    nc.vector.tensor_tensor(odiag[:], OP.rearrange("p (h q) -> p h q", h=4), heads, ALU.mult).then_inc(o_masked, 1)
                    dve.wait_ge(o_masked, n + 1)
                    nc.vector.tensor_reduce(oT[:, bass.ds(n * LAT, LAT)], odiag[:].rearrange("p h q -> p q h"), AXX, ALU.add).then_inc(o_copied, 1)

                def body(i, first, last):
                    for s in range(UNITS):
                        j, g = divmod(s, QUADS)
                        if not (first and s < 2):
                            normalise(i, s - 2)
                        dve.wait_ge(s_made, i * UNITS + (s + 1))
                        nc.vector.tensor_reduce(nmax[:, j, g:g + 1], S[s % RING], AXX, ALU.max, negate=True).then_inc(max_made, 1)
                        if g == 1:
                            values(i, j, first)
                        if g == 2 and not (first and j == 0):
                            last_key(i, j - 1)
                        if g == 3 and not (first and j == 0):
                            output(i, j - 1, first)

                dve.wait_ge(w_loaded, 128)
                peeled(dve, PAIRS, body)
                normalise(PAIRS, -2)
                normalise(PAIRS, -1)
                last_key(PAIRS, -1)
                output(PAIRS, -1)

        with nc.Block() as block:
            vb = sb("a_vb", [128, TOK])

            @block.vector
            def _(dve):
                for c in range(NCH):
                    nc.vector.tensor_scalar(chunk(vb, c), chunk(oT, c), bias[:, 2:3], None, ALU.add).then_inc(q_copied, 1)
                for c in range(NCH):
                    dve.wait_ge(out_made, c + 1)
                    nc.vector.scalar_tensor_tensor(chunk(core.xT, c), core.bank[:, c, :], bias[:, 3:4], chunk(core.xT, c),
                                                   ALU.add, ALU.add)

            @block.tensor
            def _(pe):
                for c in range(NCH):
                    pe.wait_ge(q_copied, NCH + c + 1)
                    nc.tensor.matmul(core.bank[:, c, :], wo[:], chunk(vb, c), start=True, stop=True).then_inc(out_made, 1)


def memory_attention_0(core, t):
    nc = core.nc
    DH, KV = 8, 64
    GROUPS = BATCH // 4
    layernorm(core, "ln1", core.xT, core.yT)
    with ExitStack() as own:
        sb = lambda n, s, dt=F32: core.sb(n, s, dt, own)
        sem = core.sem
        wq, wk, wv, mem, norm_col, gate = (core.weights.b[n] for n in ("wq", "wk", "wv", "mem", "norm_col", "gate"))
        w_loaded = core.weights.b_loaded
        norm = sb("b_norm", [128, 2])
        place = sb("b_place", [2 * TILES, TILES, 2, KV])
        qT, kT, aT = sb("b_qT", [128, TOK]), sb("b_kT", [128, TOK]), sb("b_aT", [128, TOK])
        own_head = sb("b_own_head", [128, 4])
        key_scale = sb("b_key_scale", [128, 4])
        gate_step, mask_step = sem("b_gate_step"), sem("b_mask_step")
        q_made, q_copied = sem("b_q_made"), sem("b_q_copied")

        with nc.Block() as block:

            @block.gpsimd
            def _(pool):
                step = 0

                def select(m, base, pattern, by):
                    nonlocal step
                    pool.wait_ge(mask_step, step)
                    nc.gpsimd.affine_select(out=m, in_=m, compare_op=ALU.is_ge, fill=0.0, base=base, pattern=pattern,
                                            channel_multiplier=by).then_inc(mask_step, 1)
                    step += 1

                nc.gpsimd.memset(own_head[:], 1.0).then_inc(mask_step, 1)
                nc.gpsimd.memset(place[:], 0.0).then_inc(mask_step, 1)
                nc.gpsimd.memset(key_scale[:], DH ** -0.5).then_inc(mask_step, 1)
                step = 3
                pool.wait_ge(mask_step, step)
                nc.gpsimd.affine_select(out=place[:], in_=place[:], compare_op=ALU.not_equal, fill=1.0, base=0,
                                        pattern=[[-2, TILES], [-1, 2], [0, KV]], channel_multiplier=1).then_inc(mask_step, 1)
                step += 1
                for g in range(4):
                    rows = own_head[32 * g:32 * g + 32, :]
                    select(rows, 0, [[-DH, 4]], 1)
                    select(rows, DH - 1, [[DH, 4]], -1)
                select(key_scale[:], 0, [[-32, 4]], 1)
                select(key_scale[:], 31, [[32, 4]], -1)

            @block.tensor
            def _(pe):
                pe.wait_ge(w_loaded, 160)
                for n, w in enumerate((wq, wk)):
                    for c in range(NCH):
                        nc.tensor.matmul(core.bank[:, n * NCH + c, :], w[:], chunk(core.yT, c), start=True, stop=True).then_inc(q_made, 1)

            @block.vector
            def _(dve):
                nc.vector.memset(norm[:], 0.0).then_inc(gate_step, 1)
                nc.vector.memset(gate[:, 1:2], 0.0).then_inc(gate_step, 1)
                dve.wait_ge(w_loaded, 160)
                dve.wait_ge(gate_step, 2)
                for r in range(2):
                    rows = slice(KV * r, KV * r + KV)
                    nc.vector.tensor_copy(norm[rows, r:r + 1], norm_col[rows, :])
                for n, dst in enumerate((qT, kT)):
                    for c in range(NCH):
                        dve.wait_ge(q_made, n * NCH + c + 1)
                        nc.vector.tensor_copy(chunk(dst, c), core.bank[:, n * NCH + c, :]).then_inc(q_copied, 1)
                dve.wait_ge(gate_step, 3)
                nc.vector.tensor_scalar(gate[:, 2:3], gate[:, 1:2], 1.0, None, ALU.add).then_inc(gate_step, 1)
                dve.wait_ge(gate_step, 4)
                nc.vector.reciprocal(gate[:, 2:3], gate[:, 2:3]).then_inc(gate_step, 1)
                dve.wait_ge(gate_step, 5)
                nc.vector.tensor_scalar(gate[:, 3:4], gate[:, 2:3], -1.0, 1.0, ALU.mult, ALU.add)

            @block.scalar
            def _(act):
                act.wait_ge(w_loaded, 160)
                act.wait_ge(gate_step, 2)
                nc.scalar.activation(gate[:, 1:2], gate[:, 0:1], ACT.Exp, scale=-1.0).then_inc(gate_step, 1)

        with ExitStack() as loop:
            sb = lambda n, s, dt=F32: core.sb(n, s, dt, loop)
            qb = sb("b_qb", [128, 2, 4, 4, LAT])
            kb = sb("b_kb", [128, 2, 4, 4, LAT])
            yg = sb("b_yg", [128, 2, 4, 4, LAT])
            vb = sb("b_vb", [128, 2, 4, 128])
            p = sb("b_p", [128, 2, 4, 4, LAT])
            pT = sb("b_pT", [128, 2, 4, 128])
            top, total, rtotal = (sb(f"b_{n}", [128, 2, 16]) for n in ("top", "total", "rtotal"))
            odiag = sb("b_odiag", [128, 2, 4, 4, LAT])
            S = [core.bank[:, n, :].rearrange("p (c k) -> p c k", k=LAT) for n in (0, 1)]
            TP, OP, VP = (core.bank[:, n, :].rearrange("p (b k) -> p b k", b=4) for n in (2, 3, 4))
            qb_made, yg_made, vb_cleared, v_made, v_copied, s_made = (sem(f"b_{n}") for n in ("qb_made", "yg_made", "vb_cleared", "v_made", "v_copied", "s_made"))
            top_made, shifted, exp_made, summed, recip, normed = (sem(f"b_{n}") for n in ("top_made", "shifted", "exp_made", "summed", "recip", "normed"))
            t_made, t_copied, o_made, o_masked, o_copied = (sem(f"b_{n}") for n in ("t_made", "t_copied", "o_made", "o_masked", "o_copied"))
            block = loop.enter_context(nc.Block())

            @block.gpsimd
            def _(pool):
                def body(i, first, last):
                    for j in range(2):
                        n = i * 2 + j
                        if not first:
                            pool.wait_ge(s_made, n - 1)
                        toks = bass.ds(n * 128, 128)
                        queries, keys = (m[:, toks].rearrange("p (b q) -> p b q", b=4) for m in (qT, kT))
                        for g in range(4):
                            nc.gpsimd.tensor_tensor(kb[:, j, :, g, :], keys, key_scale[:, g:g + 1].unsqueeze(2).broadcast_to([128, 4, LAT]), ALU.mult)
                            ins = nc.gpsimd.tensor_tensor(qb[:, j, :, g, :], queries, own_head[:, g:g + 1].unsqueeze(2).broadcast_to([128, 4, LAT]), ALU.mult)
                        ins.then_inc(qb_made, 1)

                nc.gpsimd.memset(vb[:], 0.0).then_inc(vb_cleared, 1)
                peeled(pool, GROUPS // 2, body)

            @block.tensor
            def _(pe):
                def transposes(i, j, first=False):
                    n = i * 2 + j
                    pe.wait_ge(normed, n + 1)
                    if not first:
                        pe.wait_ge(t_copied, n)
                    for b in range(4):
                        ins = nc.tensor.transpose(TP[:, b, :], p[:, j % 2, b].rearrange("p c k -> p (c k)"), core.ident[:])
                    ins.then_inc(t_made, 1)

                def scores(i, j, first):
                    n = i * 2 + j
                    pe.wait_ge(qb_made, n + 1)
                    if not first:
                        pe.wait_ge(shifted, n - 1)
                    for b in range(4):
                        ins = nc.tensor.matmul(S[j].rearrange("p (b g) k -> p b (g k)", b=4)[:, b, :], qb[:, j, b].rearrange("p h q -> p (h q)"),
                                               kb[:, j, b].rearrange("p g k -> p (g k)"), start=True, stop=True)
                    ins.then_inc(s_made, 1)

                def output(i, j, first=False):
                    n = i * 2 + j
                    pe.wait_ge(t_copied, n + 1)
                    pe.wait_ge(v_copied, n + 1)
                    if not first:
                        pe.wait_ge(o_masked, n)
                    for b in range(4):
                        ins = nc.tensor.matmul(OP[:, b, :], vb[:, j % 2, b, :], pT[:, j % 2, b, :], start=True, stop=True)
                    ins.then_inc(o_made, 1)

                def values(i, j, first):
                    n = i * 2 + j
                    if not (first and j == 0):
                        pe.wait_ge(v_copied, n)
                    pe.wait_ge(yg_made, n + 1)
                    for b in range(4):
                        ins = nc.tensor.matmul(VP[:, b, :], yg[:, j, b].rearrange("p r q -> p (r q)"), wv[:], start=True, stop=True)
                    ins.then_inc(v_made, 1)

                def body(i, first, last):
                    for j in range(2):
                        if not first:
                            transposes(i, j - 2)
                        scores(i, j, first)
                        if not first:
                            output(i, j - 2)
                        values(i, j, first)

                body(0, True, False)
                transposes(1, -2, True)
                scores(1, 0, False)
                output(1, -2, True)
                values(1, 0, False)
                transposes(1, -1)
                scores(1, 1, False)
                output(1, -1)
                values(1, 1, False)
                with pe.Fori(2, GROUPS // 2) as i:
                    body(i, False, False)
                for j in (-2, -1):
                    transposes(GROUPS // 2, j)
                    output(GROUPS // 2, j)

            @block.scalar
            def _(act):
                def transposed(i, j):
                    act.wait_ge(t_made, i * 2 + j + 1)
                    nc.scalar.activation(pT[:, j % 2], TP, ACT.Copy).then_inc(t_copied, 1)

                def masked(i, j, first=False):
                    act.wait_ge(o_made, i * 2 + j + 1)
                    if not first:
                        act.wait_ge(o_copied, i * 2 + j - 1)
                    for h in range(4):
                        ins = nc.scalar.activation(odiag[:, j % 2, :, h, :], OP[:, :, 32 * h:32 * h + 32], ACT.Copy, scale=own_head[:, h:h + 1])
                    ins.then_inc(o_masked, 1)

                def exponential(i, j):
                    act.wait_ge(shifted, i * 2 + j + 1)
                    nc.scalar.activation(p[:, j], p[:, j], ACT.Exp).then_inc(exp_made, 1)

                def values(i, j):
                    act.wait_ge(v_made, i * 2 + j + 1)
                    for g in range(4):
                        rows = slice(32 * g, 32 * g + 32)
                        ins = nc.scalar.activation(vb[rows, j, :, rows], VP[rows, :, rows], ACT.Copy)
                    ins.then_inc(v_copied, 1)

                def tokens(i, j, first=False):
                    if not first:
                        act.wait_ge(v_made, i * 2 + j - 1)
                    feats = core.yT[:, bass.ds((i * 2 + j) * 128, 128)].rearrange("p (b q) -> p b q", b=4)
                    nc.scalar.activation(yg[:, j], feats.unsqueeze(2).broadcast_to([128, 4, 4, LAT]), ACT.Copy).then_inc(yg_made, 1)

                act.wait_ge(vb_cleared, 1)
                for j in range(2):
                    tokens(0, j, True)
                    exponential(0, j)
                    values(0, j)
                for j in range(2):
                    tokens(1, j)
                    transposed(1, j - 2)
                    exponential(1, j)
                    masked(1, j - 2, True)
                    values(1, j)
                with act.Fori(2, GROUPS // 2) as i:
                    for j in range(2):
                        tokens(i, j)
                        transposed(i, j - 2)
                        exponential(i, j)
                        masked(i, j - 2)
                        values(i, j)
                for j in (-2, -1):
                    transposed(GROUPS // 2, j)
                    masked(GROUPS // 2, j)

            @block.vector
            def _(dve):
                def shift(i, j):
                    n = i * 2 + j
                    dve.wait_ge(s_made, n + 1)
                    nc.vector.tensor_reduce(top[:, j], S[j], AXX, ALU.max).then_inc(top_made, 1)
                    dve.wait_ge(top_made, n + 1)
                    nc.vector.tensor_tensor(p[:, j].rearrange("p b c k -> p (b c) k"), S[j], top[:, j].unsqueeze(2).broadcast_to([128, 16, LAT]),
                                            ALU.subtract).then_inc(shifted, 1)

                def normalise(i, j):
                    n, jj = i * 2 + j, j % 2
                    probs = p[:, jj].rearrange("p b c k -> p (b c) k")
                    dve.wait_ge(exp_made, n + 1)
                    nc.vector.tensor_reduce(total[:, jj], probs, AXX, ALU.add).then_inc(summed, 1)
                    dve.wait_ge(summed, n + 1)
                    nc.vector.reciprocal(rtotal[:, jj], total[:, jj]).then_inc(recip, 1)
                    dve.wait_ge(recip, n + 1)
                    nc.vector.tensor_tensor(probs, probs, rtotal[:, jj].unsqueeze(2).broadcast_to([128, 16, LAT]), ALU.mult).then_inc(normed, 1)

                def output(i, j):
                    n = i * 2 + j
                    dve.wait_ge(o_masked, n + 1)
                    nc.vector.tensor_reduce(aT[:, bass.ds(n * 128, 128)].rearrange("p (b q) -> p b q", b=4),
                                            odiag[:, j % 2].rearrange("p b h q -> p b q h"), AXX, ALU.add).then_inc(o_copied, 1)

                def body(i, outputs):
                    for j in range(2):
                        if not (isinstance(i, int) and i == j == 0):
                            normalise(i, j - 1)
                        shift(i, j)
                        if j >= 2 - outputs:
                            output(i, j - 3)

                body(0, 0)
                body(1, 1)
                with dve.Fori(2, GROUPS // 2) as i:
                    body(i, 2)
                normalise(GROUPS // 2, -1)
                output(GROUPS // 2, -3)
                output(GROUPS // 2, -2)
                output(GROUPS // 2, -1)

        with ExitStack() as last:
            low, high = core.sb("b_low", [128, TOK], ctx=last), core.sb("b_high", [128, TOK], ctx=last)
            inverse = core.sb("b_inverse", [128, 2 * TILES], ctx=last)
            inverse_t = core.sb("b_inverse_t", [2 * TILES, 128], ctx=last)
            clipped, expd, elu_made = (sem(f"b_{n}") for n in ("clipped", "expd", "elu_made"))
            num_made, num_kept, den_made, inverted = (sem(f"b_{n}") for n in ("num_made", "num_kept", "den_made", "inverted"))
            turned, turned_kept, spread, chain = (sem(f"b_{n}") for n in ("turned", "turned_kept", "spread", "chain"))
            NUM, DEN, TURNED = core.bank[:, 0:4, :], core.bank[:, 7, 0:2 * TILES], core.bank[0:2 * TILES, 6, 0:128]
            SPREAD = [core.bank[:, n, :] for n in (4, 5, 0, 1)]
            block = last.enter_context(nc.Block())

            @block.vector
            def _(dve):
                for c in range(NCH):
                    nc.vector.tensor_scalar(chunk(low, c), chunk(qT, c), 0.0, None, ALU.min).then_inc(clipped, 1)
                for c in range(NCH):
                    dve.wait_ge(expd, 2 * c + 2)
                    nc.vector.scalar_tensor_tensor(chunk(high, c), chunk(low, c), -1.0, chunk(high, c), ALU.add, ALU.add).then_inc(elu_made, 1)
                for c in range(NCH):
                    nc.vector.scalar_tensor_tensor(chunk(core.xT, c), chunk(aT, c), gate[:, 3:4], chunk(core.xT, c), ALU.mult, ALU.add).then_inc(chain, 1)
                dve.wait_ge(den_made, 1)
                nc.vector.reciprocal(inverse[:], DEN).then_inc(inverted, 1)
                done = NCH
                for c in range(NCH):
                    dve.wait_ge(num_kept, c + 1)
                    dve.wait_ge(spread, c + 1)
                    nc.vector.tensor_tensor(chunk(qT, c), chunk(low, c), SPREAD[c], ALU.mult).then_inc(chain, 1)
                    done += 1
                    dve.wait_ge(chain, done)
                    nc.vector.scalar_tensor_tensor(chunk(core.xT, c), chunk(qT, c), gate[:, 2:3], chunk(core.xT, c), ALU.mult, ALU.add)

            @block.scalar
            def _(act):
                for c in range(NCH):
                    nc.scalar.activation(chunk(high, c), chunk(qT, c), ACT.Relu).then_inc(expd, 1)
                    act.wait_ge(clipped, c + 1)
                    nc.scalar.activation(chunk(low, c), chunk(low, c), ACT.Exp).then_inc(expd, 1)
                for c in range(NCH):
                    act.wait_ge(num_made, c + 1)
                    nc.scalar.activation(chunk(low, c), NUM[:, c, :], ACT.Copy).then_inc(num_kept, 1)
                act.wait_ge(turned, 1)
                nc.scalar.activation(inverse_t[:], TURNED, ACT.Copy).then_inc(turned_kept, 1)

            @block.tensor
            def _(pe):
                for c in range(NCH):
                    pe.wait_ge(elu_made, c + 1)
                    nc.tensor.matmul(NUM[:, c, :], mem[:], chunk(high, c), start=True, stop=True).then_inc(num_made, 1)
                    for m in range(4 * c, 4 * c + 4):
                        ins = nc.tensor.matmul(DEN[:, 2 * m:2 * m + 2], high[:, 128 * m:128 * m + 128], norm[:], start=True, stop=True)
                ins.then_inc(den_made, 1)
                pe.wait_ge(inverted, 1)
                nc.tensor.transpose(TURNED, inverse[:], core.ident[:]).then_inc(turned, 1)
                pe.wait_ge(turned_kept, 1)
                for c in range(NCH):
                    if c >= 2:
                        pe.wait_ge(num_kept, c - 1)
                    for m in range(4):
                        ins = nc.tensor.matmul(SPREAD[c][:, 128 * m:128 * m + 128], place[:, 4 * c + m].rearrange("r s d -> r (s d)"), inverse_t[:],
                                               start=True, stop=True)
                    ins.then_inc(spread, 1)


class Context:

    def __init__(self, core, own):
        sb = lambda n, s, dt=F32: core.sb(n, s, dt, own)
        self.keyT = sb("x_keyT", [128, BATCH, CTX + LAT])
        self.affine = sb("x_affine", [128, 5])
        self.wqT, self.wkT, self.wvT, self.wout = (sb(f"x_{n}", [128, 8, 128]) for n in ("wqT", "wkT", "wvT", "wout"))
        self.wqk, self.wvo = sb("x_wqk", [128, HEADS, 128]), sb("x_wvo", [128, HEADS, 128])
        self.mask8, self.mask16 = sb("x_mask8", [BATCH, CTX], mybir.dt.uint8), sb("x_mask16", [BATCH, CTX], BF16)
        self.mask_dram = core.nc.dram_tensor("mask1_bf16", (BATCH, CTX), BF16, kind="Internal").ap()
        self.loaded, self.w_loaded = core.sem("x_loaded_small"), core.sem("x_w_loaded")
        self.mask_cast, self.mask_stored = (core.sem(f"x_mask_{n}") for n in ("cast", "stored"))


def experts_0(core, t, cx):
    nc = core.nc
    E, HID, KCH = 8, 512, 4
    layernorm(core, "ln2", core.xT, core.yT)
    with ExitStack() as own:
        sb = lambda n, s, dt=F32: core.sb(n, s, dt, own)
        sem = core.sem
        router, router_b, b2 = (core.weights.c[n] for n in ("router", "router_b", "b2"))
        w_loaded = core.weights.rest_loaded
        acc = sb("c_acc", [128, TILES, 128])
        gates = sb("c_gates", [128, E, TILES])
        gT = sb("c_gT", [E, TILES, 128])
        logit_made, gate_step = sem("c_logit_made"), sem("c_gate_step")
        shifted, gates_made = sem("c_shifted"), sem("c_gates_made")
        rank_made, exp_made, gt_made, gt_copied, bias_made = sem("c_rank_made"), sem("c_exp_made"), sem("c_gt_made"), sem("c_gt_copied"), sem("c_bias_made")

        with ExitStack() as route:
            rb = lambda n: core.sb(n, [128, TILES, E], ctx=route)
            logit, left, rank, hit, keep, tmp = (rb(f"c_{n}") for n in ("logit", "left", "rank", "hit", "keep", "tmp"))
            best, top, pick = (core.sb(f"c_{n}", [128, TILES], ctx=route) for n in ("best", "top", "pick"))
            wide = lambda v: v[:].unsqueeze(2).broadcast_to([128, TILES, E])
            LG = core.bank[:, 0, 0:TILES * E].rearrange("p (t e) -> p t e", e=E)
            block = route.enter_context(nc.Block())

            @block.sync
            def _(sp):
                sp.dma_start(cx.affine[:], t["L1_xattn_affine"]).then_inc(cx.loaded, 16)
                sp.dma_start(cx.mask8[:], t["mask1"]).then_inc(cx.loaded, 16)
                sp.wait_ge(cx.loaded, 32)

            @block.gpsimd
            def _(pool):
                for e in range(E):
                    nc.gpsimd.memset(rank[:, :, e], float(E - e)).then_inc(rank_made, 1)

            @block.tensor
            def _(pe):
                pe.wait_ge(w_loaded, 176)
                for m in range(TILES):
                    ins = nc.tensor.matmul(LG[:, m, :], core.yT[:, 128 * m:128 * m + 128], router[:], start=True, stop=True)
                ins.then_inc(logit_made, 1)
                pe.wait_ge(gates_made, 1)
                for m in range(TILES):
                    ins = nc.tensor.transpose(core.bank[0:E, 1 + m // 4, 128 * (m % 4):128 * (m % 4) + 128], tmp[:, m, :], core.ident[:])
                ins.then_inc(gt_made, 1)
                pe.wait_ge(gt_copied, 1)
                for m in range(TILES):
                    ins = nc.tensor.matmul(core.bank[:, (5 + m // 4) % 8, 128 * (m % 4):128 * (m % 4) + 128], gT[:, m, :], b2[:], start=True, stop=True)
                    if m % 4 == 3:
                        ins.then_inc(bias_made, 1)

            @block.scalar
            def _(act):
                act.wait_ge(shifted, 1)
                nc.scalar.activation(tmp[:], tmp[:], ACT.Exp).then_inc(exp_made, 1)

            @block.vector
            def _(dve):
                step = 0

                def then(ins):
                    nonlocal step
                    ins.then_inc(gate_step, 1)
                    step += 1
                    dve.wait_ge(gate_step, step)

                v = nc.vector
                dve.wait_ge(logit_made, 1)
                dve.wait_ge(w_loaded, 176)
                dve.wait_ge(rank_made, E)
                then(v.tensor_tensor(logit[:], LG, router_b[:].unsqueeze(1).broadcast_to([128, TILES, E]), ALU.add))
                then(v.tensor_reduce(best[:], logit[:], AXX, ALU.max))
                then(v.tensor_tensor(hit[:], logit[:], wide(best), ALU.is_equal))
                then(v.tensor_tensor(hit[:], hit[:], rank[:], ALU.mult))
                then(v.tensor_reduce(pick[:], hit[:], AXX, ALU.max))
                then(v.tensor_tensor(keep[:], hit[:], wide(pick), ALU.is_equal))
                then(v.scalar_tensor_tensor(left[:], keep[:], -3e38, logit[:], ALU.mult, ALU.add))
                then(v.tensor_reduce(top[:], left[:], AXX, ALU.max))
                then(v.tensor_tensor(hit[:], left[:], wide(top), ALU.is_equal))
                then(v.tensor_tensor(hit[:], hit[:], rank[:], ALU.mult))
                then(v.tensor_reduce(pick[:], hit[:], AXX, ALU.max))
                then(v.tensor_tensor(hit[:], hit[:], wide(pick), ALU.is_equal))
                then(v.tensor_tensor(keep[:], keep[:], hit[:], ALU.add))
                v.tensor_tensor(tmp[:], logit[:], wide(best), ALU.subtract).then_inc(shifted, 1)
                dve.wait_ge(exp_made, 1)
                then(v.tensor_tensor(tmp[:], tmp[:], keep[:], ALU.mult))
                then(v.tensor_reduce(top[:], tmp[:], AXX, ALU.add))
                then(v.reciprocal(best[:], top[:]))
                then(v.tensor_tensor(tmp[:], tmp[:], wide(best), ALU.mult))
                v.tensor_copy(gates[:].rearrange("p e t -> p t e"), tmp[:]).then_inc(gates_made, 1)
                dve.wait_ge(gt_made, 1)
                v.tensor_copy(gT[:].rearrange("e (c m) k -> e c (m k)", c=NCH), core.bank[0:E, 1:5, :]).then_inc(gt_copied, 1)
                dve.wait_ge(cx.loaded, 32)
                v.tensor_copy(cx.mask16[:], cx.mask8[:]).then_inc(cx.mask_cast, 1)
                for c in range(NCH):
                    dve.wait_ge(bias_made, c + 1)
                    v.tensor_copy(acc[:, 4 * c:4 * c + 4, :].rearrange("p m d -> p (m d)"), core.bank[:, (5 + c) % 8, :])

        WIDTH = 2 * HID + KCH
        w = sb("c_w", [128, 2, WIDTH])
        hs = sb("c_hs", [128, 2, KCH, CHUNK])
        RING, EDGE = 4, 4
        ct = sb("c_ct", [128, RING + 1, 4, 128])
        stats, moments, rstd = sb("c_stats", [128, RING + 1, 4, 6]), sb("c_moments", [128, RING + 1, 4, 2]), sb("c_rstd", [128, RING + 1, 4])
        UP = [core.bank[:, k, :] for k in range(KCH)]
        Y = [core.bank[:, 4 + n, :].rearrange("p (m d) -> p m d", m=4) for n in (0, 1)]
        TC = [core.bank[:, n, :] for n in (6, 7)]
        we_loaded = [sem(f"c_we_loaded{n}") for n in (0, 1)]
        up_made, relu_made, down_made, added = sem("c_up_made"), sem("c_relu_made"), sem("c_down_made"), sem("c_added")
        ct_loaded = [sem(f"c_ct_loaded{n}") for n in range(RING + 1)]
        minus_half, half_made, padded = sb("c_minus_half", [128, 4]), sem("c_half_made"), sem("c_padded")
        measured, gathered, rooted, normed, turned, kept = (sem(f"c_{n}") for n in ("measured", "gathered", "rooted", "normed", "turned", "kept"))
        UNITS, TURNS = 2 * NCH, E // 2
        HEAD = 64
        acc_turned, residual, product_made = sem("c_acc_turned"), sem("c_residual"), sem("c_product_made")
        with nc.Block() as block:

            @block.sync
            def _(sp):
                def load(i, j):
                    sp.dma_start(w[:, j, :], t["L0_ffn_w"][:, bass.ds((i * 2 + j) * WIDTH, WIDTH)]).then_inc(we_loaded[j], 16)

                def load_pair(i, s):
                    for b in range(2):
                        rows = t["ctx"][bass.ds((i * (2 * UNITS) + (2 * s + b)) * CTX, 256), :].rearrange("(k p) d -> p k d", p=128)
                        sp.dma_start(ct[:, s % RING, 2 * b:2 * b + 2, :], rows).then_inc(ct_loaded[s % RING], 16)

                load(0, 0)
                sp.dma_start(ct[0:BATCH, EDGE, 0, :], t["ctx_last"]).then_inc(ct_loaded[EDGE], 16)
                for s in range(RING):
                    load_pair(0, s)
                load(0, 1)
                for dst, name in ((cx.wqT, "L1_xattn_WqT"), (cx.wkT, "L1_xattn_WkT"), (cx.wvT, "L1_xattn_WvT"), (cx.wout, "L1_xattn_Wout")):
                    sp.dma_start(dst[:].rearrange("p n d -> p (n d)"), t[name]).then_inc(cx.w_loaded, 16)
                sp.wait_ge(cx.mask_cast, 1)
                sp.dma_start(cx.mask_dram, cx.mask16[:]).then_inc(cx.mask_stored, 16)
                for s in range(RING, UNITS):
                    sp.wait_ge(turned, s - RING + 2)
                    load_pair(0, s)
                with sp.Fori(1, TURNS) as i:
                    for s in range(UNITS):
                        if s % NCH == 1:
                            sp.wait_ge(down_made, i * UNITS + NCH * (s // NCH - 1))
                            load(i, s // NCH)
                        sp.wait_ge(turned, i * UNITS + (s - RING + 2))
                        load_pair(i, s)

            @block.gpsimd
            def _(pool):
                def root(i, s):
                    pool.wait_ge(gathered, i * UNITS + (s + 2))
                    at = EDGE if s < 0 else s % RING
                    rows, tiles = (BATCH, 1) if s < 0 else (128, 4)
                    root = rstd[0:rows, at, 0:tiles]
                    nc.gpsimd.tensor_tensor(root, moments[0:rows, at, 0:tiles, 1], core.eps[0:rows, :].broadcast_to([rows, tiles]), ALU.add).then_inc(padded, 1)
                    pool.wait_ge(padded, i * UNITS + (s + 2))
                    nc.gpsimd.tensor_tensor(root, root, minus_half[0:rows, 0:tiles], ALU.pow).then_inc(rooted, 1)

                nc.gpsimd.memset(minus_half[:], -0.5).then_inc(half_made, 1)
                pool.wait_ge(half_made, 1)
                root(0, -1)

                def body(i, first, last):
                    for s in range(UNITS):
                        root(i, s)

                peeled(pool, TURNS, body)

            @block.tensor
            def _(pe):
                def up(i, s, first):
                    j, c = divmod(s, NCH)
                    if c == 0:
                        pe.wait_ge(we_loaded[j], i * 16 + 16)
                    for k in range(KCH):
                        if not (first and s == 0):
                            pe.wait_ge(relu_made, i * UNITS * KCH + ((s - 1) * KCH + k + 1))
                        nc.tensor.matmul(UP[k], w[:, j, 128 * k:128 * k + 128], chunk(core.yT, c), start=True, stop=True).then_inc(up_made, 1)

                def down(i, s, first):
                    j = s % UNITS // NCH
                    pe.wait_ge(relu_made, i * UNITS * KCH + (s + 1) * KCH)
                    if not first:
                        pe.wait_ge(added, i * UNITS + (s - 1))
                    for m in range(4):
                        for k in range(KCH):
                            ins = nc.tensor.matmul(Y[s % 2][:, m, :], hs[:, s % 2, k, 128 * m:128 * m + 128],
                                                   w[:, j, HID + 128 * k:HID + 128 * k + 128], start=(k == 0), stop=(k == KCH - 1))
                    ins.then_inc(down_made, 1)

                def turn(i, s, first):
                    pe.wait_ge(normed, i * UNITS + (s + 2))
                    if first and s < 0:
                        nc.tensor.transpose(TC[s % 2][:, 0:BATCH], ct[0:BATCH, EDGE, 0, :], core.ident[0:BATCH, 0:BATCH]).then_inc(turned, 1)
                        return
                    if not (first and s == 0):
                        pe.wait_ge(kept, i * UNITS + s)
                    for m in range(4):
                        ins = nc.tensor.transpose(TC[s % 2][:, 128 * m:128 * m + 128], ct[:, s % RING, m, :], core.ident[:])
                    ins.then_inc(turned, 1)

                def body(i, first, last):
                    for s in range(UNITS):
                        up(i, s, first)
                        if not (first and s < 1):
                            turn(i, s - 2, first)
                        if not (first and s == 0):
                            down(i, s - 1, first and s < 3)

                peeled(pe, TURNS, body)
                turn(TURNS, -2, False)
                down(TURNS, -1, False)
                turn(TURNS, -1, False)
                pe.wait_ge(added, E * NCH)
                pe.wait_ge(relu_made, E * NCH * KCH)
                for m in range(TILES):
                    ins = nc.tensor.transpose(core.bank[:, m // 4, 128 * (m % 4):128 * (m % 4) + 128], acc[:, m, :], core.ident[:])
                    if m % 4 == 3:
                        ins.then_inc(acc_turned, 1)
                pe.wait_ge(cx.w_loaded, 64)
                pe.wait_ge(kept, E * NCH + 1)
                for n, (a, b) in enumerate(((cx.wqT, cx.wkT), (cx.wvT, cx.wout))):
                    if n == 1:
                        pe.wait_ge(residual, NCH)
                    for h in range(HEADS):
                        rows = slice(HEAD * (h % 2), HEAD * (h % 2) + HEAD)
                        at = 4 * (1 - n) + 2 * (h % 2) + h // 8
                        ins = nc.tensor.matmul(core.bank[:, at, 128 * (h // 2 % 4):128 * (h // 2 % 4) + 128], a[rows, h // 2, :], b[rows, h // 2, :],
                                               start=True, stop=True)
                    ins.then_inc(product_made, 1)

            @block.scalar
            def _(act):
                def keep(i, s, first=False):
                    act.wait_ge(turned, i * UNITS + (s + 2))
                    if first and s < 0:
                        act.wait_ge(cx.loaded, 32)
                        keys, src = cx.keyT[:, :, CTX - 1], TC[s % 2][:, 0:BATCH]
                    else:
                        keys = cx.keyT[:, bass.ds(i * (2 * UNITS) + 2 * s, 2), 0:256]
                        src = TC[s % 2].rearrange("p (b k) -> p b k", b=2)
                    nc.scalar.activation(keys, src, ACT.Identity, scale=cx.affine[:, 0:1], bias=cx.affine[:, 1:2]).then_inc(kept, 1)

                def body(i, first, last):
                    for s in range(UNITS):
                        if not (first and s < 2):
                            act.wait_ge(down_made, i * UNITS + (s - 1))
                        for k in range(KCH):
                            act.wait_ge(up_made, i * UNITS * KCH + (s * KCH + k + 1))
                            nc.scalar.activation(hs[:, s % 2, k, :], UP[k], ACT.Relu,
                                                 bias=w[:, s // NCH, 2 * HID + k:2 * HID + k + 1]).then_inc(relu_made, 1)

                        if not (first and s < 1):
                            keep(i, s - 2, first)

                peeled(act, TURNS, body)
                keep(TURNS, -2)
                keep(TURNS, -1)

            @block.vector
            def _(dve):
                def measure(i, s):
                    edge = isinstance(i, int) and s < 0
                    at = EDGE if edge else s % RING
                    rows, tiles = (BATCH, 1) if edge else (128, 4)
                    dve.wait_ge(ct_loaded[at], 16 if edge else (i * (UNITS // RING) + s // RING) * 32 + 32)
                    for m in range(tiles):
                        ins = nc.vector.bn_stats(stats[0:rows, at, m, :], ct[0:rows, at, m, :])
                    ins.then_inc(measured, 1)

                def gather(i, s):
                    edge = isinstance(i, int) and s < 0
                    at = EDGE if edge else s % RING
                    rows, tiles = (BATCH, 1) if edge else (128, 4)
                    for m in range(tiles):
                        ins = nc.vector.bn_aggr(moments[0:rows, at, m, :], stats[0:rows, at, m, :])
                    ins.then_inc(gathered, 1)

                def normalise(i, s, first=False, measuring=True):
                    edge = first and s < 0
                    at = EDGE if edge else s % RING
                    rows, tiles = (BATCH, 1) if edge else (128, 4)
                    dve.wait_ge(rooted, i * UNITS + (s + 2))
                    if measuring:
                        dve.wait_ge(measured, i * UNITS + (s + 3))
                    for m in range(tiles):
                        ins = nc.vector.tensor_scalar(ct[0:rows, at, m, :], ct[0:rows, at, m, :], moments[0:rows, at, m, 0:1],
                                                      rstd[0:rows, at, m:m + 1], ALU.subtract, ALU.mult)
                    ins.then_inc(normed, 1)

                measure(0, -1)
                dve.wait_ge(measured, 1)
                gather(0, -1)

                def body(i, first, last):
                    for s in range(UNITS):
                        measure(i, s)
                        normalise(i, s - 1, first)
                        gather(i, s)
                        j, c = divmod(s, NCH)
                        dve.wait_ge(down_made, i * UNITS + (s + 1))
                        if not (first and s < NCH):
                            dve.wait_ge(added, i * UNITS + (s - NCH + 1))
                        for m in range(4):
                            tile = NCH * c + m
                            ins = nc.vector.scalar_tensor_tensor(acc[:, tile, :], Y[s % 2][:, m, :], gates[:, bass.ds(i * 2 + j, 1), tile],
                                                                 acc[:, tile, :], ALU.mult, ALU.add)
                        ins.then_inc(added, 1)

                peeled(dve, TURNS, body)
                normalise(TURNS, -1, measuring=False)
                for c in range(NCH):
                    dve.wait_ge(acc_turned, c + 1)
                    nc.vector.tensor_tensor(chunk(core.xT, c), chunk(core.xT, c), core.bank[:, c, :], ALU.add).then_inc(residual, 1)
                for n, (dst, scale) in enumerate(((cx.wqk, HEAD ** -0.5), (cx.wvo, 1.0))):
                    dve.wait_ge(product_made, n + 1)
                    for odd in range(2):
                        at = 4 * (1 - n) + 2 * odd
                        out = dst[:].rearrange("p (m two) d -> p two m d", two=2)[:, odd]
                        src = core.bank[:, at:at + 2, :].rearrange("p b (m d) -> p (b m) d", d=128)
                        nc.vector.tensor_scalar(out, src, scale, None, ALU.mult)




def cross_attention_1(core, t, cx):
    nc = core.nc
    DH, KEYS = 64, CTX + LAT
    REST = KEYS - 256
    GROUPS, GROUP = BATCH // 4, 16
    TURNS, UNITS = GROUPS // 2, 2 * GROUP
    layernorm(core, "ln3", core.xT, core.yT)
    with ExitStack() as own:
        sb = lambda n, s, dt=F32: core.sb(n, s, dt, own)
        sem = core.sem
        affine, keyT = cx.affine, cx.keyT
        latT = sb("d_latT", [128, TOK])
        wqk, wvo = cx.wqk, cx.wvo
        layernorm(core, "ln4", core.yT, latT, affine[:, 2:3], affine[:, 3:4])

        key = sb("d_key", [128, 2, KEYS])
        maskb = sb("d_maskb", [1, 2, CTX], BF16)
        lowest = sb("d_lowest", [1, 128], BF16)
        xv = sb("d_xv", [128, 2, 3, 128])
        q = sb("d_q", [128, 2, 4, HEADS, LAT])
        P = sb("d_p", [128, 4, KEYS])
        pT = sb("d_pT", [128, 2, 3, 128])
        nmax, total, rtotal = (sb(f"d_{n}", [128, 4]) for n in ("nmax", "total", "rtotal"))
        a = sb("d_a", [128, 4, HEADS, LAT])
        S = [core.bank[:, n, 0:KEYS] for n in (0, 1)]
        TP = [core.bank[:, n, 0:384] for n in (2, 3)]
        XP, OP = core.bank[:, 4, 0:384], core.bank[:, 5, :]
        Q = [core.bank[:, n, :] for n in (6, 7)]
        OUT = core.bank[:, 6, 0:128]
        key_loaded = [sem(f"d_key_loaded{n}") for n in (0, 1)]
        zeroed, low_made, latents_placed = sem("d_zeroed"), sem("d_low_made"), sem("d_latents_placed")
        xv_made, xv_copied, q_made, q_copied = sem("d_xv_made"), sem("d_xv_copied"), sem("d_q_made"), sem("d_q_copied")
        s_made, max_made, exp_made, recip, normed = (sem(f"d_{n}") for n in ("s_made", "max_made", "exp_made", "recip", "normed"))
        t_made, t_copied, o_made, o_copied = (sem(f"d_{n}") for n in ("t_made", "t_copied", "o_made", "o_copied"))
        out_made, out_added = sem("d_out_made"), sem("d_out_added")
        with nc.Block() as block:

            @block.sync
            def _(sp):
                def load(i, b, first=False):
                    n = i * 8 + b
                    if not first:
                        sp.wait_ge(s_made, (n - 1) * 4)
                        sp.wait_ge(xv_made, n - 1)
                    sp.dma_start(key[:, b % 2, :], keyT[:, bass.ds(n, 1), :].rearrange("p a k -> p (a k)")).then_inc(key_loaded[b % 2], 16)
                    sp.dma_start(maskb[:, b % 2, :], cx.mask_dram[bass.ds(n, 1), :]).then_inc(key_loaded[b % 2], 16)

                sp.wait_ge(cx.mask_stored, 16)
                sp.wait_ge(latents_placed, 1)
                for b in range(8):
                    load(0, b, b < 2)
                with sp.Fori(1, TURNS) as i:
                    for b in range(8):
                        load(i, b)

            @block.gpsimd
            def _(pool):
                nc.gpsimd.memset(lowest[:], -3.3895313892515355e38).then_inc(low_made, 1)
                nc.gpsimd.tensor_copy(keyT[:, :, CTX:KEYS], latT[:].rearrange("p (b q) -> p b q", b=BATCH)).then_inc(latents_placed, 1)

            @block.tensor
            def _(pe):
                def key_rows(i, b, first=False):
                    n = i * 8 + b
                    pe.wait_ge(key_loaded[b % 2], (i * 4 + b // 2) * 32 + 32)
                    if not first:
                        pe.wait_ge(xv_copied, n)
                    for k in range(3):
                        width = 128 if k < 2 else REST
                        ins = nc.tensor.transpose(XP[0:width, 128 * k:128 * k + 128], key[:, b % 2, 128 * k:128 * k + width], core.ident[:])
                    ins.then_inc(xv_made, 1)

                def queries(i, g, r, first=False):
                    if not (first and r < 2):
                        pe.wait_ge(q_copied, (i * 2 + g) * 4 + (r - 1))
                    if r == 0 and not first and not (isinstance(i, int) and i * 2 + g < 2):
                        pe.wait_ge(out_added, i * 2 + (g - 1))
                    for h in range(4):
                        ins = nc.tensor.matmul(Q[r % 2][:, 128 * h:128 * h + 128], wqk[:, 4 * r + h, :], latT[:, bass.ds((i * 2 + g) * 128, 128)],
                                               start=True, stop=True)
                    ins.then_inc(q_made, 1)

                def scores(i, u, first):
                    half, v = divmod(u, GROUP)
                    b, g = divmod(v, 4)
                    if v == 0:
                        pe.wait_ge(q_copied, (i * 2 + half) * 4 + 4)
                    if g == 0:
                        pe.wait_ge(key_loaded[b % 2], (i * 4 + (half * 4 + b) // 2) * 32 + 32)
                    if not (first and u < 2):
                        pe.wait_ge(exp_made, i * UNITS + (u - 1))
                    nc.tensor.matmul(S[u % 2], q[:, half, b, 4 * g:4 * g + 4, :].rearrange("p h q -> p (h q)"), key[:, b % 2, :], start=True, stop=False)
                    nc.tensor.matmul(S[u % 2][:, 0:CTX], lowest[:], maskb[:, b % 2, :], start=False, stop=True).then_inc(s_made, 1)

                def transposes(i, u, first=False):
                    pe.wait_ge(normed, i * UNITS + (u + 1))
                    if not (first and u < 2):
                        pe.wait_ge(t_copied, i * UNITS + (u - 1))
                    for k in range(3):
                        width = 128 if k < 2 else REST
                        ins = nc.tensor.transpose(TP[u % 2][0:width, 128 * k:128 * k + 128], P[:, u % 4, 128 * k:128 * k + width], core.ident[:])
                    ins.then_inc(t_made, 1)

                def means(i, u, first=False):
                    b, g = divmod(u, 4)
                    if g == 0:
                        pe.wait_ge(xv_copied, i * 8 + (b + 1))
                        if not (first and b == 0):
                            pe.wait_ge(o_copied, i * 8 + b)
                    pe.wait_ge(t_copied, i * UNITS + (u + 1))
                    for k in range(3):
                        width = 128 if k < 2 else REST
                        ins = nc.tensor.matmul(OP[:, 128 * g:128 * g + 128], xv[0:width, b % 2, k, :], pT[0:width, u % 2, k, :],
                                               start=(k == 0), stop=(k == 2))
                    ins.then_inc(o_made, 1)

                def project(i, g):
                    pe.wait_ge(o_copied, (i * 2 + g + 1) * 4)
                    for h in range(HEADS):
                        ins = nc.tensor.matmul(OUT, wvo[:, h, :], a[:, :, h, :], start=(h == 0), stop=(h == HEADS - 1))
                    ins.then_inc(out_made, 1)

                pe.wait_ge(low_made, 1)
                pe.wait_ge(zeroed, 1)
                for r in range(4):
                    queries(0, 0, r, True)
                key_rows(0, 0, True)

                def body(i, first, last):
                    for u in range(UNITS):
                        half, v = divmod(u, GROUP)
                        scores(i, u, first)
                        if not (first and u < 2):
                            transposes(i, u - 2, first)
                        if not (first and u < 3):
                            means(i, u - 3, first)
                        if u % 4 == 1 and not (last and u // 4 == 7):
                            key_rows(i, u // 4 + 1)
                        if v == 5 and not (first and half == 0):
                            project(i, half - 1)
                        if v >= GROUP - 5 and v < GROUP - 1 and not (last and half == 1):
                            queries(i, half + 1, v - (GROUP - 5))

                peeled(pe, TURNS, body)
                transposes(TURNS, -2)
                means(TURNS, -3)
                transposes(TURNS, -1)
                means(TURNS, -2)
                means(TURNS, -1)
                project(TURNS, -1)

            @block.scalar
            def _(act):
                def queries(i, g, r):
                    act.wait_ge(q_made, (i * 2 + g) * 4 + (r + 1))
                    if r == 0 and not (isinstance(i, int) and i * 2 + g < 2):
                        act.wait_ge(s_made, (i * 2 + g - 1) * GROUP)
                    nc.scalar.activation(q[:, g % 2, :, 4 * r:4 * r + 4, :].rearrange("p b h q -> p h b q"),
                                         Q[r % 2].rearrange("p (h b q) -> p h b q", h=4, b=4), ACT.Copy).then_inc(q_copied, 1)

                def transposed(i, u, first=False):
                    act.wait_ge(t_made, i * UNITS + (u + 1))
                    if not (first and u < 2):
                        act.wait_ge(o_made, i * UNITS + (u - 1))
                    nc.scalar.activation(pT[:, u % 2].rearrange("p k q -> p (k q)"), TP[u % 2], ACT.Copy).then_inc(t_copied, 1)

                def body(i, first, last):
                    for u in range(UNITS):
                        half, v = divmod(u, GROUP)
                        act.wait_ge(max_made, i * UNITS + (u + 1))
                        if not (first and u < 4):
                            act.wait_ge(t_made, i * UNITS + (u - 3))
                        nc.scalar.activation(P[:, u % 4, :], S[u % 2], ACT.Exp, bias=nmax[:, u % 4:u % 4 + 1],
                                             accum_out=total[:, u % 4:u % 4 + 1]).then_inc(exp_made, 1)
                        if not (first and u < 2):
                            transposed(i, u - 2, first)
                        if v >= GROUP - 5 and v < GROUP - 1 and not (last and half == 1):
                            queries(i, half + 1, v - (GROUP - 5))

                for r in range(4):
                    queries(0, 0, r)
                peeled(act, TURNS, body)
                transposed(TURNS, -2)
                transposed(TURNS, -1)

            @block.vector
            def _(dve):
                def key_rows(i, b, first=False):
                    n = i * 8 + b
                    dve.wait_ge(xv_made, n + 1)
                    if not first:
                        dve.wait_ge(o_made, (n - 1) * 4)
                    nc.vector.tensor_copy(xv[:, b % 2].rearrange("p k d -> p (k d)"), XP).then_inc(xv_copied, 1)

                def normalise(i, u):
                    dve.wait_ge(exp_made, i * UNITS + (u + 1))
                    nc.vector.reciprocal(rtotal[:, u % 4:u % 4 + 1], total[:, u % 4:u % 4 + 1]).then_inc(recip, 1)
                    dve.wait_ge(recip, i * UNITS + (u + 1))
                    nc.vector.tensor_scalar(P[:, u % 4, :], P[:, u % 4, :], rtotal[:, u % 4:u % 4 + 1], None, ALU.mult).then_inc(normed, 1)

                def means(i, b, first=False):
                    dve.wait_ge(o_made, i * UNITS + 4 * b + 4)
                    if b % 4 == 0 and not (first and b == 0):
                        dve.wait_ge(out_made, i * 2 + b // 4)
                    nc.vector.tensor_copy(a[:, b % 4].rearrange("p h q -> p (h q)"), OP).then_inc(o_copied, 1)

                def project(i, g):
                    n = i * 2 + g
                    dve.wait_ge(out_made, n + 1)
                    toks = bass.ds(n * 128, 128)
                    nc.vector.scalar_tensor_tensor(core.xT[:, toks], OUT, affine[:, 4:5], core.xT[:, toks], ALU.add, ALU.add).then_inc(out_added, 1)

                def body(i, first, last):
                    for u in range(UNITS):
                        half, v = divmod(u, GROUP)
                        dve.wait_ge(s_made, i * UNITS + (u + 1))
                        nc.vector.tensor_reduce(nmax[:, u % 4:u % 4 + 1], S[u % 2], AXX, ALU.max, negate=True).then_inc(max_made, 1)
                        if not (first and u < 1):
                            normalise(i, u - 1)
                        if u % 4 == 2:
                            if not (first and u == 2):
                                means(i, u // 4 - 1, first)
                            if not (last and u // 4 == 7):
                                key_rows(i, u // 4 + 1, first and u < 4)
                        if v == 5 and not (first and half == 0):
                            project(i, half - 1)

                nc.vector.memset(XP, 0.0)
                for n in range(2):
                    ins = nc.vector.memset(TP[n], 0.0)
                ins.then_inc(zeroed, 1)
                key_rows(0, 0, True)
                peeled(dve, TURNS, body)
                normalise(TURNS, -1)
                means(TURNS, -1)
                project(TURNS, -1)



def recurrent_1(core, t):
    nc = core.nc
    EXP, K, KCH = 192, 4, 4
    PER = CHUNK // LAT
    layernorm(core, "ln5", core.xT, core.yT)
    with ExitStack() as own:
        sb = lambda n, s, dt=F32: core.sb(n, s, dt, own)
        sem = core.sem
        cols, fb, pw, fw, dpa, dpb, w1, w2 = (core.weights.e[n] for n in ("cols", "fb", "pw", "fw", "dpa", "dpb", "w1", "w2"))
        fneg, fhalf = sb("e_fneg", [128, 4]), sb("e_fhalf", [128, 4])
        hT = sb("e_hT", [128, TOK])

        layernorm(core, "ln6", core.yT, hT, cols[:, 0:1], cols[:, 1:2])

        with ExitStack() as part:
            cT = core.sb("e_cT", [128, TOK], ctx=part)
            tap, pw_made = sem("e_tap"), sem("e_pw_made")
            block = part.enter_context(nc.Block())

            @block.vector
            def _(dve):
                nc.vector.tensor_scalar(fneg[:], fb[:], -1.0, None, ALU.mult)
                nc.vector.tensor_scalar(fhalf[:], fb[:], 0.5, None, ALU.add)
                for k in range(K):
                    for c in range(NCH):
                        src, dst = (chunk(v, c).rearrange("p (b t) -> p b t", t=LAT) for v in (hT, cT))
                        weight = cols[:, 9 + K - 1 - k:9 + K - k]
                        if k == 0:
                            ins = nc.vector.tensor_scalar(dst, src, weight, cols[:, 8:9], ALU.mult, ALU.add)
                        else:
                            dve.wait_ge(tap, (k - 1) * NCH + c + 1)
                            ins = nc.vector.scalar_tensor_tensor(dst[:, :, k:], src[:, :, :LAT - k], weight, dst[:, :, k:], ALU.mult, ALU.add)
                        ins.then_inc(tap, 1)
                for c in range(NCH):
                    dve.wait_ge(pw_made, c + 1)
                    nc.vector.scalar_tensor_tensor(chunk(core.yT, c), core.bank[:, c, :], cols[:, 6:7], chunk(core.yT, c), ALU.add, ALU.add)

            @block.tensor
            def _(pe):
                for c in range(NCH):
                    pe.wait_ge(tap, (K - 1) * NCH + c + 1)
                    nc.tensor.matmul(core.bank[:, c, :], pw[:], chunk(cT, c), start=True, stop=True).then_inc(pw_made, 1)

        layernorm(core, "ln7", core.yT, hT, cols[:, 2:3], cols[:, 3:4])

        with ExitStack() as part:
            pb = lambda n: core.sb(n, [128, 2, CHUNK], ctx=part)
            kept, new, cand, seq = (
                [pb(f"e_{n}{h}") for h in (0, 1)] for n in ("kept", "new", "cand", "seq"))
            f_made, sig_made, step, scanned, dp_made, dp_added = (
                sem(f"e_{n}") for n in ("f_made", "sig_made", "step", "scanned", "dp_made", "dp_added"))
            ROWS = (128, 64)
            COLS = (0, 128, EXP, EXP + 128)
            block = part.enter_context(nc.Block())

            @block.tensor
            def _(pe):
                def gates(c):
                    if c >= 2:
                        pe.wait_ge(dp_added, c - 1)
                    for n in range(4):
                        rows = ROWS[n % 2]
                        ins = nc.tensor.matmul(core.bank[0:rows, 4 * (c % 2) + n, :], fw[:, COLS[n]:COLS[n] + rows], chunk(hT, c), start=True, stop=True)
                    ins.then_inc(f_made, 1)

                gates(0)
                gates(1)
                for c in range(NCH):
                    pe.wait_ge(scanned, 2 * c + 2)
                    out = core.bank[:, 4 * (c % 2), :]
                    nc.tensor.matmul(out, dpa[:], seq[0][:, c % 2, :], start=True, stop=False)
                    nc.tensor.matmul(out, dpb[:], seq[1][0:64, c % 2, :], start=False, stop=True).then_inc(dp_made, 1)
                    if c + 2 < NCH:
                        gates(c + 2)

            @block.scalar
            def _(act):
                for c in range(NCH):
                    act.wait_ge(f_made, c + 1)
                    if c >= 2:
                        act.wait_ge(scanned, 2 * (c - 1))
                    for h, rows in enumerate(ROWS):
                        bank = [core.bank[0:rows, 4 * (c % 2) + n, :] for n in (h, 2 + h)]
                        r = slice(0, rows)
                        nc.scalar.activation(new[h][r, c % 2, :], bank[0], ACT.Sigmoid, bias=fb[r, h:h + 1])
                        nc.scalar.activation(kept[h][r, c % 2, :], bank[0], ACT.Sigmoid, bias=fneg[r, h:h + 1], scale=-1.0)
                        nc.scalar.activation(cand[h][r, c % 2, :], bank[1], ACT.Sigmoid, bias=fb[r, 2 + h:3 + h]).then_inc(sig_made, 1)

            @block.vector
            def _(dve):
                n = 0

                def then(ins):
                    nonlocal n
                    ins.then_inc(step, 1)
                    n += 1
                    dve.wait_ge(step, n)

                for c in range(NCH):
                    for h, rows in enumerate(ROWS):
                        r = slice(0, rows)
                        k_, n_, c_, s_ = (v[h][r, c % 2, :] for v in (kept, new, cand, seq))
                        dve.wait_ge(sig_made, 2 * c + h + 1)
                        if c >= 2:
                            dve.wait_ge(dp_made, c - 1)
                        then(nc.vector.scalar_tensor_tensor(c_, core.bank[r, 4 * (c % 2) + 2 + h, :], fhalf[r, 2 + h:3 + h], c_, ALU.add, ALU.max))
                        then(nc.vector.tensor_tensor(n_, n_, c_, ALU.mult))
                        first_k, first_n = (v.rearrange("p (b t) -> p b t", t=LAT)[:, :, 0:1] for v in (k_, n_))
                        then(nc.vector.scalar_tensor_tensor(first_n, first_k, 0.5, first_n, ALU.mult, ALU.add))
                        then(nc.vector.tensor_scalar(first_k, first_k, 0.0, None, ALU.mult))
                        nc.vector.tensor_tensor_scan(s_, k_, n_, 0.0, ALU.mult, ALU.add).then_inc(scanned, 1)
                    dve.wait_ge(dp_made, c + 1)
                    nc.vector.tensor_tensor(chunk(core.yT, c), chunk(core.yT, c), core.bank[:, 4 * (c % 2), :], ALU.add).then_inc(dp_added, 1)

        layernorm(core, "ln8", core.yT, hT, cols[:, 4:5], cols[:, 5:6])

        with ExitStack() as part:
            mid = core.sb("e_mid", [128, 2, KCH, CHUNK], ctx=part)
            up_made, act_made, down_made, summed = sem("e_up_made"), sem("e_act_made"), sem("e_down_made"), sem("e_summed")
            block = part.enter_context(nc.Block())

            @block.tensor
            def _(pe):
                def up(c):
                    for k in range(KCH):
                        if c >= 1:
                            pe.wait_ge(act_made, (c - 1) * KCH + k + 1)
                        nc.tensor.matmul(core.bank[:, k, :], w1[:, 128 * k:128 * k + 128], chunk(hT, c), start=True, stop=True).then_inc(up_made, 1)

                up(0)
                for c in range(NCH):
                    if c + 1 < NCH:
                        up(c + 1)
                    pe.wait_ge(act_made, (c + 1) * KCH)
                    for k in range(KCH):
                        ins = nc.tensor.matmul(core.bank[:, 4 + c, :], w2[:, k, :], mid[:, c % 2, k, :], start=(k == 0), stop=(k == KCH - 1))
                    ins.then_inc(down_made, 1)

            @block.scalar
            def _(act):
                for c in range(NCH):
                    if c >= 2:
                        act.wait_ge(down_made, c - 1)
                    for k in range(KCH):
                        act.wait_ge(up_made, c * KCH + k + 1)
                        nc.scalar.activation(mid[:, c % 2, k, :], core.bank[:, k, :], ACT.Gelu, bias=cols[:, 13 + k:14 + k]).then_inc(act_made, 1)

            @block.vector
            def _(dve):
                for c in range(NCH):
                    nc.vector.tensor_tensor(chunk(core.xT, c), chunk(core.xT, c), chunk(core.yT, c), ALU.add).then_inc(summed, 1)
                for c in range(NCH):
                    dve.wait_ge(down_made, c + 1)
                    dve.wait_ge(summed, c + 1)
                    nc.vector.scalar_tensor_tensor(chunk(core.xT, c), core.bank[:, 4 + c, :], cols[:, 7:8], chunk(core.xT, c), ALU.add, ALU.add)


def quantised_ffn_1(core, t):
    nc = core.nc
    INNER, KCH = 512, 4
    ROUND = 1.5 * 2.0 ** 23
    QMAX, QMIN, TINY = 127.0, -128.0, 1e-5
    layernorm(core, "ln9", core.xT, core.yT)
    with ExitStack() as own:
        sb = lambda n, s, dt=F32: core.sb(n, s, dt, own)
        sem = core.sem
        wq = sb("f_wq", [128, 3, INNER], BF16)
        wmean, winv = sb("f_wmean", [128, 3]), sb("f_winv", [128, 3])
        xqT = sb("f_xqT", [128, TOK], BF16)
        rows_in = sb("f_rows_in", [128, TILES])
        sg, su = sb("f_sg", [128, TILES]), sb("f_su", [128, TILES])
        bias_round, wdown = sb("f_bias_round", [128, 1]), sb("f_wdown", [128, 1])

        with ExitStack() as pre:
            w = core.sb("f_w", [128, 3, INNER], ctx=pre)
            q = core.sb("f_q", [128, TILES, 128], ctx=pre)
            inv = core.sb("f_inv", [128, TILES], ctx=pre)
            w_loaded, wsum, wmean_made, step = sem("f_w_loaded"), sem("f_wsum"), sem("f_wmean_made"), sem("f_step")
            x_turned, y_turned, x_kept, q_made, q_turned = (sem(f"f_{n}") for n in ("x_turned", "y_turned", "x_kept", "q_made", "q_turned"))
            block = pre.enter_context(nc.Block())

            @block.sync
            def _(sp):
                sp.dma_start(w[:].rearrange("p n d -> p (n d)"), t["L1_ffn_w"]).then_inc(w_loaded, 16)
                sp.wait_ge(w_loaded, 16)

            @block.tensor
            def _(pe):
                for v, base, done in ((core.yT, 0, y_turned), (core.xT, 4, x_turned)):
                    for m in range(TILES):
                        ins = nc.tensor.transpose(core.bank[:, base + m // 4, 128 * (m % 4):128 * (m % 4) + 128], v[:, 128 * m:128 * m + 128], core.ident[:])
                    ins.then_inc(done, 1)
                pe.wait_ge(wsum, 1)
                pe.wait_ge(x_kept, 1)
                nc.tensor.matmul(core.bank[:, 4, 0:3], core.mean_w[:], wmean[:], start=True, stop=True).then_inc(wmean_made, 1)
                pe.wait_ge(q_made, 1)
                for m in range(TILES):
                    ins = nc.tensor.transpose(core.bank[:, m // 4, 128 * (m % 4):128 * (m % 4) + 128], q[:, m, :], core.ident[:])
                ins.then_inc(q_turned, 1)

            @block.scalar
            def _(act):
                act.wait_ge(x_turned, 1)
                nc.scalar.activation(core.out[:].rearrange("p m d -> p (m d)"), core.bank[:, 4:8, :].rearrange("p c n -> p (c n)"), ACT.Copy).then_inc(x_kept, 1)

            @block.vector
            def _(dve):
                n = 0

                def then(ins):
                    nonlocal n
                    ins.then_inc(step, 1)
                    n += 1
                    dve.wait_ge(step, n)

                v = nc.vector
                v.memset(bias_round[:], -ROUND)
                dve.wait_ge(w_loaded, 16)
                v.tensor_reduce(wmean[:], w[:], AXX, ALU.add, apply_absolute_value=True).then_inc(wsum, 1)
                turned = core.bank[:, 0:4, :].rearrange("p c (m d) -> p (c m) d", d=128)
                dve.wait_ge(y_turned, 1)
                then(v.tensor_reduce(rows_in[:], turned, AXX, ALU.max, apply_absolute_value=True))
                then(v.tensor_scalar(rows_in[:], rows_in[:], TINY, None, ALU.max))
                then(v.reciprocal(inv[:], rows_in[:]))
                then(v.tensor_scalar(inv[:], inv[:], QMAX, None, ALU.mult))
                then(v.tensor_tensor(q[:], turned, inv[:].unsqueeze(2).broadcast_to([128, TILES, 128]), ALU.mult))
                then(v.tensor_scalar(q[:], q[:], ROUND, -ROUND, ALU.add, ALU.add))
                v.tensor_scalar(q[:], q[:], QMAX, QMIN, ALU.min, ALU.max).then_inc(q_made, 1)
                dve.wait_ge(wmean_made, 1)
                then(v.tensor_scalar(wmean[:], core.bank[:, 4, 0:3], 1.0 / INNER, TINY, ALU.mult, ALU.max))
                then(v.reciprocal(winv[:], wmean[:]))
                for m in range(3):
                    then(v.tensor_scalar(w[:, m, :], w[:, m, :], winv[:, m:m + 1], ROUND, ALU.mult, ALU.add))
                then(v.tensor_scalar(w[:], w[:], -ROUND, 1.0, ALU.add, ALU.min))
                v.tensor_scalar(wq[:], w[:], -1.0, None, ALU.max)
                then(v.tensor_scalar(rows_in[:], rows_in[:], 1.0 / QMAX, None, ALU.mult))
                v.tensor_scalar(wdown[:], wmean[:, 2:3], 1.0 / QMAX, None, ALU.mult)
                v.tensor_scalar(sg[:], rows_in[:], wmean[:, 0:1], None, ALU.mult)
                v.tensor_scalar(su[:], rows_in[:], wmean[:, 1:2], None, ALU.mult)
                dve.wait_ge(q_turned, 1)
                v.tensor_copy(xqT[:].rearrange("p (c n) -> p c n", c=NCH), core.bank[:, 0:4, :])

        gs, h = sb("f_gs", [128, 2, INNER]), sb("f_h", [128, 2, INNER])
        hT = sb("f_hT", [128, 2, KCH, 128], BF16)
        alpha = sb("f_alpha", [128, 2])
        most, mult, sd = sb("f_most", [128, 2]), sb("f_mult", [128, 2]), sb("f_sd", [128, 2])
        G, U = [core.bank[:, n, :] for n in (0, 1)], [core.bank[:, n, :] for n in (2, 3)]
        T, DN = [core.bank[:, n, :] for n in (4, 5)], [core.bank[:, n, 0:128] for n in (6, 7)]
        TURNS = TILES // 2
        alpha_made, g_made, silu_made, rounded, t_made, t_copied, d_made = (
            sem(f"f_{n}") for n in ("alpha_made", "g_made", "silu_made", "rounded", "t_made", "t_copied", "d_made"))
        gu_free, finished, quant = (sem(f"f_{n}") for n in ("gu_free", "finished", "quant"))
        QUANT = 5
        with nc.Block() as block:

            @block.tensor
            def _(pe):
                def turn(i, j):
                    n = i * 2 + j
                    pe.wait_ge(rounded, n + 1)
                    pe.wait_ge(t_copied, n + 1)
                    for k in range(KCH):
                        ins = nc.tensor.transpose(T[j % 2][:, 128 * k:128 * k + 128], h[:, j % 2, 128 * k:128 * k + 128], core.ident[:])
                    ins.then_inc(t_made, 1)

                def down(i, j):
                    n = i * 2 + j
                    pe.wait_ge(t_copied, n + 3)
                    pe.wait_ge(finished, n + 1)
                    for k in range(KCH):
                        ins = nc.tensor.matmul(DN[j % 2], hT[:, j % 2, k, :], wq[:, 2, 128 * k:128 * k + 128], start=(k == 0), stop=(k == KCH - 1))
                    ins.then_inc(d_made, 1)

                def body(i, first, last):
                    for j in range(2):
                        pe.wait_ge(gu_free, i * 2 + (j + 1))
                        src = xqT[:, bass.ds((i * 2 + j) * 128, 128)]
                        nc.tensor.matmul(G[j], src, wq[:, 0, :], start=True, stop=True)
                        nc.tensor.matmul(U[j], src, wq[:, 1, :], start=True, stop=True).then_inc(g_made, 1)
                        if not first:
                            down(i, j - 2)
                        if not (first and j == 0):
                            turn(i, j - 1)

                pe.sem_inc(d_made, 2)
                peeled(pe, TURNS, body)
                down(TURNS, -2)
                turn(TURNS, -1)
                down(TURNS, -1)

            @block.scalar
            def _(act):
                def turned(i, j):
                    n = i * 2 + j
                    act.wait_ge(t_made, n + 1)
                    act.wait_ge(d_made, n + 1)
                    nc.scalar.activation(hT[:, j % 2].rearrange("p k q -> p (k q)"), T[j % 2], ACT.Identity,
                                         bias=bias_round[:, 0:1]).then_inc(t_copied, 1)

                def body(i, first, last):
                    for j in range(2):
                        act.wait_ge(alpha_made, i * 2 + (j + 1))
                        act.wait_ge(g_made, i * 2 + (j + 1))
                        nc.scalar.activation(gs[:, j, :], G[j], ACT.Silu, scale=alpha[:, j:j + 1]).then_inc(silu_made, 1)
                        if not (first and j == 0):
                            turned(i, j - 1)

                act.sem_inc(t_copied, 2)
                peeled(act, TURNS, body)
                turned(TURNS, -1)

            @block.vector
            def _(dve):
                v = nc.vector

                def finish(i, j):
                    n = i * 2 + j
                    dve.wait_ge(d_made, n + 3)
                    row = core.out[:, bass.ds(n, 1), :].rearrange("p a d -> p (a d)")
                    v.scalar_tensor_tensor(row, DN[j % 2], sd[:, j % 2:j % 2 + 1], row, ALU.mult, ALU.add).then_inc(finished, 1)

                def scale(i, j):
                    v.tensor_copy(alpha[:, j % 2:j % 2 + 1], sg[:, bass.ds(i * 2 + j, 1)]).then_inc(alpha_made, 1)

                def body(i, first, last):
                    for j in range(2):
                        n = i * 2 + j
                        J = slice(j, j + 1)
                        dve.wait_ge(silu_made, n + 1)
                        v.scalar_tensor_tensor(h[:, j, :], U[j], su[:, bass.ds(n, 1)], gs[:, j, :], ALU.mult, ALU.mult).then_inc(gu_free, 1)
                        if not (last and j == 1):
                            scale(i, j + 1)
                        dve.wait_ge(gu_free, n + 3)
                        v.tensor_reduce(most[:, J], h[:, j, :], AXX, ALU.max, apply_absolute_value=True).then_inc(quant, 1)
                        dve.wait_ge(quant, n * QUANT + 1)
                        v.tensor_scalar(most[:, J], most[:, J], TINY, None, ALU.max).then_inc(quant, 1)
                        dve.wait_ge(quant, n * QUANT + 2)
                        v.reciprocal(mult[:, J], most[:, J]).then_inc(quant, 1)
                        dve.wait_ge(quant, n * QUANT + 3)
                        v.tensor_scalar(mult[:, J], mult[:, J], QMAX, None, ALU.mult).then_inc(quant, 1)
                        if not first:
                            finish(i, j - 2)
                        dve.wait_ge(finished, n + 1)
                        v.tensor_scalar(sd[:, J], most[:, J], wdown[:, 0:1], None, ALU.mult)
                        dve.wait_ge(quant, n * QUANT + 4)
                        v.tensor_scalar(h[:, j, :], h[:, j, :], mult[:, J], ROUND, ALU.mult, ALU.add).then_inc(quant, 1)
                        dve.wait_ge(quant, n * QUANT + 5)
                        v.tensor_scalar(h[:, j, :], h[:, j, :], ROUND + QMAX, ROUND + QMIN, ALU.min, ALU.max).then_inc(rounded, 1)

                dve.sem_inc(gu_free, 2)
                dve.sem_inc(finished, 2)
                scale(0, 0)
                peeled(dve, TURNS, body)
                finish(TURNS, -2)
                finish(TURNS, -1)


def perceiver(nc, t, out):
    with ExitStack() as ctx:
        core = Core(nc, ctx)
        core.weights = Weights(core)
        setup(core, t)
        cross_attention_0(core, t)
        memory_attention_0(core, t)
        with ExitStack() as own:
            cx = Context(core, own)
            experts_0(core, t, cx)
            cross_attention_1(core, t, cx)
        recurrent_1(core, t)
        quantised_ffn_1(core, t)
        with nc.Block() as block:

            @block.sync
            def _(sp):
                sp.dma_start(out.rearrange("(m p) d -> p m d", p=128), core.out[:]).then_inc(core.rows_moved, 16)
                sp.wait_ge(core.rows_moved, (NCH + 1) * 16)


def layouts(inputs):
    import numpy as np

    a = {k: np.asarray(v) for k, v in inputs.items()}
    put = {"xT": a["x"].reshape(TOK, D).T, "ctxT": a["ctx_1024"].reshape(BATCH * CTX, D).T,
           "ctx": a["ctx_1024"].reshape(BATCH * CTX, D), "ctx_last": a["ctx_1024"][:, CTX - 1, :],
           "mask0": a["mask_Bx1x1xS2_fk0"].reshape(1, BATCH * CTX)}
    for n in ("Wq", "Wk", "Wv", "Wo"):
        put[f"L0_xattn_{n}"] = a[f"L0_xattn_{n}"]
    for n in ("bq", "bk", "bv", "bo"):
        put[f"L0_xattn_{n}"] = a[f"L0_xattn_{n}"].reshape(D, 1)
    for n in ("Wq", "Wk", "Wv", "memory"):
        put[f"L0_attn_{n}"] = a[f"L0_attn_{n}"]
    put["L0_attn_memory_norm"] = a["L0_attn_memory_norm"].reshape(64, 1)
    put["L0_attn_memory_weight"] = a["L0_attn_memory_weight"].reshape(1, 1)
    put["L0_ffn_router_w"], put["L0_ffn_b2"] = a["L0_ffn_router_w"], a["L0_ffn_b2"]
    put["L0_ffn_router_b"] = a["L0_ffn_router_b"].reshape(1, 8)
    put["L0_ffn_w"] = np.concatenate([a["L0_ffn_w1"].transpose(1, 0, 2),
                                      a["L0_ffn_w2"].reshape(8, 4, 128, 128).transpose(2, 0, 1, 3).reshape(128, 8, 512),
                                      a["L0_ffn_b1"].reshape(8, 4, 128).transpose(2, 0, 1)], axis=2).reshape(128, -1)
    pairs = lambda w: w.reshape(8, 128, 128).transpose(1, 0, 2).reshape(128, 1024)
    put["L1_xattn_WqT"] = pairs(a["L1_xattn_Wq"].T)
    put["L1_xattn_WkT"] = pairs(a["L1_xattn_Wkv"][:, :1024].T)
    put["L1_xattn_WvT"] = pairs(a["L1_xattn_Wkv"][:, 1024:].T)
    put["L1_xattn_Wout"] = pairs(a["L1_xattn_Wout"])
    put["L1_xattn_affine"] = np.stack([a[f"L1_xattn_{n}"] for n in ("g_media", "b_media", "g_latent", "b_latent", "bout")], axis=1)
    cols = [a[f"L1_attn_{n}"] for n in ("ln1_g", "ln1_b", "ln2_g", "ln2_b", "ln3_g", "ln3_b", "pw_b", "mlp_b2", "dw_b")]
    cols += list(a["L1_attn_dw_w"][:, 0, :].T) + list(a["L1_attn_mlp_b1"].reshape(4, 128))
    put["L1_attn_cols"] = np.stack(cols, axis=1)
    fb = a["L1_attn_f_b"]
    put["L1_attn_f_b"] = np.stack([fb[0:128], np.concatenate([fb[128:192]] * 2), fb[192:320], np.concatenate([fb[320:384]] * 2)], axis=1)
    put["L1_attn_pwT"], put["L1_attn_fT"], put["L1_attn_dpT"] = a["L1_attn_pw_w"].T, a["L1_attn_f_w"].T, a["L1_attn_dp_w"].T
    put["L1_attn_mlp_w1T"] = a["L1_attn_mlp_w1"].T
    put["L1_attn_mlp_w2T"] = a["L1_attn_mlp_w2"].T.reshape(4, 128, 128).transpose(1, 0, 2).reshape(128, 512)
    put["L1_ffn_w"] = np.concatenate([a["L1_ffn_w_gate"].T, a["L1_ffn_w_up"].T,
                                      a["L1_ffn_w_down"].T.reshape(4, 128, 128).transpose(1, 0, 2).reshape(128, 512)], axis=1)
    put["mask1"] = a["mask_BxS2_bk0"]
    return {k: np.ascontiguousarray(v) for k, v in put.items()}


def kernel(**inputs):
    import concourse.bacc as bacc
    import numpy as np
    from concourse.bass_utils import run_bass_kernel_spmd

    nc = bacc.Bacc("TRN2", target_bir_lowering=False, num_devices=1)
    arrays = layouts(inputs)
    t = {k: nc.dram_tensor(f"in_{k}", v.shape, mybir.dt.from_np(v.dtype), kind="ExternalInput").ap() for k, v in arrays.items()}
    out = nc.dram_tensor("out_rows", (TOK, D), F32, kind="ExternalOutput").ap()
    perceiver(nc, t, out)
    r = run_bass_kernel_spmd(nc, [{f"in_{k}": v for k, v in arrays.items()}], core_ids=[0])
    return np.ascontiguousarray(r.results[0]["out_rows"]).reshape(BATCH, LAT, D)
```
